# Optimizing a Trainium2 kernel written in Bass

```python
import numpy as np
import jax
import jax.numpy as jnp

def _softmax(x, axis=-1):
    return jax.nn.softmax(x, axis=axis)

def _gelu(x):
    return jax.nn.gelu(x, approximate=True)

def _silu(x):
    return jax.nn.silu(x)

def _sigmoid(x):
    return jax.nn.sigmoid(x)

def _layernorm(x, axis=-1, eps=1e-05):
    m = jnp.mean(x, axis=axis, keepdims=True)
    v = jnp.var(x, axis=axis, keepdims=True)
    return (x - m) / jnp.sqrt(v + eps)

def _scatter_add(tgt, idx, src, axis=0):
    return tgt.at[idx].add(src)

def _segment_sum(src, seg, n):
    return jax.ops.segment_sum(src, seg, n)
kernel_name = 'mk_adaln_attn_ffn_d1_seqx_r4_b5839a'

def setup_inputs(seed: int=0):
    np.random.seed(seed)
    _w = jnp.asarray

    def _rec_inputs():
        import jax
        import jax.numpy as jnp
        _rk = jax.random.key(seed)
        x = -1.394e-06 + 0.9999 * jax.random.normal(jax.random.fold_in(_rk, 1), (4, 512, 512), jnp.float32)
        _lenS = 512 - jax.random.randint(jax.random.fold_in(_rk, 7), (4,), 0, max(1, 512 // 4) + 1, jnp.int32)
        _lenS2 = 512 - jax.random.randint(jax.random.fold_in(_rk, 8), (4,), 0, max(1, 512 // 4) + 1, jnp.int32)
        cond_2048 = -0.00499425 + 1.0058 * jax.random.normal(jax.random.fold_in(_rk, 11), (4, 512), jnp.float32)
        return (x, cond_2048)
    x, cond_2048 = _rec_inputs()

    def _L0_cond_setup():
        import jax, jax.numpy as jnp
        import numpy as np
        B, T, D = (16, 128, 512)
        key = jax.random.key(seed)
        k0, k1, k2, k3 = jax.random.split(key, 4)
        scale = 1.0 / np.sqrt(D)
        return {'initial_state': jax.random.normal(k0, (B, D), jnp.float32), 'inputs': jax.random.normal(k1, (B, T, D), jnp.float32), 'W_ih': jax.random.normal(k2, (D, 3 * D), jnp.float32) * scale, 'W_hh': jax.random.normal(k3, (D, 3 * D), jnp.float32) * scale, 'b_ih': jnp.zeros((3 * D,), jnp.float32), 'b_hh': jnp.zeros((3 * D,), jnp.float32)}
    _L0_cond_all = _L0_cond_setup()
    _L0_cond_in = {k: v for k, v in _L0_cond_all.items() if k in ('W_ih', 'W_hh', 'b_ih', 'b_hh')}
    del _L0_cond_all

    def _L0_attn_setup():
        import jax, jax.numpy as jnp
        import numpy as np
        C = 8.0

        def _linear_scan(alpha, xbeta):

            def combine(e1, e2):
                a1, b1 = e1
                a2, b2 = e2
                return (a2 * a1, a2 * b1 + b2)
            _, h = jax.lax.associative_scan(combine, (alpha, xbeta), axis=1)
            return h
        dim = 512
        B, T = (4, 1024)
        key = jax.random.key(seed)
        k_x, k_wi, k_wg = jax.random.split(key, 3)
        std = dim ** (-0.5)
        x = jax.random.normal(k_x, (B, T, dim), dtype=jnp.float32)
        W_in = jax.random.normal(k_wi, (dim, dim), dtype=jnp.float32) * std
        b_in = jnp.zeros((dim,), dtype=jnp.float32)
        W_gate = jax.random.normal(k_wg, (dim, dim), dtype=jnp.float32) * std
        b_gate = jnp.zeros((dim,), dtype=jnp.float32)
        forget_lambda = jnp.linspace(-4.323, -9.0, dim, dtype=jnp.float32)
        return {'x': x, 'W_in': W_in, 'b_in': b_in, 'W_gate': W_gate, 'b_gate': b_gate, 'forget_lambda': forget_lambda}
    _L0_attn_all = _L0_attn_setup()
    _L0_attn_in = {k: v for k, v in _L0_attn_all.items() if k in ('W_in', 'b_in', 'W_gate', 'b_gate', 'forget_lambda')}
    del _L0_attn_all

    def _L0_cond2_setup():
        import jax, jax.numpy as jnp
        import numpy as np
        NUM_BLOCKS = 8
        NUM_LAYERS = 4
        EPS = 1e-06
        key = jax.random.key(seed)
        ks = jax.random.split(key, 6)
        B, S, H = (4, 1024, 512)
        inputs = jax.random.normal(ks[0], (B, S, H), dtype=jnp.float32)
        query_vectors = jax.random.normal(ks[1], (NUM_LAYERS, H), dtype=jnp.float32) * 0.01
        lim = float(np.sqrt(6.0 / (H + H)))
        Wk = jax.random.uniform(ks[2], (H, H), minval=-lim, maxval=lim, dtype=jnp.float32)
        Wo = jax.random.uniform(ks[3], (H, H), minval=-lim, maxval=lim, dtype=jnp.float32)
        rms_weight = jnp.ones((H,), dtype=jnp.float32)
        ln_gamma = jnp.ones((H,), dtype=jnp.float32)
        ln_beta = jnp.zeros((H,), dtype=jnp.float32)
        return {'inputs': inputs, 'layer_idx': 1, 'rms_weight': rms_weight, 'query_vectors': query_vectors, 'Wk': Wk, 'Wo': Wo, 'ln_gamma': ln_gamma, 'ln_beta': ln_beta}
    _L0_cond2_all = _L0_cond2_setup()
    _L0_cond2_in = {k: v for k, v in _L0_cond2_all.items() if k in ('rms_weight', 'Wk', 'Wo', 'ln_gamma', 'ln_beta')}
    del _L0_cond2_all

    def _L0_ffn_setup():
        import jax, jax.numpy as jnp
        import numpy as np
        D_MODEL = 512
        HIDDEN = int(2 * D_MODEL * 4 / 3)

        def ternary_quant(w):
            s = jnp.mean(jnp.abs(w))
            q = jnp.clip(jnp.round(w / s), -1.0, 1.0) * s
            return w + jax.lax.stop_gradient(q - w)
        key = jax.random.key(seed)
        k0, k1, k2, k3 = jax.random.split(key, 4)
        x = jax.random.normal(k0, (4, 1024, D_MODEL), dtype=jnp.float32)
        std_in = 1.0 / np.sqrt(D_MODEL)
        std_h = 1.0 / np.sqrt(HIDDEN)
        w1 = jax.random.uniform(k1, (HIDDEN, D_MODEL), jnp.float32, -std_in, std_in)
        w3 = jax.random.uniform(k2, (HIDDEN, D_MODEL), jnp.float32, -std_in, std_in)
        w2 = jax.random.uniform(k3, (D_MODEL, HIDDEN), jnp.float32, -std_h, std_h)
        return {'x': x, 'w1': w1, 'w3': w3, 'w2': w2}
    _L0_ffn_all = _L0_ffn_setup()
    _L0_ffn_in = {k: v for k, v in _L0_ffn_all.items() if k in ('w1', 'w3', 'w2')}
    del _L0_ffn_all
    return {'x': x, 'cond_2048': cond_2048, 'L0_cond_W_ih': _L0_cond_in['W_ih'], 'L0_cond_W_hh': _L0_cond_in['W_hh'], 'L0_cond_b_ih': _L0_cond_in['b_ih'], 'L0_cond_b_hh': _L0_cond_in['b_hh'], 'L0_attn_W_in': _L0_attn_in['W_in'], 'L0_attn_b_in': _L0_attn_in['b_in'], 'L0_attn_W_gate': _L0_attn_in['W_gate'], 'L0_attn_b_gate': _L0_attn_in['b_gate'], 'L0_attn_forget_lambda': _L0_attn_in['forget_lambda'], 'L0_cond2_rms_weight': _L0_cond2_in['rms_weight'], 'L0_cond2_Wk': _L0_cond2_in['Wk'], 'L0_cond2_Wo': _L0_cond2_in['Wo'], 'L0_cond2_ln_gamma': _L0_cond2_in['ln_gamma'], 'L0_cond2_ln_beta': _L0_cond2_in['ln_beta'], 'L0_ffn_w1': _L0_ffn_in['w1'], 'L0_ffn_w3': _L0_ffn_in['w3'], 'L0_ffn_w2': _L0_ffn_in['w2']}

def reference(x, cond_2048, L0_cond_W_ih, L0_cond_W_hh, L0_cond_b_ih, L0_cond_b_hh, L0_attn_W_in, L0_attn_b_in, L0_attn_W_gate, L0_attn_b_gate, L0_attn_forget_lambda, L0_cond2_rms_weight, L0_cond2_Wk, L0_cond2_Wo, L0_cond2_ln_gamma, L0_cond2_ln_beta, L0_ffn_w1, L0_ffn_w3, L0_ffn_w2):
    import jax
    import jax.numpy as jnp

    def _L0_cond_ref(initial_state, inputs, W_ih, W_hh, b_ih, b_hh):
        import jax, jax.numpy as jnp
        import numpy as np
        B, T, D = (16, 128, 512)
        "ScanOverTime(GRU cell): sequential per-timestep module call with\n            dict-state passing; merge_dict_trees stacks the per-step\n            'state_predicted' tensors along axis=1 -> [B, T, D]."

        def cell(h, x):
            gi = x @ W_ih + b_ih
            gh = h @ W_hh + b_hh
            i_r, i_z, i_n = jnp.split(gi, 3, axis=-1)
            h_r, h_z, h_n = jnp.split(gh, 3, axis=-1)
            r = jax.nn.sigmoid(i_r + h_r)
            z = jax.nn.sigmoid(i_z + h_z)
            n = jnp.tanh(i_n + r * h_n)
            h_new = (1.0 - z) * n + z * h
            return (h_new, h_new)
        xs = jnp.swapaxes(inputs, 0, 1)
        _, hs = jax.lax.scan(cell, initial_state, xs)
        return jnp.swapaxes(hs, 0, 1)

    def _L0_attn_ref(x, W_in, b_in, W_gate, b_gate, forget_lambda):
        import jax, jax.numpy as jnp
        import numpy as np
        C = 8.0

        def _linear_scan(alpha, xbeta):

            def combine(e1, e2):
                a1, b1 = e1
                a2, b2 = e2
                return (a2 * a1, a2 * b1 + b2)
            _, h = jax.lax.associative_scan(combine, (alpha, xbeta), axis=1)
            return h
        input_gate = jnp.einsum('btd,ed->bte', x, W_in) + b_in
        recurrence_gate = jnp.einsum('btd,ed->bte', x, W_gate) + b_gate
        alpha = jnp.exp(-C * jax.nn.softplus(forget_lambda) * jax.nn.sigmoid(recurrence_gate))
        beta = jnp.sqrt(1.0 - alpha ** 2 + 1e-06)
        xbeta = beta * jax.nn.sigmoid(input_gate) * x
        return _linear_scan(alpha, xbeta)

    def _L0_cond2_ref(inputs, layer_idx, rms_weight, query_vectors, Wk, Wo, ln_gamma, ln_beta):
        import jax, jax.numpy as jnp
        import numpy as np
        NUM_BLOCKS = 8
        NUM_LAYERS = 4
        EPS = 1e-06
        B, S, H = inputs.shape
        block_size = max(1, S // NUM_BLOCKS)
        n_blocks = S // block_size
        block_repr = inputs.reshape(B, n_blocks, block_size, H).sum(axis=2)
        keys = jnp.einsum('bnh,kh->bnk', block_repr, Wk)
        rms = jnp.sqrt(jnp.mean(keys * keys, axis=-1, keepdims=True) + EPS)
        keys = keys / rms * rms_weight
        q = query_vectors[layer_idx]
        scores = jnp.einsum('bnh,h->bn', keys, q)
        attn = jax.nn.softmax(scores, axis=-1)
        attended = jnp.einsum('bn,bnh->bh', attn, block_repr)
        attended = jnp.broadcast_to(attended[:, None, :], (B, S, H))
        proj = jnp.einsum('bsh,kh->bsk', attended, Wo)
        x = inputs + proj
        mu = jnp.mean(x, axis=-1, keepdims=True)
        var = jnp.mean((x - mu) ** 2, axis=-1, keepdims=True)
        out = (x - mu) / jnp.sqrt(var + EPS) * ln_gamma + ln_beta
        return out

    def _L0_ffn_ref(x, w1, w3, w2):
        import jax, jax.numpy as jnp
        import numpy as np
        D_MODEL = 512
        HIDDEN = int(2 * D_MODEL * 4 / 3)

        def ternary_quant(w):
            s = jnp.mean(jnp.abs(w))
            q = jnp.clip(jnp.round(w / s), -1.0, 1.0) * s
            return w + jax.lax.stop_gradient(q - w)
        w1q = ternary_quant(w1)
        w3q = ternary_quant(w3)
        w2q = ternary_quant(w2)
        h1 = jnp.einsum('bsd,hd->bsh', x, w1q)
        h3 = jnp.einsum('bsd,hd->bsh', x, w3q)
        g = jax.nn.silu(h1) * h3
        return jnp.einsum('bsh,dh->bsd', g, w2q)
    x = x + _L0_attn_ref(_L0_cond_ref(cond_2048, x, L0_cond_W_ih, L0_cond_W_hh, L0_cond_b_ih, L0_cond_b_hh), L0_attn_W_in, L0_attn_b_in, L0_attn_W_gate, L0_attn_b_gate, L0_attn_forget_lambda)
    x = x + _L0_ffn_ref(_L0_cond2_ref(x, 1, L0_cond2_rms_weight, cond_2048, L0_cond2_Wk, L0_cond2_Wo, L0_cond2_ln_gamma, L0_cond2_ln_beta), L0_ffn_w1, L0_ffn_w3, L0_ffn_w2)
    return x

_drawn_inputs = setup_inputs


def setup_inputs(seed=0):
    import zlib

    import numpy as np

    out = dict(_drawn_inputs(seed))
    spreads = {'L0_cond_b_ih': (0.0, 0.1),
     'L0_cond_b_hh': (0.0, 0.1),
     'L0_attn_b_in': (0.0, 0.333),
     'L0_attn_b_gate': (0.0, 0.8),
     'L0_cond2_rms_weight': (1.0, 0.6),
     'L0_cond2_ln_gamma': (1.0, 0.6),
     'L0_cond2_ln_beta': (0.0, 0.8)}
    factors = {}
    for name, (base, spread) in spreads.items():
        noise = np.random.default_rng([zlib.crc32(name.encode()), seed]).standard_normal(out[name].shape)
        drawn = base * np.exp(spread * noise) if base else spread * noise
        out[name] = jnp.asarray(drawn.astype(out[name].dtype))
    for name, factor in factors.items():
        out[name] = (out[name] * factor).astype(out[name].dtype)
    return out
```

```python
from contextlib import ExitStack

import concourse.bass as bass
from concourse import mybir
import numpy as np

ALU = mybir.AluOpType
ACT = mybir.ActivationFunctionType
AX = mybir.AxisListType
F32 = mybir.dt.float32
F16 = mybir.dt.float16
BF16 = mybir.dt.bfloat16
U32 = mybir.dt.uint32
RMAX = bass.bass_isa.ReduceOp.max
RADD = bass.bass_isa.ReduceOp.add

P = 128
B, T, D = 4, 512, 512
KT = D // P
G3 = 3 * D
HID = 1365
CH = 16
NCH = T // CH
TOK = CH * B
SB = KT * B
XT = 32
NXT = T // XT


def gru(nc, x, cond, W_ih, W_hh, b_ih, b_hh, W_in, b_in, W_gate, b_gate, lam_d, rmsw, Wk, Wo, gam, bet, w1, w3, w2, ident_d, sel_d, out):
    with ExitStack() as ctx:
        def sb(name, shape, dt=F32):
            return ctx.enter_context(nc.sbuf_tensor(name, shape, dt))

        def sem(name):
            return ctx.enter_context(nc.semaphore(name))

        HT = (HID + P - 1) // P
        HP = HT * P
        A_reg = sb("A_reg", [P, KT * T * B])
        B_reg = sb("B_reg", [P, KT * T * B])
        X_reg = sb("X_reg", [P, KT * (T + 2 * CH) * B])
        W_reg = sb("W_reg", [P, 16640])
        Q_reg = sb("Q_reg", [P, 3 * KT * HP // 2])

        def view(reg, at, shape, dt=F32):
            n = int(np.prod(shape))
            words = n if dt == F32 else n // 2
            a = reg[:, at:at + words]
            if dt != F32:
                a = a.bitcast(dt)
            names = "abcd"[:len(shape)]
            return a.rearrange("p (%s) -> p %s" % (" ".join(names), " ".join(names)), **dict(zip(names, shape)))

        xT = view(X_reg, 0, [KT, T + 2 * CH, B])
        wih = view(W_reg, 0, [KT, G3])
        wh16 = view(W_reg, KT * G3, [2, KT, G3], F16)
        wgT = view(W_reg, 2 * KT * G3, [2, KT, D])
        sih = view(A_reg, 0, [KT, T, B])
        sgate = view(B_reg, 0, [KT, T, B])
        whh = view(A_reg, 0, [KT, G3])
        xnat = view(B_reg, 0, [NXT, D])
        wnat = view(W_reg, KT * G3, [2, KT, D])
        tmp = view(W_reg, 0, [KT, T * B])
        WT = view(W_reg, 0, [2, KT, D])
        nat = view(W_reg, 8192, [KT * HP])
        qn = view(W_reg, 8192 + KT * HP, [KT * HP], F16)
        wkn = view(Q_reg, 4352, [2, KT, D])
        q1T = view(Q_reg, 0, [KT, HP], F16)
        q3T = view(Q_reg, KT * HP // 2, [KT, HP], F16)
        q2T = view(Q_reg, KT * HP, [HT, D], F16)
        X2 = view(B_reg, 0, [KT, B, T])
        xc = view(A_reg, 0, [KT, T])
        sq = view(A_reg, 2048, [KT, T])
        yhl = view(A_reg, 4096, [2, 2, KT * T], F16)
        gp = view(X_reg, 0, [3, HT, T], BF16)
        sl = view(W_reg, 4096, [2, T])
        gf = view(W_reg, 5120, [2, T])
        g1 = view(W_reg, 6144, [2, T])
        xn = view(W_reg, 0, [2, D])
        ob = view(W_reg, 1024, [2, D])
        std = view(W_reg, 2048, [2, T])
        brT = sb("brT", [P, KT, 32])
        br2 = sb("br2", [P, KT, 32])
        attT = sb("attT", [P, KT * B])
        projT = sb("projT", [P, KT * B])
        ones = sb("ones", [P, P])
        ones1 = sb("ones1", [P, P])
        kq = sb("kq", [32, D])
        kqr = sb("kqr", [32, D])
        sm = sb("sm", [32, 16])
        at1 = sb("at1", [1, 128])
        gb = sb("gb", [P, 4 * KT])
        gb2 = sb("gb2", [P, KT])
        id16 = sb("id16", [P, P], F16)
        lam = sb("lam", [P, 6 * KT])
        fq = sb("fq", [P, 32])
        xs = view(Q_reg, 0, [KT, TOK])
        gi_next = view(Q_reg, 256, [CH, 64])
        gi_cur = view(Q_reg, 1280, [CH, 64])
        hist = view(Q_reg, 2304, [CH, SB])
        hprev = view(Q_reg, 2560, [CH, SB])
        sin_c = view(Q_reg, 2816, [KT, TOK])
        H = sb("H", [P, KT, 16], F16)
        C = view(Q_reg, 3072, [3, P])
        r_il = sb("r_il", [P, 2 * SB])
        y = sb("y", [P, 2 * SB])
        n_t = sb("n_t", [P, SB])
        z_t = sb("z_t", [P, SB])
        omz = sb("omz", [P, SB])
        zh = sb("zh", [P, SB])
        v_t = sb("v_t", [P, SB])
        ident = sb("ident", [P, P])
        selm = sb("selm", [P, 48])
        sel = sb("sel", [P, 48])
        bih = sb("bih", [P, 12])
        bhh = sb("bhh", [P, 12])
        bsum = sb("bsum", [P, 12])
        brow = sb("brow", [P, 64])
        zero4 = sb("zero4", [P, 8])
        bat = sb("bat", [P, 2, KT])
        condn = Q_reg[0:B, 3456:3456 + D]
        condT = sb("condT", [P, SB])
        mx = sb("mx", [P, 8])
        scl = sb("scl", [P, 8])

        bank = [ctx.enter_context(nc.psum_tensor(f"bank{k}", [P, 512], F32)) for k in range(8)]
        Gr, Gn, Gz, Pr, Pn, Pz = bank[0:6]
        F = bank[6:8]

        S = {}
        for n in ("ld_x ld_wih ld_whh ld_w ld_c ld_small tr tr_e0 tr_e1 wmax amax scale w16 hinit consts "
                  "gr gn gz cr cn cz pr pn pz sr scan th sz hp hs fil gi_e at_e xs_c gc_a gc_b hp_c sih_c out0 out1 chain ginit ld_v ld_wk ld_nat nat0 xq absq aq hsq qa qn_r tq tq_e0 tq_e1 wkT wkT_e c8 e_x e_s e_q xb sc x2 br keys ssq dot rms scr scT mxs ex den att atb prod attT pj pjs x3 mean xcs sqs var stds rst yn yf yh yl st1 slu gfd ghi gm1 gmid glo o2 xt xns obs yB").split():
            S[n] = sem("s_" + n)

        block = ctx.enter_context(nc.Block())

        def jobs(s, attn):
            l = []
            if s < 12:
                l.append(("gi", s))
            if attn:
                if s in (1, 4, 7, 10):
                    l.append(("at", (1, 4, 7, 10).index(s)))
                if s >= 12:
                    l.append(("at", 4 + s - 12))
            return l

        @block.sync
        def _(sp):
            sp.dma_start(ident[:, :], ident_d).then_inc(S["ld_c"], 16)
            sp.dma_start(selm[:, :], sel_d).then_inc(S["ld_c"], 16)
            sp.dma_start(condn[:, :], cond).then_inc(S["ld_c"], 16)
            with nc.allow_non_contiguous_dma(reason="small vectors"):
                sp.dma_start(bih[:, :], b_ih.rearrange("(m p) -> p m", p=P)).then_inc(S["ld_small"], 16)
                sp.dma_start(bhh[:, :], b_hh.rearrange("(m p) -> p m", p=P)).then_inc(S["ld_small"], 16)
                sp.dma_start(bat[:, 0, :], b_in.rearrange("(m p) -> p m", p=P)).then_inc(S["ld_small"], 16)
                sp.dma_start(bat[:, 1, :], b_gate.rearrange("(m p) -> p m", p=P)).then_inc(S["ld_small"], 16)
            sp.dma_start(whh, W_hh.rearrange("(k p) n -> p k n", p=P)).then_inc(S["ld_whh"], 16)
            sp.dma_start(wnat[:, 0], W_in.rearrange("(m p) d -> p m d", p=P)).then_inc(S["ld_w"], 16)
            sp.dma_start(wnat[:, 1], W_gate.rearrange("(m p) d -> p m d", p=P)).then_inc(S["ld_w"], 16)
            for c in range(NXT):
                for b in range(B):
                    sp.dma_start(xnat[XT * b:XT * b + XT, c, :], x[b, XT * c:XT * c + XT, :]).then_inc(S["ld_x"], 16)
            sp.dma_start(wih[:, :, :], W_ih.rearrange("(k p) n -> p k n", p=P)).then_inc(S["ld_wih"], 16)
            with nc.allow_non_contiguous_dma(reason="small vectors"):
                sp.dma_start(lam[:, 0:KT], lam_d.rearrange("(m p) -> p m", p=P)).then_inc(S["ld_v"], 16)
                sp.dma_start(gb[:, 0:KT], gam.rearrange("(m p) -> p m", p=P)).then_inc(S["ld_v"], 16)
                sp.dma_start(gb[:, KT:2 * KT], bet.rearrange("(m p) -> p m", p=P)).then_inc(S["ld_v"], 16)
            sp.dma_start(kqr[:, :], rmsw.unsqueeze(0).broadcast_to([32, D])).then_inc(S["ld_v"], 16)
            sp.dma_start(kq[:, :], cond[1:2, :].broadcast_to([32, D])).then_inc(S["ld_v"], 16)
            sp.wait_ge(S["hinit"], 3)
            sp.dma_start(wkn[:, 0], Wk.rearrange("(m p) d -> p m d", p=P)).then_inc(S["ld_wk"], 16)
            sp.dma_start(wkn[:, 1], Wo.rearrange("(m p) d -> p m d", p=P)).then_inc(S["ld_wk"], 16)
            nfull = HID // P
            rest = HID - nfull * P
            for n, w in enumerate((w1, w3, w2)):
                sp.wait_ge(S["nat0"], n + 1)
                if n < 2:
                    v = nat.rearrange("p (h d) -> p h d", d=D)
                    sp.dma_start(v[:, 0:nfull, :], w[0:nfull * P, :].rearrange("(h p) d -> p h d", p=P)).then_inc(S["ld_nat"], 16)
                    sp.dma_start(v[0:rest, nfull, :], w[nfull * P:HID, :]).then_inc(S["ld_nat"], 16)
                else:
                    v = nat.rearrange("p (k h) -> p k h", k=KT)
                    for k in range(2):
                        sp.dma_start(v[:, 2 * k:2 * k + 2, 0:HID], w.rearrange("(k p) h -> p k h", p=P)[:, 2 * k:2 * k + 2, :]).then_inc(S["ld_nat"], 16)
            for b in range(B):
                for tt in range(4):
                    n = 4 * b + tt
                    sp.wait_ge(S["obs"], n + 1)
                    sp.dma_start(out[b, tt * P:(tt + 1) * P, :], ob[:, n % 2, :]).then_inc(S["out%d" % (n % 2)], 16)
            sp.wait_ge(S["out0"], 8 * 16)
            sp.wait_ge(S["out1"], 8 * 16)

        @block.gpsimd
        def _(pool):
            pool.wait_ge(S["wmax"], 2)
            nc.gpsimd.partition_all_reduce(mx[:, 2:4], mx[:, 0:2], P, RMAX).then_inc(S["amax"], 1)

            pool.wait_ge(S["xq"], 1)
            nc.gpsimd.partition_all_reduce(fq[:, 10:12], fq[:, 8:10], P, RMAX).then_inc(S["xq"], 1)

            def load_xs(chunk, n_before):
                pool.wait_ge(S["ginit"], 12)
                if not isinstance(n_before, int) or n_before:
                    pool.wait_ge(S["gi_e"], 12 * n_before)
                nc.gpsimd.tensor_copy(xs[:, :, :].rearrange("p k (t b) -> p k t b", b=B),
                                      xT[:, :, bass.ds(chunk * CH, CH), :]).then_inc(S["xs_c"], 1)

            load_xs(1, 0)

            def chunk(i, attn):
                if attn:
                    pool.wait_ge(S["amax"], 1)
                    pool.wait_ge(S["hs"], CH * i)
                    pool.wait_ge(S["at_e"], 8 * i)
                    pool.wait_ge(S["sih_c"], i)
                    nc.gpsimd.tensor_tensor(hprev[:, :, :], hist[:, :, :], scl[:, 2:3].unsqueeze(2).broadcast_to([P, CH, SB]), ALU.mult).then_inc(S["hp_c"], 1)
                pool.wait_ge(S["amax"], 1)
                pool.wait_ge(S["gi_e"], 12 * (i + 1))
                pool.wait_ge(S["pr"], CH * i + 12)
                pool.wait_ge(S["pz"], CH * i + 12)
                nc.gpsimd.tensor_tensor(gi_cur[:, 0:12, :], gi_next[:, 0:12, :], brow[:, :].unsqueeze(1).broadcast_to([P, 12, 64]), ALU.add).then_inc(S["gc_a"], 1)
                load_xs(i + 2, i + 1)
                if attn:
                    pool.wait_ge(S["at_e"], 8 * i + 4)
                    pool.wait_ge(S["hp_c"], i)
                    nc.gpsimd.tensor_tensor(
                        sih[:, :, bass.ds((i - 1) * CH, CH), :].rearrange("p k t b -> p k t b"),
                        sin_c[:, :, :].rearrange("p k (t b) -> p k t b", b=B),
                        hprev[:, :, :].rearrange("p t (k b) -> p k t b", b=B), ALU.mult).then_inc(S["sih_c"], 1)
                pool.wait_ge(S["amax"], 1)
                pool.wait_ge(S["pr"], CH * i + 16)
                pool.wait_ge(S["pz"], CH * i + 16)
                nc.gpsimd.tensor_tensor(gi_cur[:, 12:16, :], gi_next[:, 12:16, :], brow[:, :].unsqueeze(1).broadcast_to([P, 4, 64]), ALU.add).then_inc(S["gc_b"], 1)

            chunk(0, False)
            with pool.Fori(1, NCH) as i:
                chunk(i, True)

            pool.wait_ge(S["hs"], T)
            pool.wait_ge(S["at_e"], 8 * NCH)
            pool.wait_ge(S["sih_c"], NCH)
            nc.gpsimd.tensor_tensor(hprev[:, :, :], hist[:, :, :], scl[:, 2:3].unsqueeze(2).broadcast_to([P, CH, SB]), ALU.mult).then_inc(S["hp_c"], 1)
            pool.wait_ge(S["at_e"], 8 * NCH + 4)
            pool.wait_ge(S["hp_c"], NCH)
            nc.gpsimd.tensor_tensor(sih[:, :, T - CH:T, :], sin_c[:, :, :].rearrange("p k (t b) -> p k t b", b=B),
                                    hprev[:, :, :].rearrange("p t (k b) -> p k t b", b=B), ALU.mult).then_inc(S["sih_c"], 1)
            for n in range(3):
                if n == 0:
                    pool.wait_ge(S["fil"], 24 + 20 * (NCH - 1) + 8)
                else:
                    pool.wait_ge(S["qn_r"], n)
                nc.gpsimd.memset(nat, 0.0).then_inc(S["nat0"], 1)
                pool.wait_ge(S["absq"], n + 1)
                nc.gpsimd.partition_all_reduce(fq[:, 4 + n:5 + n], fq[:, n:n + 1], P, RADD).then_inc(S["aq"], 1)
                if n == 0:
                    for k in range(KT):
                        pool.wait_ge(S["sc"], 4 * k + 4)
                        nc.gpsimd.tensor_tensor(X2[:, k], xT[:, k, 0:T, :].rearrange("p t b -> p b t"),
                                                sih[:, k].rearrange("p t b -> p b t"), ALU.add).then_inc(S["x2"], 1)

        @block.tensor
        def _(pe):
            pe.wait_ge(S["ld_c"], 48)
            pe.wait_ge(S["consts"], 1)
            n = 0

            def bank_free(n):
                if n >= 4:
                    pe.wait_ge(S["tr_e0"] if n % 2 == 0 else S["tr_e1"], (n - 4) // 2 + 1)

            pe.wait_ge(S["ld_w"], 32)
            for w in range(2):
                for k in range(KT):
                    bank_free(n)
                    for m in range(KT):
                        mm = pe.transpose(bank[n % 4][:, m * P:(m + 1) * P], wnat[:, w, m, k * P:(k + 1) * P], ident[:, :])
                    mm.then_inc(S["tr"], 1)
                    n += 1
            for c in range(NXT):
                pe.wait_ge(S["ld_x"], 64 * NXT)
                bank_free(n)
                for k in range(KT):
                    mm = pe.transpose(bank[n % 4][:, k * P:(k + 1) * P], xnat[:, c, k * P:(k + 1) * P], ident[:, :])
                mm.then_inc(S["tr"], 1)
                n += 1
            bank_free(n)
            for k in range(KT):
                mm = pe.transpose(bank[n % 4][:, k * B:(k + 1) * B], condn[:, k * P:(k + 1) * P], ident[0:B, 0:B])
            mm.then_inc(S["tr"], 1)

            pe.wait_ge(S["ld_wih"], 16)
            pe.wait_ge(S["tr_e0"], 12)
            pe.wait_ge(S["tr_e1"], 12)
            for m in range(12):
                if m >= 2:
                    pe.wait_ge(S["ginit"], m - 1)
                for k in range(KT):
                    mm = pe.matmul(F[m % 2][:, 0:TOK], wih[:, k, m * P:(m + 1) * P],
                                   xT[:, k, 0:CH, :].rearrange("p t b -> p (t b)"), start=(k == 0), stop=(k == KT - 1))
                mm.then_inc(S["fil"], 1)
            pe.wait_ge(S["hinit"], 3)
            pe.wait_ge(S["w16"], 2 * KT)
            pe.wait_ge(S["ginit"], 12)

            fcount = [12]

            def step(i, s, attn):
                t = i * CH + s
                if s == 0 and attn:
                    pe.wait_ge(S["gc_a"], i)
                if s == 12 and attn:
                    pe.wait_ge(S["gc_b"], i)
                if attn or s:
                    pe.wait_ge(S["sr"], t)
                    pe.wait_ge(S["scan"], t)
                    pe.wait_ge(S["sz"], t)
                pe.matmul(Pr[:, 0:SB], ident[:, :], gi_cur[:, s, 0:16], start=True, stop=False)
                pe.matmul(Pn[:, 0:2 * SB], ident[:, :], gi_cur[:, s, 32:64], start=True, stop=False)
                pe.matmul(Pz[:, 0:SB], ident[:, :], gi_cur[:, s, 16:32], start=True, stop=False)
                if attn or s:
                    pe.wait_ge(S["hp"], t)
                for g, bk, done in ((0, Gr, "gr"), (2, Gn, "gn"), (1, Gz, "gz")):
                    for w in range(2):
                        for k in range(KT):
                            for j in range(4):
                                mm = pe.matmul(bk[32 * j:32 * j + 16, 0:P], H[:, k, :],
                                               wh16[:, w, k, g * D + j * P:g * D + (j + 1) * P],
                                               start=(w == 0 and k == 0), stop=(w == 1 and k == KT - 1))
                    mm.then_inc(S[done], 1)
                for c, bk, wd, off, cs, ps in ((0, Pr, SB, 0, "cr", "pr"), (1, Pn, 2 * SB, 16, "cn", "pn"), (2, Pz, SB, 0, "cz", "pz")):
                    pe.wait_ge(S[cs], t + 1)
                    pe.matmul(bk[:, 0:wd], C[:, c, :], sel[:, off:off + wd], start=False, stop=True).then_inc(S[ps], 1)
                for kind, m in jobs(s, attn):
                    jl = [x for ss in range(CH) for x in jobs(ss, attn)]
                    q = jl.index((kind, m))
                    if q < 2:
                        pe.wait_ge(S["gi_e"], 12 * i)
                        if attn:
                            pe.wait_ge(S["at_e"], 8 * i)
                    else:
                        pk, pm = jl[q - 2]
                        if pk == "gi":
                            pe.wait_ge(S["gi_e"], 12 * i + pm + 1)
                        else:
                            pe.wait_ge(S["at_e"], 8 * i + pm + 1)
                    bk = F[q % 2]
                    if kind == "gi":
                        if m == 0:
                            pe.wait_ge(S["xs_c"], i + 1)
                        for k in range(KT):
                            mm = pe.matmul(bk[:, 0:TOK], wih[:, k, m * P:(m + 1) * P], xs[:, k, :],
                                           start=(k == 0), stop=(k == KT - 1))
                    else:
                        if m == 0:
                            pe.wait_ge(S["hp_c"], i)
                        w, e = divmod(m, KT)
                        for k in range(KT):
                            mm = pe.matmul(bk[:, 0:TOK], wgT[:, w, k, e * P:(e + 1) * P],
                                           hprev[:, :, k * B:(k + 1) * B], start=(k == 0), stop=(k == KT - 1))
                    mm.then_inc(S["fil"], 1)

            for s in range(CH):
                step(0, s, False)
            with pe.Fori(1, NCH) as i:
                for s in range(CH):
                    step(i, s, True)

            pe.wait_ge(S["hp_c"], NCH)
            for m in range(8):
                if m < 2:
                    pe.wait_ge(S["gi_e"], 12 * NCH)
                    pe.wait_ge(S["at_e"], 8 * NCH)
                else:
                    pe.wait_ge(S["at_e"], 8 * NCH + m - 1)
                w, e = divmod(m, KT)
                for k in range(KT):
                    mm = pe.matmul(F[m % 2][:, 0:TOK], wgT[:, w, k, e * P:(e + 1) * P],
                                   hprev[:, :, k * B:(k + 1) * B], start=(k == 0), stop=(k == KT - 1))
                mm.then_inc(S["fil"], 1)
            pe.wait_ge(S["ld_wk"], 32)
            for n in range(8):
                w, k = divmod(n, KT)
                if n >= 4:
                    pe.wait_ge(S["wkT_e"], n - 3)
                for m in range(KT):
                    mm = pe.transpose(bank[n % 4][:, m * P:(m + 1) * P], wkn[:, w, m, k * P:(k + 1) * P], ident[:, :])
                mm.then_inc(S["wkT"], 1)
            pe.wait_ge(S["wkT_e"], 8)
            nb = 0
            for n in range(3):
                pe.wait_ge(S["qn_r"], n + 1)
                for blk in range(HT * KT):
                    if blk % 8 == 0:
                        if nb >= 4:
                            pe.wait_ge(S["tq_e0"] if nb % 2 == 0 else S["tq_e1"], (nb - 4) // 2 + 1)
                        bk = bank[nb % 4][:, :].bitcast(F16)
                    if n < 2:
                        k, h = divmod(blk, HT)
                        src = qn[:, h * D + k * P:h * D + (k + 1) * P]
                    else:
                        h, k = divmod(blk, KT)
                        src = qn[:, k * HP + h * P:k * HP + (h + 1) * P]
                    mm = pe.transpose(bk[:, (blk % 8) * P:(blk % 8 + 1) * P], src, id16[:, :])
                    if blk % 8 == 7 or blk == HT * KT - 1:
                        mm.then_inc(S["tq"], 1)
                        nb += 1
            pe.wait_ge(S["br"], KT)
            for k in range(KT):
                mm = pe.matmul(bank[4][0:32, :], brT[:, k, :], WT[:, 0, k, :], start=(k == 0), stop=(k == KT - 1))
            mm.then_inc(S["keys"], 1)
            pe.wait_ge(S["scr"], 1)
            pe.transpose(bank[5][0:1, 0:32], sm[:, 4:5], ident[0:32, 0:32]).then_inc(S["scT"], 1)
            pe.wait_ge(S["att"], 1)
            pe.matmul(bank[6][:, 0:32], ones1[0:1, :], at1[0:1, 96:128], start=True, stop=True).then_inc(S["atb"], 1)
            pe.wait_ge(S["attT"], 1)
            for m in range(KT):
                for k in range(KT):
                    mm = pe.matmul(bank[7][:, m * B:(m + 1) * B], WT[:, 1, k, m * P:(m + 1) * P], attT[:, k * B:(k + 1) * B],
                                   start=(k == 0), stop=(k == KT - 1))
            mm.then_inc(S["pj"], 1)
            hA, hB, Ob, Lb, Tb = bank[0:2], bank[2:4], bank[4:6], bank[6], bank[7]

            def ln_mean(b):
                pe.wait_ge(S["x3"], b + 1)
                if b:
                    pe.wait_ge(S["stds"], b)
                for k in range(KT):
                    mm = pe.matmul(Lb[:, :], ones[:, :], xc[:, k, :], start=(k == 0), stop=(k == KT - 1))
                mm.then_inc(S["mean"], 1)

            def ln_var(b):
                pe.wait_ge(S["xcs"], b + 1)
                pe.wait_ge(S["sqs"], b + 1)
                for k in range(KT):
                    mm = pe.matmul(Lb[:, :], ones[:, :], sq[:, k, :], start=(k == 0), stop=(k == KT - 1))
                mm.then_inc(S["var"], 1)

            pe.wait_ge(S["tq_e0"], 9)
            pe.wait_ge(S["tq_e1"], 9)
            pe.wait_ge(S["pjs"], 1)
            ln_mean(0)
            ln_var(0)
            for b in range(B):
                pe.wait_ge(S["yl"], b + 1)
                pe.wait_ge(S["yh"], b + 1)
                for h in range(HT):
                    n = HT * b + h
                    if n >= 2:
                        pe.wait_ge(S["gfd"], n - 1)
                    hb = hA if n % 2 == 0 else hB
                    for qT, bk in ((q1T, hb[0]), (q3T, hb[1])):
                        for k in range(KT):
                            for part in range(2):
                                mm = pe.matmul(bk[:, :], qT[:, k, h * P:(h + 1) * P], yhl[:, b % 2, part, k * T:(k + 1) * T],
                                               start=(k == 0 and part == 0), stop=(k == KT - 1 and part == 1))
                    mm.then_inc(S["st1"], 1)
                    if b < B - 1 and h == 3:
                        ln_mean(b + 1)
                    if b < B - 1 and h == 7:
                        ln_var(b + 1)
                for tt in range(4):
                    n = 4 * b + tt
                    if n >= 1:
                        pe.wait_ge(S["xns"], n)
                    for k in range(KT):
                        mm = pe.transpose(Tb[:, k * P:(k + 1) * P], X2[:, k, b, tt * P:(tt + 1) * P], ident[:, :])
                    mm.then_inc(S["xt"], 1)
                    if n >= 2:
                        pe.wait_ge(S["obs"], n - 1)
                    for h in range(HT):
                        if tt == 0:
                            pe.wait_ge(S["glo"], HT * b + h + 1)
                            pe.wait_ge(S["gmid"], HT * b + h + 1)
                        for part in range(3):
                            mm = pe.matmul(Ob[n % 2][:, :], gp[:, part, h, tt * P:(tt + 1) * P], q2T[:, h, :],
                                           start=(h == 0 and part == 0), stop=(h == HT - 1 and part == 2))
                    mm.then_inc(S["o2"], 1)

        @block.scalar
        def _(act):
            for n in range(1, 24, 2):
                act.wait_ge(S["tr"], n + 1)
                if n < 8:
                    act.copy(wgT[:, n // KT, n % KT, :], bank[n % 4][:, :]).then_inc(S["tr_e1"], 1)
                else:
                    c = n - 8
                    act.copy(xT[:, :, XT * c:XT * c + XT, :].rearrange("p k t b -> p k b t"),
                             bank[n % 4][:, :].rearrange("p (k b t) -> p k b t", k=KT, b=B)).then_inc(S["tr_e1"], 1)
            act.wait_ge(S["scale"], 2)
            act.wait_ge(S["tr_e0"], 4)
            act.wait_ge(S["tr_e1"], 4)
            for k in range(KT):
                act.activation(wh16[:, 0, k, :], whh[:, k, :], ACT.Copy, scale=scl[:, 1:2]).then_inc(S["w16"], 1)

            act.wait_ge(S["c8"], 1)
            act.activation(lam[:, 8:12], lam[:, 4:8], ACT.Exp).then_inc(S["c8"], 1)
            act.wait_ge(S["c8"], 2)
            act.activation(lam[:, 12:16], lam[:, 8:12], ACT.Ln, bias=1.0).then_inc(S["c8"], 1)

            def step(i, s, attn):
                t = i * CH + s
                act.wait_ge(S["gr"], t + 1)
                act.copy(C[:, 0, :], Gr[:, 0:P]).then_inc(S["cr"], 1)
                act.wait_ge(S["pr"], t + 1)
                act.activation(r_il[:, 1:2 * SB:2], Pr[:, 0:SB], ACT.Sigmoid).then_inc(S["sr"], 1)
                act.wait_ge(S["scan"], t + 1)
                act.activation(n_t[:, :], y[:, 1:2 * SB:2], ACT.Tanh).then_inc(S["th"], 1)
                act.wait_ge(S["pz"], t + 1)
                act.activation(omz[:, :], Pz[:, 0:SB], ACT.Sigmoid, scale=-1.0).then_inc(S["th"], 1)
                act.activation(z_t[:, :], Pz[:, 0:SB], ACT.Sigmoid).then_inc(S["sz"], 1)
                for kind, m in jobs(s, attn):
                    if kind != "at":
                        continue
                    jl = [x for ss in range(CH) for x in jobs(ss, attn)]
                    q = jl.index((kind, m))
                    w, e = divmod(m, KT)
                    act.wait_ge(S["fil"], 24 + 20 * (i - 1) + q + 1)
                    if w == 0:
                        if e == 0:
                            act.wait_ge(S["sih_c"], i)
                        o = sin_c[:, e, :]
                        act.activation(o, F[q % 2][:, 0:TOK], ACT.Sigmoid, bias=bat[:, w, e:e + 1]).then_inc(S["at_e"], 1)
                    else:
                        o = sgate[:, e, bass.ds((i - 1) * CH, CH), :]
                        act.activation(o, F[q % 2][:, 0:TOK].rearrange("p (t b) -> p t b", b=B), ACT.Sigmoid,
                                       bias=bat[:, w, e:e + 1]).then_inc(S["at_e"], 1)

            for s in range(CH):
                step(0, s, False)
            with act.Fori(1, NCH) as i:
                for s in range(CH):
                    step(i, s, True)

            for m in range(8):
                w, e = divmod(m, KT)
                act.wait_ge(S["fil"], 24 + 20 * (NCH - 1) + m + 1)
                if m == 0:
                    act.wait_ge(S["sih_c"], NCH)
                if w == 0:
                    act.activation(sin_c[:, e, :], F[m % 2][:, 0:TOK], ACT.Sigmoid, bias=bat[:, w, e:e + 1]).then_inc(S["at_e"], 1)
                else:
                    act.activation(sgate[:, e, T - CH:T, :], F[m % 2][:, 0:TOK].rearrange("p (t b) -> p t b", b=B), ACT.Sigmoid,
                                   bias=bat[:, w, e:e + 1]).then_inc(S["at_e"], 1)
            act.wait_ge(S["at_e"], 8 * NCH + 8)
            act.wait_ge(S["fil"], 24 + 20 * (NCH - 1) + 8)
            al = B_reg[:, :].rearrange("p (k n) -> p k n", k=KT)
            for k in range(KT):
                act.activation(al[:, k], al[:, k], ACT.Exp, scale=lam[:, 16 + k:17 + k]).then_inc(S["e_x"], 1)
            for k in range(KT):
                act.wait_ge(S["e_x"], k + 1)
                act.activation(tmp[:, k], al[:, k], ACT.Square).then_inc(S["e_s"], 1)
            for k in range(KT):
                act.wait_ge(S["e_s"], k + 1)
                act.activation(tmp[:, k], tmp[:, k], ACT.Sqrt, scale=-1.0, bias=gb[:, 12:13]).then_inc(S["e_q"], 1)
            for n in range(8):
                w, k = divmod(n, KT)
                act.wait_ge(S["wkT"], n + 1)
                if n == 0:
                    act.wait_ge(S["xb"], 2)
                act.copy(WT[:, w, k, :], bank[n % 4][:, :]).then_inc(S["wkT_e"], 1)
            nb = 0
            for n in range(3):
                act.wait_ge(S["ld_nat"], 32 * (n + 1))
                if n:
                    act.wait_ge(S["qn_r"], n)
                act.wait_ge(S["tq_e1"], nb // 2) if nb else None
                act.activation(qn, nat, ACT.Abs, accum_out=fq[:, n:n + 1]).then_inc(S["absq"], 1)
                for _ in range(6):
                    if nb % 2:
                        act.wait_ge(S["tq"], nb + 1)
                        g = nb % 6
                        w = 1024 if g < 5 else 512
                        dst = Q_reg[:, n * KT * HP // 2 + 512 * g:n * KT * HP // 2 + 512 * g + w // 2].bitcast(F16)
                        act.copy(dst, bank[nb % 4][:, 0:w // 2].bitcast(F16)).then_inc(S["tq_e1"], 1)
                    nb += 1
            act.wait_ge(S["keys"], 1)
            act.activation(xc[0:32, 0, :], bank[4][0:32, :], ACT.Square, accum_out=sm[:, 0:1]).then_inc(S["ssq"], 1)
            act.wait_ge(S["ssq"], 1)
            act.activation(sm[:, 1:2], sm[:, 0:1], ACT.Sqrt, scale=1.0 / D, bias=gb[0:32, 13:14]).then_inc(S["rms"], 1)
            act.wait_ge(S["mxs"], 1)
            act.activation(at1[0:1, 32:64], at1[0:1, 0:32], ACT.Exp).then_inc(S["ex"], 1)

            def ln_sq(b):
                act.wait_ge(S["xcs"], b + 1)
                if b:
                    act.wait_ge(S["yl"], b)
                act.activation(sq[:, :, :], xc[:, :, :], ACT.Square).then_inc(S["sqs"], 1)

            def ln_act(b):
                act.wait_ge(S["var"], b + 1)
                act.activation(std[:, 0, :], Lb[:, :], ACT.Sqrt, bias=gb[:, 13:14]).then_inc(S["stds"], 1)
                act.wait_ge(S["yn"], b + 1)
                if b >= 2:
                    act.wait_ge(S["st1"], HT * (b - 1))
                for k in range(KT):
                    act.activation(sq[:, k, :], xc[:, k, :], ACT.Identity, scale=gb[:, 8 + k:9 + k], bias=gb2[:, k:k + 1]).then_inc(S["yf"], 1)
                for k in range(KT):
                    act.activation(yhl[:, b % 2, 0, k * T:(k + 1) * T], xc[:, k, :], ACT.Identity, scale=gb[:, 8 + k:9 + k], bias=gb2[:, k:k + 1]).then_inc(S["yB"], 1)
                act.wait_ge(S["yB"], 4 * (b + 1))
                act.activation(fq[:, 30:31], fq[:, 29:30], ACT.Copy).then_inc(S["yh"], 1)

            Lb = bank[6]
            ln_sq(0)
            ln_act(0)
            for b in range(B):
                for h in range(HT):
                    n = HT * b + h
                    hb = bank[0:2] if n % 2 == 0 else bank[2:4]
                    act.wait_ge(S["st1"], n + 1)
                    if n >= 2:
                        act.wait_ge(S["gfd"], n - 1)
                    act.activation(sl[:, n % 2, :], hb[0][:, :], ACT.Silu, scale=fq[:, 16:17]).then_inc(S["slu"], 1)
                    act.wait_ge(S["gfd"], n + 1)
                    if h == 0 and b:
                        act.wait_ge(S["o2"], 4 * b)
                    act.copy(gp[:, 0, h, :], gf[:, n % 2, :]).then_inc(S["ghi"], 1)
                    act.wait_ge(S["gm1"], n + 1)
                    act.copy(gp[:, 1, h, :], g1[:, n % 2, :]).then_inc(S["gmid"], 1)
                    if b < B - 1 and h == 5:
                        ln_sq(b + 1)
                    if b < B - 1 and h == 8:
                        ln_act(b + 1)
                for tt in range(4):
                    n = 4 * b + tt
                    act.wait_ge(S["xt"], n + 1)
                    if n >= 2:
                        act.wait_ge(S["obs"], n - 1)
                    act.copy(xn[:, n % 2, :], bank[7][:, :]).then_inc(S["xns"], 1)

        @block.vector
        def _(v):
            ch = [0]

            def link(ins):
                ch[0] += 1
                ins.then_inc(S["chain"], 1)
                v.wait_ge(S["chain"], ch[0])

            for k in range(8):
                m = v.memset(bank[k][:, :], 0.0)
            m.then_inc(S["consts"], 1)
            v.memset(xT[:, :, T:T + 2 * CH, :], 0.0)
            v.memset(r_il[:, :], 0.0).then_inc(S["at_e"], 8)
            v.memset(gi_next[:, :, :], 0.0).then_inc(S["sih_c"], 1)
            link(v.memset(gi_cur[:, :, :], 0.0))
            v.wait_ge(S["ld_small"], 64)
            v.wait_ge(S["ld_c"], 48)
            v.tensor_tensor(bsum[:, 0:8], bih[:, 0:8], bhh[:, 0:8], ALU.add)
            v.tensor_copy(bsum[:, 8:12], bih[:, 8:12])
            link(v.memset(zero4[:, :], 0.0))
            for m in range(12):
                g, k = divmod(m, KT)
                o = brow[:, 16 * g + 4 * k:16 * g + 4 * k + 4] if g < 2 else brow[:, 33 + 8 * k:40 + 8 * k:2]
                v.tensor_scalar(o, zero4[:, 0:4], bsum[:, m:m + 1], None, ALU.add)
            for k in range(KT):
                m = v.tensor_scalar(brow[:, 32 + 8 * k:39 + 8 * k:2], zero4[:, 0:4], bhh[:, 8 + k:9 + k], None, ALU.add)
            link(m)
            link(v.tensor_tensor(gi_cur[:, :, :], gi_cur[:, :, :], brow[:, :].unsqueeze(1).broadcast_to([P, CH, 64]), ALU.add))
            for n in range(0, 26, 2):
                if n == 24:
                    break
                v.wait_ge(S["tr"], n + 1)
                if n < 8:
                    v.tensor_copy(wgT[:, n // KT, n % KT, :], bank[n % 4][:, :]).then_inc(S["tr_e0"], 1)
                else:
                    c = n - 8
                    v.tensor_copy(xT[:, :, XT * c:XT * c + XT, :].rearrange("p k t b -> p k b t"),
                                  bank[n % 4][:, :].rearrange("p (k b t) -> p k b t", k=KT, b=B)).then_inc(S["tr_e0"], 1)
            v.wait_ge(S["tr"], 25)
            link(v.tensor_copy(condT[:, :], bank[0][:, 0:SB]))
            v.wait_ge(S["ld_whh"], 16)
            v.tensor_reduce(mx[:, 0:1], whh, AX.XY, ALU.max, apply_absolute_value=True).then_inc(S["wmax"], 1)
            v.tensor_reduce(mx[:, 1:2], condT[:, :], AX.X, ALU.max, apply_absolute_value=True).then_inc(S["wmax"], 1)
            v.wait_ge(S["amax"], 1)
            link(v.tensor_scalar(mx[:, 4:5], mx[:, 2:3], 1e-30, None, ALU.max))
            link(v.tensor_scalar(mx[:, 5:6], mx[:, 3:4], 1.0, None, ALU.max))
            link(v.tensor_scalar(mx[:, 6:8].bitcast(U32), mx[:, 4:6].bitcast(U32), 0x7F800000, None, ALU.bitwise_and))
            link(v.tensor_scalar(scl[:, 2:4], mx[:, 6:8], 2.0 ** -13, None, ALU.mult))
            link(v.reciprocal(scl[:, 4:6], scl[:, 2:4]))
            v.tensor_copy(scl[:, 0:1], scl[:, 5:6])
            link(v.tensor_copy(scl[:, 1:2], scl[:, 4:5]))
            link(v.tensor_tensor(scl[:, 6:7], scl[:, 2:3], scl[:, 3:4], ALU.mult))
            link(v.tensor_copy(scl[:, 2:3], scl[:, 3:4]))
            v.tensor_copy(scl[:, 3:4], scl[:, 6:7]).then_inc(S["scale"], 2)
            v.wait_ge(S["scale"], 2)
            link(v.tensor_scalar(sel[:, :], selm[:, :], scl[:, 3:4], None, ALU.mult))
            v.tensor_scalar(hist[:, CH - 1, :], condT[:, :], scl[:, 0:1], None, ALU.mult)
            v.tensor_scalar(H[:, :, 0:4], condT[:, :].rearrange("p (k b) -> p k b", b=B), scl[:, 0:1], None, ALU.mult).then_inc(S["hinit"], 1)
            v.memset(H[:, :, 8:16], 0.0).then_inc(S["hinit"], 1)
            v.wait_ge(S["hinit"], 2)
            v.tensor_tensor(H[:, :, 4:8], hist[:, CH - 1, :].rearrange("p (k b) -> p k b", b=B), H[:, :, 0:4], ALU.subtract).then_inc(S["hinit"], 1)
            for k in range(KT):
                v.wait_ge(S["w16"], 2 * k + 1 if k == 0 else k + 1)
                v.scalar_tensor_tensor(wh16[:, 1, k, :], whh[:, k, :], scl[:, 1:2], wh16[:, 0, k, :], ALU.mult, ALU.subtract).then_inc(S["chain"], 1)
                ch[0] += 1
            v.wait_ge(S["chain"], ch[0])
            v.wait_ge(S["w16"], KT)
            v.memset(omz[:, :], 0.0).then_inc(S["w16"], KT)

            v.wait_ge(S["ld_v"], 80)
            link(v.tensor_scalar(lam[:, 20:24], lam[:, 0:4], -1.0, None, ALU.mult))
            v.tensor_tensor(lam[:, 4:8], lam[:, 0:4], lam[:, 20:24], ALU.min).then_inc(S["c8"], 1)
            v.memset(gb[:, 12:13], 1.0 + 1e-6)
            v.memset(gb[:, 13:14], 1e-6)
            v.memset(fq[:, 29:30], 0.0)
            v.memset(ones[:, :], 1.0 / D)
            v.memset(ones1[:, :], 1.0)
            v.tensor_copy(id16[:, :], ident[:, :])
            v.tensor_tensor(kq[:, :], kq[:, :], kqr[:, :], ALU.mult)
            v.tensor_reduce(fq[:, 8:9], gb[:, 0:4], AX.X, ALU.max, apply_absolute_value=True)
            v.tensor_reduce(fq[:, 9:10], gb[:, 4:8], AX.X, ALU.max, apply_absolute_value=True).then_inc(S["xq"], 1)
            v.wait_ge(S["xq"], 2)
            link(v.tensor_scalar(fq[:, 12:13], fq[:, 10:11], float(D) ** 0.5 * 1.01, None, ALU.mult))
            link(v.tensor_tensor(fq[:, 12:13], fq[:, 12:13], fq[:, 11:12], ALU.add))
            link(v.tensor_scalar(fq[:, 12:13], fq[:, 12:13], 1e-30, None, ALU.max))
            link(v.tensor_scalar(fq[:, 13:14].bitcast(U32), fq[:, 12:13].bitcast(U32), 0x7F800000, None, ALU.bitwise_and))
            link(v.tensor_scalar(fq[:, 13:14], fq[:, 13:14], 2.0 ** -14, None, ALU.mult))
            link(v.reciprocal(fq[:, 14:15], fq[:, 13:14]))
            v.tensor_scalar(gb[:, 8:12], gb[:, 0:4], fq[:, 14:15], None, ALU.mult)
            v.tensor_scalar(gb2[:, :], gb[:, 4:8], fq[:, 14:15], None, ALU.mult)
            v.wait_ge(S["c8"], 3)
            link(v.tensor_scalar(lam[:, 20:24], lam[:, 0:4], 0.0, None, ALU.max))
            link(v.tensor_tensor(lam[:, 16:20], lam[:, 20:24], lam[:, 12:16], ALU.add))
            link(v.tensor_scalar(lam[:, 16:20], lam[:, 16:20], -8.0, None, ALU.mult))

            def gi_evac(dst, m, bk):
                g, k = divmod(m, KT)
                if g < 2:
                    o = dst[:, :, 16 * g + 4 * k:16 * g + 4 * k + 4]
                else:
                    o = dst[:, :, 33 + 8 * k:40 + 8 * k:2]
                i = bk[:, 0:TOK].rearrange("p (t b) -> p t b", b=B)
                if dst is gi_cur:
                    return v.tensor_scalar(o, i, bsum[:, m:m + 1], None, ALU.add)
                return v.tensor_copy(o, i)

            for m in range(12):
                v.wait_ge(S["fil"], m + 1)
                gi_evac(gi_cur, m, F[m % 2]).then_inc(S["ginit"], 1)

            def kb(a):
                return a.rearrange("p (k b) -> p k b", b=B)

            def step(i, s, attn):
                t = i * CH + s
                v.wait_ge(S["gn"], t + 1)
                v.tensor_copy(C[:, 1, :], Gn[:, 0:P]).then_inc(S["cn"], 1)
                v.wait_ge(S["gz"], t + 1)
                v.tensor_copy(C[:, 2, :], Gz[:, 0:P]).then_inc(S["cz"], 1)
                v.wait_ge(S["sr"], t + 1)
                v.wait_ge(S["pn"], t + 1)
                v.tensor_tensor_scan(y[:, :], r_il[:, :], Pn[:, 0:2 * SB], 0.0, ALU.mult, ALU.add).then_inc(S["scan"], 1)
                v.wait_ge(S["th"], 2 * t + 2)
                v.scalar_tensor_tensor(v_t[:, :], n_t[:, :], scl[:, 0:1], omz[:, :], ALU.mult, ALU.mult).then_inc(S["chain"], 1)
                v.scalar_tensor_tensor(H[:, :, 8:12], kb(n_t[:, :]), scl[:, 0:1], kb(omz[:, :]), ALU.mult, ALU.mult).then_inc(S["chain"], 1)
                v.wait_ge(S["sz"], t + 1)
                v.tensor_tensor(zh[:, :], z_t[:, :], hist[:, (s - 1) % CH, :], ALU.mult).then_inc(S["chain"], 1)
                v.tensor_tensor(H[:, :, 0:4], kb(z_t[:, :]), kb(hist[:, (s - 1) % CH, :]), ALU.mult).then_inc(S["chain"], 1)
                v.wait_ge(S["chain"], ch0 + 4 * t + 2)
                v.tensor_tensor(H[:, :, 12:16], kb(v_t[:, :]), H[:, :, 8:12], ALU.subtract)
                v.wait_ge(S["chain"], ch0 + 4 * t + 4)
                v.tensor_tensor(H[:, :, 4:8], kb(zh[:, :]), H[:, :, 0:4], ALU.subtract).then_inc(S["hp"], 1)
                if s == 0 and attn:
                    v.wait_ge(S["hp_c"], i)
                v.tensor_tensor(hist[:, s, :], zh[:, :], v_t[:, :], ALU.add).then_inc(S["hs"], 1)
                for kind, m in jobs(s, attn):
                    if kind != "gi":
                        continue
                    jl = [x for ss in range(CH) for x in jobs(ss, attn)]
                    q = jl.index((kind, m))
                    v.wait_ge(S["fil"], (24 + 20 * (i - 1) if attn else 12) + q + 1)
                    if attn and m == 0:
                        v.wait_ge(S["gc_b"], i)
                    gi_evac(gi_next, m, F[q % 2]).then_inc(S["gi_e"], 1)

            ch0 = ch[0]
            for s in range(CH):
                step(0, s, False)
            with v.Fori(1, NCH) as i:
                for s in range(CH):
                    step(i, s, True)


            ch[0] = ch0 + 4 * T
            al = B_reg[:, :].rearrange("p (k n) -> p k n", k=KT)
            sf = A_reg[:, :].rearrange("p (k n) -> p k n", k=KT)
            v.wait_ge(S["sih_c"], NCH + 1)

            nb = [0]

            def evac_q():
                n, g = divmod(nb[0], 6)
                if nb[0] % 2 == 0:
                    v.wait_ge(S["tq"], nb[0] + 1)
                    w = 1024 if g < 5 else 512
                    dst = Q_reg[:, n * KT * HP // 2 + 512 * g:n * KT * HP // 2 + 512 * g + w // 2].bitcast(F16)
                    v.tensor_copy(dst, bank[nb[0] % 4][:, 0:w // 2].bitcast(F16)).then_inc(S["tq_e0"], 1)
                nb[0] += 1

            def quant(n):
                v.wait_ge(S["aq"], n + 1)
                link(v.tensor_scalar(fq[:, 20 + n:21 + n], fq[:, 4 + n:5 + n], 0.5 / (HID * D), None, ALU.mult))
                link(v.tensor_scalar(fq[:, 24 + n:25 + n], fq[:, 20 + n:21 + n], -1.0, None, ALU.mult))
                if n:
                    v.wait_ge(S["tq"], 6 * n)
                link(v.tensor_scalar(qn, nat, fq[:, 20 + n:21 + n], None, ALU.is_gt))
                v.scalar_tensor_tensor(qn, nat, fq[:, 24 + n:25 + n], qn, ALU.is_lt, ALU.subtract).then_inc(S["qn_r"], 1)

            for k in range(KT):
                v.wait_ge(S["e_q"], k + 1)
                v.tensor_tensor(sf[:, k], tmp[:, k], sf[:, k], ALU.mult).then_inc(S["xb"], 1)
                v.wait_ge(S["xb"], k + 1)
                for b in range(B):
                    v.tensor_tensor_scan(sih[:, k, :, b], sgate[:, k, :, b], sih[:, k, :, b], 0.0, ALU.mult, ALU.add).then_inc(S["sc"], 1)
                if k >= 1:
                    v.wait_ge(S["x2"], k)
                    v.tensor_reduce(brT[:, k - 1, :], X2[:, k - 1].rearrange("p b (n t) -> p (b n) t", t=64), AX.X, ALU.add).then_inc(S["br"], 1)
            v.wait_ge(S["x2"], KT)
            v.tensor_reduce(brT[:, KT - 1, :], X2[:, KT - 1].rearrange("p b (n t) -> p (b n) t", t=64), AX.X, ALU.add).then_inc(S["br"], 1)
            v.wait_ge(S["wkT_e"], 8)
            for n in range(3):
                quant(n)
                for _ in range(6):
                    evac_q()
            link(v.tensor_scalar(fq[:, 27:28], fq[:, 26:27], 2.0, None, ALU.mult))
            link(v.reciprocal(fq[:, 28:29], fq[:, 14:15]))
            link(v.tensor_scalar(fq[:, 16:18], fq[:, 24:26], fq[:, 28:29], 2.0, ALU.mult, ALU.mult))
            v.wait_ge(S["keys"], 1)
            v.wait_ge(S["ssq"], 1)
            v.tensor_tensor_reduce(out=kqr[:, :], in0=bank[4][0:32, :], in1=kq[:, :], scale=1.0, scalar=0.0,
                                   op0=ALU.mult, op1=ALU.add, accum_out=sm[:, 2:3]).then_inc(S["dot"], 1)
            v.wait_ge(S["rms"], 1)
            link(v.reciprocal(sm[:, 3:4], sm[:, 1:2]))
            v.wait_ge(S["dot"], 1)
            v.tensor_tensor(sm[:, 4:5], sm[:, 2:3], sm[:, 3:4], ALU.mult).then_inc(S["scr"], 1)
            v.wait_ge(S["scT"], 1)
            scT = bank[5][0:1, 0:32].rearrange("p (b n) -> p b n", n=8)

            def row(o):
                return at1[0:1, o:o + 32].rearrange("p (b n) -> p b n", n=8)

            def per_b(o):
                return sm[0:1, o:o + 4].unsqueeze(2).broadcast_to([1, 4, 8])

            link(v.tensor_reduce(sm[0:1, 8:12], scT, AX.X, ALU.max))
            v.tensor_tensor(row(0), scT, per_b(8), ALU.subtract).then_inc(S["mxs"], 1)
            v.wait_ge(S["ex"], 1)
            link(v.tensor_reduce(sm[0:1, 12:16], row(32), AX.X, ALU.add))
            link(v.reciprocal(sm[0:1, 8:12], sm[0:1, 12:16]))
            v.tensor_tensor(row(96), row(32), per_b(8), ALU.mult).then_inc(S["att"], 1)
            v.wait_ge(S["atb"], 1)
            link(v.tensor_tensor(br2[:, :, :], brT[:, :, :], bank[6][:, 0:32].unsqueeze(1).broadcast_to([P, KT, 32]), ALU.mult))
            v.tensor_reduce(attT[:, :], br2[:, :, :].rearrange("p k (b n) -> p (k b) n", n=8), AX.X, ALU.add).then_inc(S["attT"], 1)
            v.wait_ge(S["pj"], 1)
            v.tensor_copy(projT[:, :], bank[7][:, 0:SB]).then_inc(S["pjs"], 1)
            v.wait_ge(S["pjs"], 1)

            Lb = bank[6]
            Ob = bank[4:6]

            def ln_a(b):
                if b:
                    v.wait_ge(S["yB"], 4 * b)
                    v.wait_ge(S["yf"], 4 * b)
                for k in range(KT):
                    x3 = v.tensor_scalar(xc[:, k, :], X2[:, k, b, :], projT[:, k * B + b:k * B + b + 1], None, ALU.add)
                    link(x3)
                v.memset(fq[:, 31:32], 0.0).then_inc(S["x3"], 1)
                v.wait_ge(S["mean"], b + 1)
                v.tensor_tensor(xc[:, :, :], xc[:, :, :], Lb[:, :].unsqueeze(1).broadcast_to([P, KT, T]), ALU.subtract).then_inc(S["xcs"], 1)

            def ln_b(b):
                v.wait_ge(S["stds"], b + 1)
                v.reciprocal(std[:, 1, :], std[:, 0, :]).then_inc(S["rst"], 1)
                v.wait_ge(S["rst"], b + 1)
                v.wait_ge(S["sqs"], b + 1)
                v.tensor_tensor(xc[:, :, :], xc[:, :, :], std[:, 1, :].unsqueeze(1).broadcast_to([P, KT, T]), ALU.mult).then_inc(S["yn"], 1)
                v.wait_ge(S["yh"], b + 1)
                v.wait_ge(S["yf"], 4 * b + 4)
                v.tensor_tensor(yhl[:, b % 2, 1, :], sq[:, :, :].rearrange("p k t -> p (k t)"), yhl[:, b % 2, 0, :], ALU.subtract).then_inc(S["yl"], 1)

            ln_a(0)
            ln_b(0)
            for b in range(B):
                for h in range(HT):
                    n = HT * b + h
                    hb = bank[0:2] if n % 2 == 0 else bank[2:4]
                    v.wait_ge(S["slu"], n + 1)
                    if n >= 2:
                        v.wait_ge(S["ghi"], n - 1)
                    v.scalar_tensor_tensor(gf[:, n % 2, :], hb[1][:, :], fq[:, 17:18], sl[:, n % 2, :], ALU.mult, ALU.mult).then_inc(S["gfd"], 1)
                    v.wait_ge(S["ghi"], n + 1)
                    if n >= 2:
                        v.wait_ge(S["glo"], n - 1)
                        v.wait_ge(S["gmid"], n - 1)
                    v.tensor_tensor(g1[:, n % 2, :], gf[:, n % 2, :], gp[:, 0, h, :], ALU.subtract).then_inc(S["gm1"], 1)
                    v.wait_ge(S["gmid"], n + 1)
                    v.tensor_tensor(gp[:, 2, h, :], g1[:, n % 2, :], gp[:, 1, h, :], ALU.subtract).then_inc(S["glo"], 1)
                    if b < B - 1 and h == 2:
                        ln_a(b + 1)
                    if b < B - 1 and h == 8:
                        ln_b(b + 1)
                for tt in range(4):
                    n = 4 * b + tt
                    v.wait_ge(S["o2"], n + 1)
                    v.wait_ge(S["xns"], n + 1)
                    if n >= 2:
                        v.wait_ge(S["out%d" % (n % 2)], 16 * (n // 2))
                    v.scalar_tensor_tensor(ob[:, n % 2, :], Ob[n % 2][:, :], fq[:, 27:28], xn[:, n % 2, :], ALU.mult, ALU.add).then_inc(S["obs"], 1)


def kernel(**a):
    import numpy as np
    import concourse.bacc as _bacc
    from concourse.bass_utils import run_bass_kernel_spmd as _run
    nc = _bacc.Bacc("TRN2", target_bir_lowering=False, num_devices=1)
    ident = np.eye(P, dtype=np.float32)
    sel = np.zeros((P, 48), np.float32)
    for p in range(P):
        if p % 32 < 16:
            c = 4 * (p // 32) + p % 4
            sel[p, c] = 1.0
            sel[p, 16 + 2 * c] = 1.0
    names = ["x", "cond_2048", "L0_cond_W_ih", "L0_cond_W_hh", "L0_cond_b_ih", "L0_cond_b_hh", "L0_attn_W_in", "L0_attn_b_in", "L0_attn_W_gate", "L0_attn_b_gate", "L0_attn_forget_lambda", "L0_cond2_rms_weight", "L0_cond2_Wk", "L0_cond2_Wo", "L0_cond2_ln_gamma", "L0_cond2_ln_beta", "L0_ffn_w1", "L0_ffn_w3", "L0_ffn_w2"]
    arrs = {n: np.ascontiguousarray(a[n]) for n in names}
    arrs["ident"] = ident
    arrs["sel"] = sel
    aps = [nc.dram_tensor("in_" + n, v.shape, F32, kind="ExternalInput").ap() for n, v in arrs.items()]
    o = nc.dram_tensor("o", (B, T, D), F32, kind="ExternalOutput").ap()
    gru(nc, *aps, o)
    r = _run(nc, [{"in_" + k: v for k, v in arrs.items()}], core_ids=[0])
    return r.results[0]["o"]
```

```python
from contextlib import ExitStack

import concourse.bass as bass
from concourse import mybir
import numpy as np

ALU = mybir.AluOpType
ACT = mybir.ActivationFunctionType
AX = mybir.AxisListType
F32 = mybir.dt.float32
F16 = mybir.dt.float16
BF16 = mybir.dt.bfloat16
U32 = mybir.dt.uint32
RMAX = bass.bass_isa.ReduceOp.max
RADD = bass.bass_isa.ReduceOp.add

P = 128
B, T, D = 4, 512, 512
KT = D // P
G3 = 3 * D
HID = 1365
CH = 16
NCH = T // CH
TOK = CH * B
SB = KT * B
XT = 32
NXT = T // XT


def gru(nc, x, cond, W_ih, W_hh, b_ih, b_hh, W_in, b_in, W_gate, b_gate, lam_d, rmsw, Wk, Wo, gam, bet, w1, w3, w2, ident_d, out):
    with ExitStack() as ctx:
        def sb(name, shape, dt=F32):
            return ctx.enter_context(nc.sbuf_tensor(name, shape, dt))

        def sem(name):
            return ctx.enter_context(nc.semaphore(name))

        HT = (HID + P - 1) // P
        HP = HT * P
        A_reg = sb("A_reg", [P, KT * T * B])
        B_reg = sb("B_reg", [P, KT * T * B])
        X_reg = sb("X_reg", [P, KT * (T + 2 * CH) * B])
        W_reg = sb("W_reg", [P, 16640])
        Q_reg = sb("Q_reg", [P, 3 * KT * HP // 2])

        def view(reg, at, shape, dt=F32):
            n = int(np.prod(shape))
            words = n if dt == F32 else n // 2
            a = reg[:, at:at + words]
            if dt != F32:
                a = a.bitcast(dt)
            names = "abcd"[:len(shape)]
            return a.rearrange("p (%s) -> p %s" % (" ".join(names), " ".join(names)), **dict(zip(names, shape)))

        xT = view(X_reg, 0, [KT, T + 2 * CH, B])
        wih16 = view(W_reg, 0, [2, KT, G3], F16)
        wh16 = view(W_reg, KT * G3, [2, KT, G3], F16)
        wg16 = view(W_reg, 2 * KT * G3, [2, 2, KT, D], F16)
        sih = view(A_reg, 0, [KT, T, B])
        sgate = view(B_reg, 0, [KT, T, B])
        whh = view(A_reg, 0, [KT, G3])
        wih = view(Q_reg, 2304, [KT, G3])
        xnat = view(B_reg, 0, [NXT, D])
        wnat = view(W_reg, KT * G3, [2, KT, D])
        tmp = view(W_reg, 0, [KT, T * B])
        WT = view(W_reg, 0, [2, KT, D])
        nat = view(W_reg, 8192, [KT * HP])
        qn = view(W_reg, 8192 + KT * HP, [KT * HP], F16)
        wkn = view(Q_reg, 4352, [2, KT, D])
        q1T = view(Q_reg, 0, [KT, HP], F16)
        q3T = view(Q_reg, KT * HP // 2, [KT, HP], F16)
        q2T = view(Q_reg, KT * HP, [HT, D], F16)
        X2 = view(B_reg, 0, [KT, B, T])
        xc = view(A_reg, 0, [KT, T])
        sq = view(A_reg, 2048, [KT, T])
        yhl = view(A_reg, 4096, [2, 2, KT * T], F16)
        gp = view(X_reg, 0, [3, HT, T], BF16)
        sl = view(W_reg, 4096, [2, T])
        gf = view(W_reg, 5120, [2, T])
        g1 = view(W_reg, 6144, [2, T])
        xn = view(W_reg, 0, [2, D])
        ob = view(W_reg, 1024, [2, D])
        std = view(W_reg, 2048, [2, T])
        brT = sb("brT", [P, KT, 32])
        br2 = sb("br2", [P, KT, 32])
        attT = sb("attT", [P, KT * B])
        projT = sb("projT", [P, KT * B])
        ones = sb("ones", [P, P])
        ones1 = sb("ones1", [P, P])
        kq = sb("kq", [32, D])
        kqr = sb("kqr", [32, D])
        sm = sb("sm", [32, 16])
        at1 = sb("at1", [1, 128])
        gb = sb("gb", [P, 4 * KT])
        gb2 = sb("gb2", [P, KT])
        id16 = sb("id16", [P, P], F16)
        lam = sb("lam", [P, 6 * KT])
        fq = sb("fq", [P, 32])
        xs16 = view(Q_reg, 0, [KT, 2, TOK], F16)
        gi_next = view(Q_reg, 256, [CH, KT, 12])
        GI = view(Q_reg, 1024, [CH, KT, 60], BF16)
        hist = view(Q_reg, 2944, [CH, SB])
        hprev = view(Q_reg, 3200, [CH, SB])
        hp16 = view(Q_reg, 3456, [KT, 2, TOK], F16)
        sin_c = view(Q_reg, 3712, [KT, TOK])
        xsf = view(Q_reg, 3968, [KT, TOK])
        H = sb("H", [P, KT, B, 4], F16)
        r7 = sb("r7", [P, 7 * SB])
        y7 = sb("y7", [P, 7 * SB])
        rsum = sb("rsum", [P, SB])
        zsum = sb("zsum", [P, SB])
        n_t = sb("n_t", [P, SB])
        z_t = sb("z_t", [P, SB])
        omz = sb("omz", [P, SB])
        zh = sb("zh", [P, SB])
        v_t = sb("v_t", [P, SB])
        identS = sb("identS", [P, P], BF16)
        bn16 = sb("bn16", [P, 3, KT], BF16)
        bnr = sb("bnr", [P, 2, KT])
        ident = sb("ident", [P, P])
        bih = sb("bih", [P, 12])
        bhh = sb("bhh", [P, 12])
        bsum = sb("bsum", [P, 12])
        zero4 = sb("zero4", [P, 8])
        bat = sb("bat", [P, 2, KT])
        condn = Q_reg[0:B, 0:D]
        condT = sb("condT", [P, SB])
        mx = sb("mx", [P, 16])
        scl = sb("scl", [P, 16])

        bank = [ctx.enter_context(nc.psum_tensor(f"bank{k}", [P, 512], F32)) for k in range(8)]
        GB = ((bank[0], bank[3]), (bank[1], bank[4]), (bank[2], bank[5]))
        F = bank[6:8]

        S = {}
        for n in ("ld_x ld_wih ld_whh ld_w ld_c ld_small tr tr_e0 tr_e1 wmax amax scale w16 hinit consts "
                  "r_ps z_ps n_ps r_sum z_sum r_sig z_sig o_sig scan th zh_ok v_ok h_ok hs wmx ghw wih_c wgh wgl w16h w16l xmax condt fil gi_e at_e xs_c gsp hp_c sih_c out0 out1 chain ginit ld_v ld_wk ld_nat nat0 xq absq aq hsq qa qn_r tq tq_e0 tq_e1 wkT wkT_e c8 e_x e_s e_q xb sc x2 br keys ssq dot rms scr scT mxs ex den att atb prod attT pj pjs x3 mean xcs sqs var stds rst yn yf yh yl st1 slu gfd ghi gm1 gmid glo o2 xt xns obs yB").split():
            S[n] = sem("s_" + n)

        block = ctx.enter_context(nc.Block())

        GW = (16, 16, 28)
        GO = (0, 16, 32)

        MPS = 16

        def tiles(attn):
            return [("gi", m) for m in range(12)] + ([("at", m) for m in range(8)] if attn else [])

        def done_in(s, attn):
            return [(q, k, m) for q, (k, m) in enumerate(tiles(attn)) if 1 + (12 * q + 11) // MPS == s]

        @block.sync
        def _(sp):
            sp.dma_start(ident[:, :], ident_d).then_inc(S["ld_c"], 16)
            sp.dma_start(condn[:, :], cond).then_inc(S["ld_c"], 16)
            with nc.allow_non_contiguous_dma(reason="small vectors"):
                sp.dma_start(bih[:, :], b_ih.rearrange("(m p) -> p m", p=P)).then_inc(S["ld_small"], 16)
                sp.dma_start(bhh[:, :], b_hh.rearrange("(m p) -> p m", p=P)).then_inc(S["ld_small"], 16)
                sp.dma_start(bat[:, 0, :], b_in.rearrange("(m p) -> p m", p=P)).then_inc(S["ld_small"], 16)
                sp.dma_start(bat[:, 1, :], b_gate.rearrange("(m p) -> p m", p=P)).then_inc(S["ld_small"], 16)
            sp.dma_start(whh, W_hh.rearrange("(k p) n -> p k n", p=P)).then_inc(S["ld_whh"], 16)
            sp.dma_start(wnat[:, 0], W_in.rearrange("(m p) d -> p m d", p=P)).then_inc(S["ld_w"], 16)
            sp.dma_start(wnat[:, 1], W_gate.rearrange("(m p) d -> p m d", p=P)).then_inc(S["ld_w"], 16)
            sp.dma_start(wih[:, :, :], W_ih.rearrange("(k p) n -> p k n", p=P)).then_inc(S["ld_wih"], 16)
            for c in range(NXT):
                for b in range(B):
                    sp.dma_start(xnat[XT * b:XT * b + XT, c, :], x[b, XT * c:XT * c + XT, :]).then_inc(S["ld_x"], 16)
            with nc.allow_non_contiguous_dma(reason="small vectors"):
                sp.dma_start(lam[:, 0:KT], lam_d.rearrange("(m p) -> p m", p=P)).then_inc(S["ld_v"], 16)
                sp.dma_start(gb[:, 0:KT], gam.rearrange("(m p) -> p m", p=P)).then_inc(S["ld_v"], 16)
                sp.dma_start(gb[:, KT:2 * KT], bet.rearrange("(m p) -> p m", p=P)).then_inc(S["ld_v"], 16)
            sp.dma_start(kqr[:, :], rmsw.unsqueeze(0).broadcast_to([32, D])).then_inc(S["ld_v"], 16)
            sp.dma_start(kq[:, :], cond[1:2, :].broadcast_to([32, D])).then_inc(S["ld_v"], 16)
            sp.wait_ge(S["hinit"], 3)
            sp.dma_start(wkn[:, 0], Wk.rearrange("(m p) d -> p m d", p=P)).then_inc(S["ld_wk"], 16)
            sp.dma_start(wkn[:, 1], Wo.rearrange("(m p) d -> p m d", p=P)).then_inc(S["ld_wk"], 16)
            nfull = HID // P
            rest = HID - nfull * P
            for n, w in enumerate((w1, w3, w2)):
                sp.wait_ge(S["nat0"], n + 1)
                if n < 2:
                    v = nat.rearrange("p (h d) -> p h d", d=D)
                    sp.dma_start(v[:, 0:nfull, :], w[0:nfull * P, :].rearrange("(h p) d -> p h d", p=P)).then_inc(S["ld_nat"], 16)
                    sp.dma_start(v[0:rest, nfull, :], w[nfull * P:HID, :]).then_inc(S["ld_nat"], 16)
                else:
                    v = nat.rearrange("p (k h) -> p k h", k=KT)
                    for k in range(2):
                        sp.dma_start(v[:, 2 * k:2 * k + 2, 0:HID], w.rearrange("(k p) h -> p k h", p=P)[:, 2 * k:2 * k + 2, :]).then_inc(S["ld_nat"], 16)
            for b in range(B):
                for tt in range(4):
                    n = 4 * b + tt
                    sp.wait_ge(S["obs"], n + 1)
                    sp.dma_start(out[b, tt * P:(tt + 1) * P, :], ob[:, n % 2, :]).then_inc(S["out%d" % (n % 2)], 16)
            sp.wait_ge(S["out0"], 8 * 16)
            sp.wait_ge(S["out1"], 8 * 16)

        @block.gpsimd
        def _(pool):
            pool.wait_ge(S["wmax"], 4)
            nc.gpsimd.partition_all_reduce(mx[:, 5:9], mx[:, 0:4], P, RMAX).then_inc(S["amax"], 1)
            pool.wait_ge(S["wmax"], 5)
            nc.gpsimd.partition_all_reduce(mx[:, 9:10], mx[:, 4:5], P, RMAX).then_inc(S["amax"], 1)

            pool.wait_ge(S["xq"], 1)
            nc.gpsimd.partition_all_reduce(fq[:, 10:12], fq[:, 8:10], P, RMAX).then_inc(S["xq"], 1)

            def zero(n, w):
                return zero4[:, 0:1].unsqueeze(2).broadcast_to([P, n, w])

            def load_xs(chunk, gi_done):
                if gi_done is not None:
                    pool.wait_ge(S["gi_e"], gi_done)
                nc.gpsimd.tensor_tensor(xsf.rearrange("p k (t b) -> p k t b", b=B), xT[:, :, bass.ds(chunk * CH, CH), :],
                                        scl[:, 4:5].unsqueeze(2).unsqueeze(3).broadcast_to([P, KT, CH, B]), ALU.mult).then_inc(S["xs_c"], 1)
                pool.wait_ge(S["xs_c"], 3 * chunk + 1)
                nc.gpsimd.tensor_tensor(xs16[:, :, 0, :], xsf, zero(KT, TOK), ALU.add).then_inc(S["xs_c"], 1)
                pool.wait_ge(S["xs_c"], 3 * chunk + 2)
                nc.gpsimd.tensor_tensor(xs16[:, :, 1, :], xsf, xs16[:, :, 0, :], ALU.subtract).then_inc(S["xs_c"], 1)

            def split(lo, hi, base):
                n = (hi - lo) * KT
                src = gi_next[:, lo:hi].rearrange("p s k c -> p (s k) c")
                dst = GI[:, lo:hi].rearrange("p s k c -> p (s k) c")
                rz, nn = src[:, :, 0:8], src[:, :, 8:12]

                def slots(c):
                    return dst[:, :, c:32:4], dst[:, :, 36 + c:60:7]

                for e, (a, w) in enumerate(((rz, 8), (nn, 4))):
                    nc.gpsimd.tensor_tensor(slots(0)[e], a, zero(n, w), ALU.add).then_inc(S["gsp"], 1)
                pool.wait_ge(S["gsp"], base + 2)
                for e, (a, w) in enumerate(((rz, 8), (nn, 4))):
                    nc.gpsimd.tensor_tensor(a, a, slots(0)[e], ALU.subtract).then_inc(S["gsp"], 1)
                pool.wait_ge(S["gsp"], base + 4)
                for e, (a, w) in enumerate(((rz, 8), (nn, 4))):
                    nc.gpsimd.tensor_tensor(slots(1)[e], a, zero(n, w), ALU.add).then_inc(S["gsp"], 1)
                pool.wait_ge(S["gsp"], base + 6)
                for e, (a, w) in enumerate(((rz, 8), (nn, 4))):
                    nc.gpsimd.tensor_tensor(slots(2)[e], a, slots(1)[e], ALU.subtract).then_inc(S["gsp"], 1)

            def split_h(i):
                pool.wait_ge(S["hs"], 2 * CH * i)
                pool.wait_ge(S["at_e"], 8 * i)
                pool.wait_ge(S["sih_c"], i)
                nc.gpsimd.tensor_tensor(hprev[:, :, :], hist[:, :, :], scl[:, 6:7].unsqueeze(2).broadcast_to([P, CH, SB]), ALU.mult).then_inc(S["hp_c"], 1)
                src = hist.rearrange("p t (k b) -> p t k b", b=B)

                def part(c):
                    return hp16[:, :, c, :].rearrange("p k (t b) -> p t k b", b=B)

                nc.gpsimd.tensor_tensor(part(0), src, zero4[:, 0:1].unsqueeze(2).unsqueeze(3).broadcast_to([P, CH, KT, B]), ALU.add).then_inc(S["hp_c"], 1)
                pool.wait_ge(S["hp_c"], 3 * i - 1)
                nc.gpsimd.tensor_tensor(part(1), src, part(0), ALU.subtract).then_inc(S["hp_c"], 1)

            def gate_h(i, at_done):
                pool.wait_ge(S["at_e"], at_done)
                pool.wait_ge(S["hp_c"], 3 * i)
                nc.gpsimd.tensor_tensor(
                    sih[:, :, bass.ds((i - 1) * CH, CH), :],
                    sin_c[:, :, :].rearrange("p k (t b) -> p k t b", b=B),
                    hprev[:, :, :].rearrange("p t (k b) -> p k t b", b=B), ALU.mult).then_inc(S["sih_c"], 1)

            pool.wait_ge(S["scale"], 2)
            load_xs(0, None)
            pool.wait_ge(S["gi_e"], 12)
            split(0, 12, 0)
            split(12, 16, 8)
            load_xs(1, 12)

            def chunk(i, attn):
                if attn:
                    split_h(i)
                pool.wait_ge(S["gi_e"], 12 * (i + 2))
                pool.wait_ge(S["n_ps"], 2 * (CH * i + 12))
                split(0, 12, 16 * (i + 1))
                load_xs(i + 2, 12 * (i + 2))
                if attn:
                    gate_h(i, 8 * i + 4)
                pool.wait_ge(S["n_ps"], 2 * (CH * i + 16))
                split(12, 16, 16 * (i + 1) + 8)

            chunk(0, False)
            with pool.Fori(1, NCH) as i:
                chunk(i, True)

            split_h(NCH)
            gate_h(NCH, 8 * NCH + 4)
            for n in range(3):
                if n == 0:
                    pool.wait_ge(S["fil"], 24 + 20 * (NCH - 1) + 8)
                else:
                    pool.wait_ge(S["qn_r"], n)
                nc.gpsimd.memset(nat, 0.0).then_inc(S["nat0"], 1)
                pool.wait_ge(S["absq"], n + 1)
                nc.gpsimd.partition_all_reduce(fq[:, 4 + n:5 + n], fq[:, n:n + 1], P, RADD).then_inc(S["aq"], 1)
                if n == 0:
                    for k in range(KT):
                        pool.wait_ge(S["sc"], 4 * k + 4)
                        nc.gpsimd.tensor_tensor(X2[:, k], xT[:, k, 0:T, :].rearrange("p t b -> p b t"),
                                                sih[:, k].rearrange("p t b -> p b t"), ALU.add).then_inc(S["x2"], 1)

        @block.tensor
        def _(pe):
            pe.wait_ge(S["ld_c"], 32)
            pe.wait_ge(S["consts"], 1)
            for k in range(KT):
                mm = pe.transpose(bank[7][:, k * B:(k + 1) * B], condn[:, k * P:(k + 1) * P], ident[0:B, 0:B])
            mm.then_inc(S["condt"], 1)
            pe.wait_ge(S["ld_w"], 32)
            for n in range(8):
                w, k = divmod(n, KT)
                if n >= 4:
                    pe.wait_ge(S["wgl"], n - 3)
                for m in range(KT):
                    mm = pe.transpose(bank[n % 4][:, m * P:(m + 1) * P], wnat[:, w, m, k * P:(k + 1) * P], ident[:, :])
                mm.then_inc(S["tr"], 1)
            pe.wait_ge(S["ld_x"], 64 * NXT)
            for c in range(NXT):
                if c < 2:
                    pe.wait_ge(S["wgl"], 4 + c + 1)
                elif c < 4:
                    pe.wait_ge(S["wgl"], 4 + c + 1)
                else:
                    pe.wait_ge(S["tr_e0"] if c % 2 == 0 else S["tr_e1"], (c - 4) // 2 + 1)
                for k in range(KT):
                    mm = pe.transpose(bank[c % 4][:, k * P:(k + 1) * P], xnat[:, c, k * P:(k + 1) * P], ident[:, :])
                mm.then_inc(S["tr"], 1)

            PRODUCTS = [(k, w, p) for k in range(KT) for w, p in ((0, 0), (0, 1), (1, 0))]

            def product(kind, m, j, bk):
                k, w, p = PRODUCTS[j]
                if kind == "gi":
                    lhs, rhs = wih16[:, w, k, m * P:(m + 1) * P], xs16[:, k, p, :]
                else:
                    gate, e = divmod(m, KT)
                    lhs, rhs = wg16[:, gate, w, k, e * P:(e + 1) * P], hp16[:, k, p, :]
                mm = pe.matmul(bk[:, 0:TOK], lhs, rhs, start=(j == 0), stop=(j == 11))
                if j == 11:
                    mm.then_inc(S["fil"], 1)

            pe.wait_ge(S["condt"], 2)
            pe.wait_ge(S["xs_c"], 3)
            pe.wait_ge(S["wih_c"], 2 * KT)
            for m in range(12):
                if m >= 2:
                    pe.wait_ge(S["gi_e"], m - 1)
                for j in range(12):
                    product("gi", m, j, F[m % 2])
            pe.wait_ge(S["hinit"], 3)
            pe.wait_ge(S["w16l"], KT)
            pe.wait_ge(S["tr_e0"], 8)
            pe.wait_ge(S["tr_e1"], 8)

            def inject(g, hf, s):
                w = GW[g]
                pe.matmul(GB[g][hf][:, 0:2 * w].rearrange("p (k c) -> p k c", k=2), identS[:, :],
                          GI[:, s, 2 * hf:2 * hf + 2, GO[g]:GO[g] + w], start=True, stop=False, skip_group_check=True)

            def products(g, hf, kh):
                w7 = GW[g] // B
                for m in range(2):
                    o = GB[g][hf][:, m * GW[g]:(m + 1) * GW[g]].rearrange("p (b c) -> p b c", c=w7)[:, :, 0:4]
                    for w in range(2):
                        for k in (2 * kh, 2 * kh + 1):
                            mm = pe.matmul(o, wh16[:, w, k, g * D + (2 * hf + m) * P:g * D + (2 * hf + m + 1) * P], H[:, k, :, :],
                                           start=False, stop=(kh == 1 and w == 1 and k == KT - 1), skip_group_check=True)
                return mm

            def step(i, s, attn):
                t = i * CH + s
                first = not attn and s == 0
                if s == 0:
                    pe.wait_ge(S["gsp"], 16 * i + 8)
                if s == 12:
                    pe.wait_ge(S["gsp"], 16 * i + 16)
                for hf in range(2):
                    for g, rd in ((0, "r_sum"), (1, "z_sum"), (2, "scan")):
                        if not first:
                            pe.wait_ge(S[rd], 2 * t - 1 + hf)
                        inject(g, hf, s)
                    if hf == 0 and not first:
                        pe.wait_ge(S["h_ok"], 2 * t - 1)
                    for g in range(3):
                        products(g, hf, 0)
                if not first:
                    pe.wait_ge(S["h_ok"], 2 * t)
                for hf in range(2):
                    for g, done in ((0, "r_ps"), (1, "z_ps"), (2, "n_ps")):
                        products(g, hf, 1).then_inc(S[done], 1)
                if s == 0:
                    return
                for f in range(MPS * (s - 1), MPS * s):
                    q, j = divmod(f, 12)
                    if q >= len(tiles(attn)):
                        break
                    kind, m = tiles(attn)[q]
                    if j == 0:
                        if q == 0:
                            pe.wait_ge(S["xs_c"], 3 * (i + 2))
                        if kind == "at" and m == 0:
                            pe.wait_ge(S["hp_c"], 3 * i)
                        if q < 2:
                            pe.wait_ge(S["gi_e"], 12 * (i + 1))
                            if attn:
                                pe.wait_ge(S["at_e"], 8 * i)
                        else:
                            pk, pm = tiles(attn)[q - 2]
                            if pk == "gi":
                                pe.wait_ge(S["gi_e"], 12 * (i + 1) + pm + 1)
                            else:
                                pe.wait_ge(S["at_e"], 8 * i + pm + 1)
                    product(kind, m, j, F[q % 2])

            for s in range(CH):
                step(0, s, False)
            with pe.Fori(1, NCH) as i:
                for s in range(CH):
                    step(i, s, True)

            pe.wait_ge(S["hp_c"], 3 * NCH)
            for m in range(8):
                if m < 2:
                    pe.wait_ge(S["gi_e"], 12 * (NCH + 1))
                    pe.wait_ge(S["at_e"], 8 * NCH)
                else:
                    pe.wait_ge(S["at_e"], 8 * NCH + m - 1)
                for j in range(12):
                    product("at", m, j, F[m % 2])
            pe.wait_ge(S["ld_wk"], 32)
            for n in range(8):
                w, k = divmod(n, KT)
                if n >= 4:
                    pe.wait_ge(S["wkT_e"], n - 3)
                for m in range(KT):
                    mm = pe.transpose(bank[n % 4][:, m * P:(m + 1) * P], wkn[:, w, m, k * P:(k + 1) * P], ident[:, :])
                mm.then_inc(S["wkT"], 1)
            pe.wait_ge(S["wkT_e"], 8)
            nb = 0
            for n in range(3):
                pe.wait_ge(S["qn_r"], n + 1)
                for blk in range(HT * KT):
                    if blk % 8 == 0:
                        if nb >= 4:
                            pe.wait_ge(S["tq_e0"] if nb % 2 == 0 else S["tq_e1"], (nb - 4) // 2 + 1)
                        bk = bank[nb % 4][:, :].bitcast(F16)
                    if n < 2:
                        k, h = divmod(blk, HT)
                        src = qn[:, h * D + k * P:h * D + (k + 1) * P]
                    else:
                        h, k = divmod(blk, KT)
                        src = qn[:, k * HP + h * P:k * HP + (h + 1) * P]
                    mm = pe.transpose(bk[:, (blk % 8) * P:(blk % 8 + 1) * P], src, id16[:, :])
                    if blk % 8 == 7 or blk == HT * KT - 1:
                        mm.then_inc(S["tq"], 1)
                        nb += 1
            pe.wait_ge(S["br"], KT)
            for k in range(KT):
                mm = pe.matmul(bank[4][0:32, :], brT[:, k, :], WT[:, 0, k, :], start=(k == 0), stop=(k == KT - 1))
            mm.then_inc(S["keys"], 1)
            pe.wait_ge(S["scr"], 1)
            pe.transpose(bank[5][0:1, 0:32], sm[:, 4:5], ident[0:32, 0:32]).then_inc(S["scT"], 1)
            pe.wait_ge(S["att"], 1)
            pe.matmul(bank[6][:, 0:32], ones1[0:1, :], at1[0:1, 96:128], start=True, stop=True).then_inc(S["atb"], 1)
            pe.wait_ge(S["attT"], 1)
            for m in range(KT):
                for k in range(KT):
                    mm = pe.matmul(bank[7][:, m * B:(m + 1) * B], WT[:, 1, k, m * P:(m + 1) * P], attT[:, k * B:(k + 1) * B],
                                   start=(k == 0), stop=(k == KT - 1))
            mm.then_inc(S["pj"], 1)
            hA, hB, Ob, Lb, Tb = bank[0:2], bank[2:4], bank[4:6], bank[6], bank[7]

            def ln_mean(b):
                pe.wait_ge(S["x3"], b + 1)
                if b:
                    pe.wait_ge(S["stds"], b)
                for k in range(KT):
                    mm = pe.matmul(Lb[:, :], ones[:, :], xc[:, k, :], start=(k == 0), stop=(k == KT - 1))
                mm.then_inc(S["mean"], 1)

            def ln_var(b):
                pe.wait_ge(S["xcs"], b + 1)
                pe.wait_ge(S["sqs"], b + 1)
                for k in range(KT):
                    mm = pe.matmul(Lb[:, :], ones[:, :], sq[:, k, :], start=(k == 0), stop=(k == KT - 1))
                mm.then_inc(S["var"], 1)

            pe.wait_ge(S["tq_e0"], 9)
            pe.wait_ge(S["tq_e1"], 9)
            pe.wait_ge(S["pjs"], 1)
            ln_mean(0)
            ln_var(0)
            for b in range(B):
                pe.wait_ge(S["yl"], b + 1)
                pe.wait_ge(S["yh"], b + 1)
                for h in range(HT):
                    n = HT * b + h
                    if n >= 2:
                        pe.wait_ge(S["gfd"], n - 1)
                    hb = hA if n % 2 == 0 else hB
                    for qT, bk in ((q1T, hb[0]), (q3T, hb[1])):
                        for k in range(KT):
                            for part in range(2):
                                mm = pe.matmul(bk[:, :], qT[:, k, h * P:(h + 1) * P], yhl[:, b % 2, part, k * T:(k + 1) * T],
                                               start=(k == 0 and part == 0), stop=(k == KT - 1 and part == 1))
                    mm.then_inc(S["st1"], 1)
                    if b < B - 1 and h == 3:
                        ln_mean(b + 1)
                    if b < B - 1 and h == 7:
                        ln_var(b + 1)
                for tt in range(4):
                    n = 4 * b + tt
                    if n >= 1:
                        pe.wait_ge(S["xns"], n)
                    for k in range(KT):
                        mm = pe.transpose(Tb[:, k * P:(k + 1) * P], X2[:, k, b, tt * P:(tt + 1) * P], ident[:, :])
                    mm.then_inc(S["xt"], 1)
                    if n >= 2:
                        pe.wait_ge(S["obs"], n - 1)
                    for h in range(HT):
                        if tt == 0:
                            pe.wait_ge(S["glo"], HT * b + h + 1)
                            pe.wait_ge(S["gmid"], HT * b + h + 1)
                        for part in range(3):
                            mm = pe.matmul(Ob[n % 2][:, :], gp[:, part, h, tt * P:(tt + 1) * P], q2T[:, h, :],
                                           start=(h == 0 and part == 0), stop=(h == HT - 1 and part == 2))
                    mm.then_inc(S["o2"], 1)

        @block.scalar
        def _(act):
            act.wait_ge(S["scale"], 1)
            for k in range(KT):
                act.activation(wih16[:, 0, k, :], wih[:, k, :], ACT.Copy, scale=scl[:, 2:3]).then_inc(S["wih_c"], 1)
            for n in range(8):
                w, k = divmod(n, KT)
                act.wait_ge(S["tr"], n + 1)
                act.activation(wg16[:, w, 0, k, :], bank[n % 4][:, :], ACT.Copy, scale=scl[:, 3:4]).then_inc(S["wgh"], 1)
            act.wait_ge(S["tr"], 8)
            for k in range(KT):
                act.activation(wh16[:, 0, k, :], whh[:, k, :], ACT.Copy, scale=scl[:, 0:1]).then_inc(S["w16h"], 1)
            for c in range(1, NXT, 2):
                act.wait_ge(S["tr"], 8 + c + 1)
                act.copy(xT[:, :, XT * c:XT * c + XT, :].rearrange("p k t b -> p k b t"),
                         bank[c % 4][:, :].rearrange("p (k b t) -> p k b t", k=KT, b=B)).then_inc(S["tr_e1"], 1)

            act.wait_ge(S["c8"], 1)
            act.activation(lam[:, 8:12], lam[:, 4:8], ACT.Exp).then_inc(S["c8"], 1)
            act.wait_ge(S["c8"], 2)
            act.activation(lam[:, 12:16], lam[:, 8:12], ACT.Ln, bias=1.0).then_inc(S["c8"], 1)

            def at_tile(i, m, bk):
                w, e = divmod(m, KT)
                if m == 0:
                    act.wait_ge(S["sih_c"], i)
                if w == 0:
                    act.activation(sin_c[:, e, :], bk[:, 0:TOK], ACT.Sigmoid, scale=scl[:, 8:9], bias=bat[:, w, e:e + 1]).then_inc(S["at_e"], 1)
                else:
                    act.activation(sgate[:, e, bass.ds((i - 1) * CH, CH), :], bk[:, 0:TOK].rearrange("p (t b) -> p t b", b=B),
                                   ACT.Sigmoid, scale=scl[:, 8:9], bias=bat[:, w, e:e + 1]).then_inc(S["at_e"], 1)

            def step(i, s, attn):
                t = i * CH + s
                for hf in range(2):
                    j = 2 * t + hf
                    u = slice(8 * hf, 8 * hf + 8)
                    act.wait_ge(S["r_sum"], j + 1)
                    act.activation(r7[:, 56 * hf + 4:56 * hf + 56:7], rsum[:, u], ACT.Sigmoid, scale=scl[:, 5:6]).then_inc(S["r_sig"], 1)
                    act.wait_ge(S["z_sum"], j + 1)
                    act.activation(z_t[:, u], zsum[:, u], ACT.Sigmoid, scale=scl[:, 5:6]).then_inc(S["z_sig"], 1)
                    act.activation(omz[:, u], zsum[:, u], ACT.Sigmoid, scale=scl[:, 7:8]).then_inc(S["o_sig"], 1)
                    act.wait_ge(S["scan"], j + 1)
                    act.activation(n_t[:, u], y7[:, 56 * hf + 6:56 * hf + 56:7], ACT.Tanh, scale=scl[:, 5:6]).then_inc(S["th"], 1)
                for q, kind, m in done_in(s, attn):
                    if kind == "at":
                        act.wait_ge(S["fil"], 24 + 20 * (i - 1) + q + 1)
                        at_tile(i, m, F[q % 2])

            for s in range(CH):
                step(0, s, False)
            with act.Fori(1, NCH) as i:
                for s in range(CH):
                    step(i, s, True)

            for m in range(8):
                act.wait_ge(S["fil"], 24 + 20 * (NCH - 1) + m + 1)
                at_tile(NCH, m, F[m % 2])
            act.wait_ge(S["at_e"], 8 * NCH + 8)
            act.wait_ge(S["fil"], 24 + 20 * (NCH - 1) + 8)
            al = B_reg[:, :].rearrange("p (k n) -> p k n", k=KT)
            for k in range(KT):
                act.activation(al[:, k], al[:, k], ACT.Exp, scale=lam[:, 16 + k:17 + k]).then_inc(S["e_x"], 1)
            for k in range(KT):
                act.wait_ge(S["e_x"], k + 1)
                act.activation(tmp[:, k], al[:, k], ACT.Square).then_inc(S["e_s"], 1)
            for k in range(KT):
                act.wait_ge(S["e_s"], k + 1)
                act.activation(tmp[:, k], tmp[:, k], ACT.Sqrt, scale=-1.0, bias=gb[:, 12:13]).then_inc(S["e_q"], 1)
            for n in range(8):
                w, k = divmod(n, KT)
                act.wait_ge(S["wkT"], n + 1)
                if n == 0:
                    act.wait_ge(S["xb"], 2)
                act.copy(WT[:, w, k, :], bank[n % 4][:, :]).then_inc(S["wkT_e"], 1)
            nb = 0
            for n in range(3):
                act.wait_ge(S["ld_nat"], 32 * (n + 1))
                if n:
                    act.wait_ge(S["qn_r"], n)
                act.wait_ge(S["tq_e1"], nb // 2) if nb else None
                act.activation(qn, nat, ACT.Abs, accum_out=fq[:, n:n + 1]).then_inc(S["absq"], 1)
                for _ in range(6):
                    if nb % 2:
                        act.wait_ge(S["tq"], nb + 1)
                        g = nb % 6
                        w = 1024 if g < 5 else 512
                        dst = Q_reg[:, n * KT * HP // 2 + 512 * g:n * KT * HP // 2 + 512 * g + w // 2].bitcast(F16)
                        act.copy(dst, bank[nb % 4][:, 0:w // 2].bitcast(F16)).then_inc(S["tq_e1"], 1)
                    nb += 1
            act.wait_ge(S["keys"], 1)
            act.activation(xc[0:32, 0, :], bank[4][0:32, :], ACT.Square, accum_out=sm[:, 0:1]).then_inc(S["ssq"], 1)
            act.wait_ge(S["ssq"], 1)
            act.activation(sm[:, 1:2], sm[:, 0:1], ACT.Sqrt, scale=1.0 / D, bias=gb[0:32, 13:14]).then_inc(S["rms"], 1)
            act.wait_ge(S["mxs"], 1)
            act.activation(at1[0:1, 32:64], at1[0:1, 0:32], ACT.Exp).then_inc(S["ex"], 1)

            def ln_sq(b):
                act.wait_ge(S["xcs"], b + 1)
                if b:
                    act.wait_ge(S["yl"], b)
                act.activation(sq[:, :, :], xc[:, :, :], ACT.Square).then_inc(S["sqs"], 1)

            def ln_act(b):
                act.wait_ge(S["var"], b + 1)
                act.activation(std[:, 0, :], Lb[:, :], ACT.Sqrt, bias=gb[:, 13:14]).then_inc(S["stds"], 1)
                act.wait_ge(S["yn"], b + 1)
                if b >= 2:
                    act.wait_ge(S["st1"], HT * (b - 1))
                for k in range(KT):
                    act.activation(sq[:, k, :], xc[:, k, :], ACT.Identity, scale=gb[:, 8 + k:9 + k], bias=gb2[:, k:k + 1]).then_inc(S["yf"], 1)
                for k in range(KT):
                    act.activation(yhl[:, b % 2, 0, k * T:(k + 1) * T], xc[:, k, :], ACT.Identity, scale=gb[:, 8 + k:9 + k], bias=gb2[:, k:k + 1]).then_inc(S["yB"], 1)
                act.wait_ge(S["yB"], 4 * (b + 1))
                act.activation(fq[:, 30:31], fq[:, 29:30], ACT.Copy).then_inc(S["yh"], 1)

            Lb = bank[6]
            ln_sq(0)
            ln_act(0)
            for b in range(B):
                for h in range(HT):
                    n = HT * b + h
                    hb = bank[0:2] if n % 2 == 0 else bank[2:4]
                    act.wait_ge(S["st1"], n + 1)
                    if n >= 2:
                        act.wait_ge(S["gfd"], n - 1)
                    act.activation(sl[:, n % 2, :], hb[0][:, :], ACT.Silu, scale=fq[:, 16:17]).then_inc(S["slu"], 1)
                    act.wait_ge(S["gfd"], n + 1)
                    if h == 0 and b:
                        act.wait_ge(S["o2"], 4 * b)
                    act.copy(gp[:, 0, h, :], gf[:, n % 2, :]).then_inc(S["ghi"], 1)
                    act.wait_ge(S["gm1"], n + 1)
                    act.copy(gp[:, 1, h, :], g1[:, n % 2, :]).then_inc(S["gmid"], 1)
                    if b < B - 1 and h == 5:
                        ln_sq(b + 1)
                    if b < B - 1 and h == 8:
                        ln_act(b + 1)
                for tt in range(4):
                    n = 4 * b + tt
                    act.wait_ge(S["xt"], n + 1)
                    if n >= 2:
                        act.wait_ge(S["obs"], n - 1)
                    act.copy(xn[:, n % 2, :], bank[7][:, :]).then_inc(S["xns"], 1)

        @block.vector
        def _(v):
            ch = [0]

            def link(ins):
                ch[0] += 1
                ins.then_inc(S["chain"], 1)
                v.wait_ge(S["chain"], ch[0])

            for k in range(8):
                m = v.memset(bank[k][:, :], 0.0)
            m.then_inc(S["consts"], 1)
            v.memset(xT[:, :, T:T + 2 * CH, :], 0.0)
            v.memset(n_t[:, :], 0.0).then_inc(S["at_e"], 8)
            v.memset(omz[:, :], 0.0).then_inc(S["sih_c"], 1)
            v.memset(zero4[:, :], 0.0)
            link(v.memset(r7[:, :], 1.0))
            link(v.memset(r7[:, 0:7 * SB:7], 0.0))
            v.wait_ge(S["ld_small"], 64)
            v.tensor_tensor(bsum[:, 0:8], bih[:, 0:8], bhh[:, 0:8], ALU.add)
            link(v.tensor_copy(bsum[:, 8:12], bih[:, 8:12]))
            link(v.tensor_copy(bn16[:, 0, :], bhh[:, 8:12]))
            link(v.tensor_tensor(bnr[:, 0, :], bhh[:, 8:12], bn16[:, 0, :], ALU.subtract))
            link(v.tensor_copy(bn16[:, 1, :], bnr[:, 0, :]))
            link(v.tensor_tensor(bn16[:, 2, :], bnr[:, 0, :], bn16[:, 1, :], ALU.subtract))
            v.wait_ge(S["condt"], 1)
            v.tensor_copy(condT[:, :], bank[7][:, 0:SB]).then_inc(S["condt"], 1)
            v.wait_ge(S["condt"], 2)
            v.tensor_reduce(mx[:, 1:2], condT[:, :], AX.X, ALU.max, apply_absolute_value=True).then_inc(S["wmax"], 1)
            v.wait_ge(S["ld_whh"], 16)
            v.tensor_reduce(mx[:, 0:1], whh, AX.XY, ALU.max, apply_absolute_value=True).then_inc(S["wmax"], 1)
            v.wait_ge(S["ld_w"], 32)
            v.tensor_reduce(mx[:, 3:4], wnat.rearrange("p w m d -> p (w m) d"), AX.XY, ALU.max, apply_absolute_value=True).then_inc(S["wmax"], 1)
            v.wait_ge(S["ld_wih"], 16)
            v.tensor_reduce(mx[:, 2:3], wih, AX.XY, ALU.max, apply_absolute_value=True).then_inc(S["wmax"], 1)

            def scales(a, b):
                link(v.tensor_scalar(mx[:, 5 + a:5 + b], mx[:, 5 + a:5 + b], 1e-30, None, ALU.max))
                if a == 0:
                    link(v.tensor_scalar(mx[:, 6:7], mx[:, 6:7], 1.0, None, ALU.max))
                link(v.tensor_scalar(mx[:, 11 + a:11 + b].bitcast(U32), mx[:, 5 + a:5 + b].bitcast(U32), 0x7F800000, None, ALU.bitwise_and))
                link(v.tensor_scalar(mx[:, 11 + a:11 + b], mx[:, 11 + a:11 + b], 2.0 ** -13, None, ALU.mult))
                link(v.reciprocal(scl[:, a:b], mx[:, 11 + a:11 + b]))

            v.wait_ge(S["amax"], 1)
            scales(0, 4)
            v.tensor_scalar(scl[:, 6:7], mx[:, 12:13], 1.0, None, ALU.mult).then_inc(S["scale"], 1)
            link(v.tensor_tensor(scl[:, 5:6], mx[:, 11:12], mx[:, 12:13], ALU.mult))
            v.tensor_scalar(scl[:, 7:8], scl[:, 5:6], -1.0, None, ALU.mult)
            v.tensor_tensor(scl[:, 8:9], mx[:, 12:13], mx[:, 14:15], ALU.mult)
            link(v.tensor_tensor(scl[:, 10:11], scl[:, 0:1], scl[:, 1:2], ALU.mult))
            v.tensor_scalar(identS[:, :], ident[:, :], scl[:, 10:11], None, ALU.mult)
            for k in range(KT):
                v.wait_ge(S["wih_c"], 2 * k + 1 if k == 0 else k + 1)
                link(v.scalar_tensor_tensor(wih16[:, 1, k, :], wih[:, k, :], scl[:, 2:3], wih16[:, 0, k, :], ALU.mult, ALU.subtract))
            v.wait_ge(S["wih_c"], KT)
            v.memset(GI[:, :, :, :], 0.0).then_inc(S["wih_c"], KT)
            for n in range(8):
                w, k = divmod(n, KT)
                v.wait_ge(S["wgh"], n + 1)
                v.scalar_tensor_tensor(wg16[:, w, 1, k, :], bank[n % 4][:, :], scl[:, 3:4], wg16[:, w, 0, k, :], ALU.mult, ALU.subtract).then_inc(S["wgl"], 1)
            for c in range(0, NXT, 2):
                v.wait_ge(S["tr"], 8 + c + 1)
                v.tensor_copy(xT[:, :, XT * c:XT * c + XT, :].rearrange("p k t b -> p k b t"),
                              bank[c % 4][:, :].rearrange("p (k b t) -> p k b t", k=KT, b=B)).then_inc(S["tr_e0"], 1)
            v.tensor_reduce(mx[:, 4:5], xnat, AX.XY, ALU.max, apply_absolute_value=True).then_inc(S["wmax"], 1)
            for k in range(KT):
                v.wait_ge(S["w16h"], k + 1)
                v.scalar_tensor_tensor(wh16[:, 1, k, :], whh[:, k, :], scl[:, 0:1], wh16[:, 0, k, :], ALU.mult, ALU.subtract).then_inc(S["w16l"], 1)
            v.wait_ge(S["amax"], 2)
            scales(4, 5)
            link(v.tensor_tensor(scl[:, 9:10], mx[:, 15:16], mx[:, 13:14], ALU.mult))
            v.wait_ge(S["tr_e0"], 8)
            v.wait_ge(S["tr_e1"], 8)
            v.tensor_scalar(hist[:, CH - 1, :], condT[:, :], scl[:, 1:2], None, ALU.mult).then_inc(S["scale"], 1)
            v.tensor_scalar(H[:, :, :, 0], condT[:, :].rearrange("p (k b) -> p k b", b=B), scl[:, 1:2], None, ALU.mult).then_inc(S["hinit"], 1)
            v.memset(H[:, :, :, 2:4], 0.0).then_inc(S["hinit"], 1)
            v.wait_ge(S["hinit"], 2)
            v.wait_ge(S["scale"], 2)
            v.tensor_tensor(H[:, :, :, 1], hist[:, CH - 1, :].rearrange("p (k b) -> p k b", b=B), H[:, :, :, 0], ALU.subtract).then_inc(S["hinit"], 1)
            for c in range(3):
                link(v.tensor_copy(GI[:, :, :, 32 + c:60:7], bn16[:, c, :].unsqueeze(1).unsqueeze(3).broadcast_to([P, CH, KT, B])))

            v.wait_ge(S["ld_v"], 80)
            link(v.tensor_scalar(lam[:, 20:24], lam[:, 0:4], -1.0, None, ALU.mult))
            v.tensor_tensor(lam[:, 4:8], lam[:, 0:4], lam[:, 20:24], ALU.min).then_inc(S["c8"], 1)
            v.memset(gb[:, 12:13], 1.0 + 1e-6)
            v.memset(gb[:, 13:14], 1e-6)
            v.memset(fq[:, 29:30], 0.0)
            v.memset(ones[:, :], 1.0 / D)
            v.memset(ones1[:, :], 1.0)
            v.tensor_copy(id16[:, :], ident[:, :])
            v.tensor_tensor(kq[:, :], kq[:, :], kqr[:, :], ALU.mult)
            v.tensor_reduce(fq[:, 8:9], gb[:, 0:4], AX.X, ALU.max, apply_absolute_value=True)
            v.tensor_reduce(fq[:, 9:10], gb[:, 4:8], AX.X, ALU.max, apply_absolute_value=True).then_inc(S["xq"], 1)
            v.wait_ge(S["xq"], 2)
            link(v.tensor_scalar(fq[:, 12:13], fq[:, 10:11], float(D) ** 0.5 * 1.01, None, ALU.mult))
            link(v.tensor_tensor(fq[:, 12:13], fq[:, 12:13], fq[:, 11:12], ALU.add))
            link(v.tensor_scalar(fq[:, 12:13], fq[:, 12:13], 1e-30, None, ALU.max))
            link(v.tensor_scalar(fq[:, 13:14].bitcast(U32), fq[:, 12:13].bitcast(U32), 0x7F800000, None, ALU.bitwise_and))
            link(v.tensor_scalar(fq[:, 13:14], fq[:, 13:14], 2.0 ** -14, None, ALU.mult))
            link(v.reciprocal(fq[:, 14:15], fq[:, 13:14]))
            v.tensor_scalar(gb[:, 8:12], gb[:, 0:4], fq[:, 14:15], None, ALU.mult)
            v.tensor_scalar(gb2[:, :], gb[:, 4:8], fq[:, 14:15], None, ALU.mult)
            v.wait_ge(S["c8"], 3)
            link(v.tensor_scalar(lam[:, 20:24], lam[:, 0:4], 0.0, None, ALU.max))
            link(v.tensor_tensor(lam[:, 16:20], lam[:, 20:24], lam[:, 12:16], ALU.add))
            link(v.tensor_scalar(lam[:, 16:20], lam[:, 16:20], -8.0, None, ALU.mult))

            def gi_evac(m, bk):
                g, k = divmod(m, KT)
                v.tensor_scalar(gi_next[:, :, k, 4 * g:4 * g + 4], bk[:, 0:TOK].rearrange("p (t b) -> p t b", b=B),
                                scl[:, 9:10], bsum[:, m:m + 1], ALU.mult, ALU.add).then_inc(S["gi_e"], 1)

            for m in range(12):
                v.wait_ge(S["fil"], m + 1)
                gi_evac(m, F[m % 2])

            def kb(a, hf):
                return a[:, 8 * hf:8 * hf + 8].rearrange("p (k b) -> p k b", b=B)

            def step(i, s, attn):
                t = i * CH + s
                before = (s - 1) % CH
                first = not attn and s == 0

                def sum_parts(name, g, dst, ready, hf):
                    v.wait_ge(S[ready], 2 * t + hf + 1)
                    v.tensor_reduce(dst[:, 8 * hf:8 * hf + 8], GB[g][hf][:, 0:32].rearrange("p (u c) -> p u c", c=4),
                                    AX.X, ALU.add).then_inc(S[name], 1)

                def scan_n(hf):
                    v.wait_ge(S["n_ps"], 2 * t + hf + 1)
                    v.wait_ge(S["r_sig"], 2 * t + hf + 1)
                    v.tensor_tensor_scan(y7[:, 56 * hf:56 * hf + 56], r7[:, 56 * hf:56 * hf + 56], GB[2][hf][:, 0:56], 0.0,
                                         ALU.mult, ALU.add).then_inc(S["scan"], 1)

                def z_h(hf):
                    v.wait_ge(S["z_sig"], 2 * t + hf + 1)
                    if not first:
                        v.wait_ge(S["hs"], 2 * t + hf - 1)
                    v.tensor_tensor(zh[:, 8 * hf:8 * hf + 8], z_t[:, 8 * hf:8 * hf + 8], hist[:, before, 8 * hf:8 * hf + 8], ALU.mult).then_inc(S["zh_ok"], 1)
                    v.tensor_tensor(H[:, 2 * hf:2 * hf + 2, :, 0], kb(z_t, hf), kb(hist[:, before, :], hf), ALU.mult).then_inc(S["zh_ok"], 1)

                def z_h_low(hf):
                    v.wait_ge(S["zh_ok"], 2 * (2 * t + hf + 1))
                    v.tensor_tensor(H[:, 2 * hf:2 * hf + 2, :, 1], kb(zh, hf), H[:, 2 * hf:2 * hf + 2, :, 0], ALU.subtract)

                def new_part(hf):
                    v.wait_ge(S["th"], 2 * t + hf + 1)
                    v.scalar_tensor_tensor(v_t[:, 8 * hf:8 * hf + 8], n_t[:, 8 * hf:8 * hf + 8], scl[:, 1:2], omz[:, 8 * hf:8 * hf + 8], ALU.mult, ALU.mult).then_inc(S["v_ok"], 1)
                    v.scalar_tensor_tensor(H[:, 2 * hf:2 * hf + 2, :, 2], kb(n_t, hf), scl[:, 1:2], kb(omz, hf), ALU.mult, ALU.mult).then_inc(S["v_ok"], 1)

                def new_low(hf):
                    v.wait_ge(S["v_ok"], 2 * (2 * t + hf + 1))
                    v.tensor_tensor(H[:, 2 * hf:2 * hf + 2, :, 3], kb(v_t, hf), H[:, 2 * hf:2 * hf + 2, :, 2], ALU.subtract).then_inc(S["h_ok"], 1)

                def state(hf):
                    if s == 0 and attn and hf == 0:
                        v.wait_ge(S["hp_c"], 3 * i)
                    v.tensor_tensor(hist[:, s, 8 * hf:8 * hf + 8], zh[:, 8 * hf:8 * hf + 8], v_t[:, 8 * hf:8 * hf + 8], ALU.add).then_inc(S["hs"], 1)

                sum_parts("r_sum", 0, rsum, "r_ps", 0)
                sum_parts("z_sum", 1, zsum, "z_ps", 0)
                scan_n(0)
                sum_parts("r_sum", 0, rsum, "r_ps", 1)
                z_h(0)
                sum_parts("z_sum", 1, zsum, "z_ps", 1)
                z_h_low(0)
                new_part(0)
                new_low(0)
                scan_n(1)
                state(0)
                z_h(1)
                z_h_low(1)
                new_part(1)
                new_low(1)
                state(1)
                for q, kind, m in done_in(s, attn):
                    if kind == "gi":
                        v.wait_ge(S["fil"], (24 + 20 * (i - 1) if attn else 12) + q + 1)
                        if m == 0:
                            v.wait_ge(S["gsp"], 16 * i + 16)
                        gi_evac(m, F[q % 2])

            for s in range(CH):
                step(0, s, False)
            with v.Fori(1, NCH) as i:
                for s in range(CH):
                    step(i, s, True)

            al = B_reg[:, :].rearrange("p (k n) -> p k n", k=KT)
            sf = A_reg[:, :].rearrange("p (k n) -> p k n", k=KT)
            v.wait_ge(S["sih_c"], NCH + 1)

            nb = [0]

            def evac_q():
                n, g = divmod(nb[0], 6)
                if nb[0] % 2 == 0:
                    v.wait_ge(S["tq"], nb[0] + 1)
                    w = 1024 if g < 5 else 512
                    dst = Q_reg[:, n * KT * HP // 2 + 512 * g:n * KT * HP // 2 + 512 * g + w // 2].bitcast(F16)
                    v.tensor_copy(dst, bank[nb[0] % 4][:, 0:w // 2].bitcast(F16)).then_inc(S["tq_e0"], 1)
                nb[0] += 1

            def quant(n):
                v.wait_ge(S["aq"], n + 1)
                link(v.tensor_scalar(fq[:, 20 + n:21 + n], fq[:, 4 + n:5 + n], 0.5 / (HID * D), None, ALU.mult))
                link(v.tensor_scalar(fq[:, 24 + n:25 + n], fq[:, 20 + n:21 + n], -1.0, None, ALU.mult))
                if n:
                    v.wait_ge(S["tq"], 6 * n)
                link(v.tensor_scalar(qn, nat, fq[:, 20 + n:21 + n], None, ALU.is_gt))
                v.scalar_tensor_tensor(qn, nat, fq[:, 24 + n:25 + n], qn, ALU.is_lt, ALU.subtract).then_inc(S["qn_r"], 1)

            for k in range(KT):
                v.wait_ge(S["e_q"], k + 1)
                v.tensor_tensor(sf[:, k], tmp[:, k], sf[:, k], ALU.mult).then_inc(S["xb"], 1)
                v.wait_ge(S["xb"], k + 1)
                for b in range(B):
                    v.tensor_tensor_scan(sih[:, k, :, b], sgate[:, k, :, b], sih[:, k, :, b], 0.0, ALU.mult, ALU.add).then_inc(S["sc"], 1)
                if k >= 1:
                    v.wait_ge(S["x2"], k)
                    v.tensor_reduce(brT[:, k - 1, :], X2[:, k - 1].rearrange("p b (n t) -> p (b n) t", t=64), AX.X, ALU.add).then_inc(S["br"], 1)
            v.wait_ge(S["x2"], KT)
            v.tensor_reduce(brT[:, KT - 1, :], X2[:, KT - 1].rearrange("p b (n t) -> p (b n) t", t=64), AX.X, ALU.add).then_inc(S["br"], 1)
            v.wait_ge(S["wkT_e"], 8)
            for n in range(3):
                quant(n)
                for _ in range(6):
                    evac_q()
            link(v.tensor_scalar(fq[:, 27:28], fq[:, 26:27], 2.0, None, ALU.mult))
            link(v.reciprocal(fq[:, 28:29], fq[:, 14:15]))
            link(v.tensor_scalar(fq[:, 16:18], fq[:, 24:26], fq[:, 28:29], 2.0, ALU.mult, ALU.mult))
            v.wait_ge(S["keys"], 1)
            v.wait_ge(S["ssq"], 1)
            v.tensor_tensor_reduce(out=kqr[:, :], in0=bank[4][0:32, :], in1=kq[:, :], scale=1.0, scalar=0.0,
                                   op0=ALU.mult, op1=ALU.add, accum_out=sm[:, 2:3]).then_inc(S["dot"], 1)
            v.wait_ge(S["rms"], 1)
            link(v.reciprocal(sm[:, 3:4], sm[:, 1:2]))
            v.wait_ge(S["dot"], 1)
            v.tensor_tensor(sm[:, 4:5], sm[:, 2:3], sm[:, 3:4], ALU.mult).then_inc(S["scr"], 1)
            v.wait_ge(S["scT"], 1)
            scT = bank[5][0:1, 0:32].rearrange("p (b n) -> p b n", n=8)

            def row(o):
                return at1[0:1, o:o + 32].rearrange("p (b n) -> p b n", n=8)

            def per_b(o):
                return sm[0:1, o:o + 4].unsqueeze(2).broadcast_to([1, 4, 8])

            link(v.tensor_reduce(sm[0:1, 8:12], scT, AX.X, ALU.max))
            v.tensor_tensor(row(0), scT, per_b(8), ALU.subtract).then_inc(S["mxs"], 1)
            v.wait_ge(S["ex"], 1)
            link(v.tensor_reduce(sm[0:1, 12:16], row(32), AX.X, ALU.add))
            link(v.reciprocal(sm[0:1, 8:12], sm[0:1, 12:16]))
            v.tensor_tensor(row(96), row(32), per_b(8), ALU.mult).then_inc(S["att"], 1)
            v.wait_ge(S["atb"], 1)
            link(v.tensor_tensor(br2[:, :, :], brT[:, :, :], bank[6][:, 0:32].unsqueeze(1).broadcast_to([P, KT, 32]), ALU.mult))
            v.tensor_reduce(attT[:, :], br2[:, :, :].rearrange("p k (b n) -> p (k b) n", n=8), AX.X, ALU.add).then_inc(S["attT"], 1)
            v.wait_ge(S["pj"], 1)
            v.tensor_copy(projT[:, :], bank[7][:, 0:SB]).then_inc(S["pjs"], 1)
            v.wait_ge(S["pjs"], 1)

            Lb = bank[6]
            Ob = bank[4:6]

            def ln_a(b):
                if b:
                    v.wait_ge(S["yB"], 4 * b)
                    v.wait_ge(S["yf"], 4 * b)
                for k in range(KT):
                    x3 = v.tensor_scalar(xc[:, k, :], X2[:, k, b, :], projT[:, k * B + b:k * B + b + 1], None, ALU.add)
                    link(x3)
                v.memset(fq[:, 31:32], 0.0).then_inc(S["x3"], 1)
                v.wait_ge(S["mean"], b + 1)
                v.tensor_tensor(xc[:, :, :], xc[:, :, :], Lb[:, :].unsqueeze(1).broadcast_to([P, KT, T]), ALU.subtract).then_inc(S["xcs"], 1)

            def ln_b(b):
                v.wait_ge(S["stds"], b + 1)
                v.reciprocal(std[:, 1, :], std[:, 0, :]).then_inc(S["rst"], 1)
                v.wait_ge(S["rst"], b + 1)
                v.wait_ge(S["sqs"], b + 1)
                v.tensor_tensor(xc[:, :, :], xc[:, :, :], std[:, 1, :].unsqueeze(1).broadcast_to([P, KT, T]), ALU.mult).then_inc(S["yn"], 1)
                v.wait_ge(S["yh"], b + 1)
                v.wait_ge(S["yf"], 4 * b + 4)
                v.tensor_tensor(yhl[:, b % 2, 1, :], sq[:, :, :].rearrange("p k t -> p (k t)"), yhl[:, b % 2, 0, :], ALU.subtract).then_inc(S["yl"], 1)

            ln_a(0)
            ln_b(0)
            for b in range(B):
                for h in range(HT):
                    n = HT * b + h
                    hb = bank[0:2] if n % 2 == 0 else bank[2:4]
                    v.wait_ge(S["slu"], n + 1)
                    if n >= 2:
                        v.wait_ge(S["ghi"], n - 1)
                    v.scalar_tensor_tensor(gf[:, n % 2, :], hb[1][:, :], fq[:, 17:18], sl[:, n % 2, :], ALU.mult, ALU.mult).then_inc(S["gfd"], 1)
                    v.wait_ge(S["ghi"], n + 1)
                    if n >= 2:
                        v.wait_ge(S["glo"], n - 1)
                        v.wait_ge(S["gmid"], n - 1)
                    v.tensor_tensor(g1[:, n % 2, :], gf[:, n % 2, :], gp[:, 0, h, :], ALU.subtract).then_inc(S["gm1"], 1)
                    v.wait_ge(S["gmid"], n + 1)
                    v.tensor_tensor(gp[:, 2, h, :], g1[:, n % 2, :], gp[:, 1, h, :], ALU.subtract).then_inc(S["glo"], 1)
                    if b < B - 1 and h == 2:
                        ln_a(b + 1)
                    if b < B - 1 and h == 8:
                        ln_b(b + 1)
                for tt in range(4):
                    n = 4 * b + tt
                    v.wait_ge(S["o2"], n + 1)
                    v.wait_ge(S["xns"], n + 1)
                    if n >= 2:
                        v.wait_ge(S["out%d" % (n % 2)], 16 * (n // 2))
                    v.scalar_tensor_tensor(ob[:, n % 2, :], Ob[n % 2][:, :], fq[:, 27:28], xn[:, n % 2, :], ALU.mult, ALU.add).then_inc(S["obs"], 1)


def kernel(**a):
    import numpy as np
    import concourse.bacc as _bacc
    from concourse.bass_utils import run_bass_kernel_spmd as _run
    nc = _bacc.Bacc("TRN2", target_bir_lowering=False, num_devices=1)
    ident = np.eye(P, dtype=np.float32)
    names = ["x", "cond_2048", "L0_cond_W_ih", "L0_cond_W_hh", "L0_cond_b_ih", "L0_cond_b_hh", "L0_attn_W_in", "L0_attn_b_in", "L0_attn_W_gate", "L0_attn_b_gate", "L0_attn_forget_lambda", "L0_cond2_rms_weight", "L0_cond2_Wk", "L0_cond2_Wo", "L0_cond2_ln_gamma", "L0_cond2_ln_beta", "L0_ffn_w1", "L0_ffn_w3", "L0_ffn_w2"]
    arrs = {n: np.ascontiguousarray(a[n]) for n in names}
    arrs["ident"] = ident
    aps = [nc.dram_tensor("in_" + n, v.shape, F32, kind="ExternalInput").ap() for n, v in arrs.items()]
    o = nc.dram_tensor("o", (B, T, D), F32, kind="ExternalOutput").ap()
    gru(nc, *aps, o)
    r = _run(nc, [{"in_" + k: v for k, v in arrs.items()}], core_ids=[0])
    return r.results[0]["o"]
```

```python
from contextlib import ExitStack

import concourse.bass as bass
from concourse import mybir
import numpy as np

ALU = mybir.AluOpType
ACT = mybir.ActivationFunctionType
AX = mybir.AxisListType
F32 = mybir.dt.float32
F16 = mybir.dt.float16
BF16 = mybir.dt.bfloat16
U32 = mybir.dt.uint32
RMAX = bass.bass_isa.ReduceOp.max
RADD = bass.bass_isa.ReduceOp.add

P = 128
B, T, D = 4, 512, 512
KT = D // P
G3 = 3 * D
HID = 1365
CH = 8
NCH = T // CH
TOK = CH * B
SB = KT * B
XT = 32
NXT = T // XT
TS = 128
TB = TS * B
NTB = T // TS


def gru(nc, x, cond, W_ih, W_hh, b_ih, b_hh, W_in, b_in, W_gate, b_gate, lam_d, rmsw, Wk, Wo, gam, bet, w1, w3, w2, ident_d, out):
    with ExitStack() as ctx:
        def sb(name, shape, dt=F32):
            return ctx.enter_context(nc.sbuf_tensor(name, shape, dt))

        def sem(name):
            return ctx.enter_context(nc.semaphore(name))

        HT = (HID + P - 1) // P
        HP = HT * P
        A_reg = sb("A_reg", [P, KT * T * B])
        B_reg = sb("B_reg", [P, KT * T * B])
        X_reg = sb("X_reg", [P, KT * (T + 4 * CH) * B])
        W_reg = sb("W_reg", [P, 16640])
        Q_reg = sb("Q_reg", [P, 3 * KT * HP // 2])

        def view(reg, at, shape, dt=F32):
            n = int(np.prod(shape))
            words = n if dt == F32 else n // 2
            a = reg[:, at:at + words]
            if dt != F32:
                a = a.bitcast(dt)
            names = "abcd"[:len(shape)]
            return a.rearrange("p (%s) -> p %s" % (" ".join(names), " ".join(names)), **dict(zip(names, shape)))

        x_units = view(X_reg, 0, [KT, T + 4 * CH, B])
        wih_parts = view(W_reg, 0, [2, KT, G3], F16)
        whh_parts = view(W_reg, KT * G3, [2, KT, G3], F16)
        gate_w_parts = view(W_reg, 2 * KT * G3, [2, 2, KT, D], F16)
        h_all = view(A_reg, 0, [KT, T, B])
        whh_f32 = view(A_reg, 0, [KT, G3])
        wih_f32 = view(Q_reg, 2304, [KT, G3])
        x_rows = view(B_reg, 0, [NXT, D])
        gate_w_rows = view(W_reg, KT * G3, [2, KT, D])
        h_parts = view(W_reg, 0, [2, KT, 2, TB], F16)
        sig_in = view(W_reg, 4096, [2, KT, TB])
        alpha = view(W_reg, 8192, [2, KT, TB])
        beta = view(Q_reg, 0, [2, KT, TB])
        proj_wT = view(W_reg, 12544, [2, KT, D])
        w_rows = [view(W_reg, 0, [KT * HP]), view(W_reg, 6912, [KT * HP]), view(W_reg, 0, [KT * HP])]
        abs_w = view(W_reg, KT * HP, [HP], F16)
        ternary_w = [view(X_reg, o, [KT * HP], F16) for o in (0, KT * HP // 2, 0)]
        proj_w_rows = view(Q_reg, 4352, [2, KT, D])
        q1T = view(Q_reg, 0, [KT, HP], F16)
        q3T = view(Q_reg, KT * HP // 2, [KT, HP], F16)
        q2T = view(Q_reg, KT * HP, [HT, D], F16)
        x_mid = view(B_reg, 0, [KT, B, T])
        centered = view(A_reg, 0, [KT, T])
        squared = view(A_reg, 2048, [KT, T])
        y_parts = view(A_reg, 4096, [2, 2, KT * T], F16)
        g_parts = view(X_reg, 0, [2, HT, T], F16)
        silu_h1 = view(W_reg, 4096, [2, T])
        g_f32 = view(W_reg, 5120, [2, T])
        x_out_rows = view(W_reg, 0, [2, D])
        out_rows = view(W_reg, 1024, [2, D])
        std_rows = view(X_reg, KT * HP, [2, T])
        block_sums_T = sb("block_sums_T", [P, KT, 32])
        weighted_sums = sb("weighted_sums", [P, KT, 32])
        attended = sb("attended", [P, KT * B])
        projected = sb("projected", [P, KT * B])
        mean_ones = sb("mean_ones", [P, P])
        row_ones = sb("row_ones", [P, P])
        query = sb("query", [32, D])
        rms_weight = sb("rms_weight", [32, D])
        keys_squared = view(Q_reg, 0, [KT * P])[0:32, :]
        att_cols = sb("att_cols", [32, 16])
        abs_sums = sb("abs_sums", [P, 2, 12])
        xsum = view(X_reg, KT * HP + 2 * T, [T])
        att_rows = sb("att_rows", [1, 128])
        ln_consts = sb("ln_consts", [P, 4 * KT])
        ln_beta_scaled = sb("ln_beta_scaled", [P, KT])
        ident16 = sb("ident16", [P, P], F16)
        lambda_consts = sb("lambda_consts", [P, 6 * KT])
        ffn_consts = sb("ffn_consts", [P, 32])
        x_parts = view(Q_reg, 0, [2, KT, 2, TOK], F16)
        gi_next = view(Q_reg, 256, [2, CH, KT, 12])
        gi_parts = view(Q_reg, 1024, [2, CH, KT, 60], BF16)
        h_steps = view(Q_reg, 2944, [2, CH, SB])
        x_scaled = view(Q_reg, 3200, [KT, TOK])
        H_parts = sb("H_parts", [P, 2, KT, B, 4], F16)
        scan_factor = sb("scan_factor", [P, 7 * SB])
        scan_out = sb("scan_out", [P, 7 * SB])
        r_parts_sum = sb("r_parts_sum", [P, SB])
        z_parts_sum = sb("z_parts_sum", [P, SB])
        n_value = sb("n_value", [P, SB])
        z_value = sb("z_value", [P, SB])
        one_minus_z_scaled = sb("one_minus_z_scaled", [P, SB])
        z_part = sb("z_part", [P, SB])
        n_part = sb("n_part", [P, SB])
        identS = sb("identS", [P, P], BF16)
        bhn_parts = sb("bhn_parts", [P, 3, KT], BF16)
        bhn_rest = sb("bhn_rest", [P, 2, KT])
        ident = sb("ident", [P, P])
        bih = sb("bih", [P, 12])
        bhh = sb("bhh", [P, 12])
        bsum = sb("bsum", [P, 12])
        zeros = sb("zeros", [P, 8])
        att_bias = sb("att_bias", [P, 2, KT])
        condn = Q_reg[0:B, 0:D]
        condT = sb("condT", [P, SB])
        maxima = sb("maxima", [P, 16])
        x_maxima = sb("x_maxima", [P, NXT // 2])
        scl = sb("scl", [P, 16])

        bank = [ctx.enter_context(nc.psum_tensor(f"bank{k}", [P, 512], F32)) for k in range(8)]
        gate_bank = ((bank[0], bank[3]), (bank[1], bank[4]), (bank[2], bank[5]))
        gi_bank = bank[6:8]

        S = {}
        for n in ("abs_sums_done maxima_all abs_sums_all gate_sigmoid_done att_broadcast att_weights_done attended_done "
                  "block_sums_done softplus_done dve_chain cond_transposed key_dots beta_done alpha_squared alpha_done "
                  "att_exp_done unit_tile_done g_done g_high_done g_low_done gi_tile_read gi_split h_parts_ready "
                  "h_high_done h_low_done h0_ready h_kept h_step_done keys_done loaded_ident_cond loaded_biases "
                  "loaded_vectors loaded_gate_w loaded_whh loaded_wih loaded_proj_w loaded_x mean_done scores_shifted "
                  "n_products_done r_products_done z_products_done w_rows_cleared out_products_done out_rows_ready "
                  "one_minus_z_done stored_even stored_odd proj_products_done projected_done ternary_done r_gate_done "
                  "r_parts_added z_parts_added z_gate_done rms_done reciprocal_done linear_scan_done scores_row_done "
                  "scales_ready n_scan_done scores_done gated_h_done silu_done squares_done key_squares_done "
                  "ffn_products_done std_done tanh_done ternary_transposed ternary_T_even_read ternary_T_odd_read "
                  "prologue_transposed x_T_even_read x_T_odd_read n_part_done var_done whh_high_done whh_low_done "
                  "gate_w_high_done gate_w_low_done wih_split proj_w_transposed proj_w_T_read maxima_done x_mid_done "
                  "ln_x_done beta_applied centered_done x_out_rows_ready ln_bound x_split k_tiles_added "
                  "x_mid_transposed y_high_done y_f32_done y_low_done normalized z_part_done loaded_w1 loaded_w3 "
                  "loaded_w2").split():
            S[n] = sem("s_" + n)

        block = ctx.enter_context(nc.Block())

        sum_cols = (16, 16, 28)
        sum_at = (0, 16, 32)

        FILL_PER_STEP = 144 // CH

        def done_in(s):
            return [m for m in range(12) if (12 * m + 11) // FILL_PER_STEP == s]

        @block.sync
        def _(sp):
            sp.dma_start(ident[:, :], ident_d).then_inc(S["loaded_ident_cond"], 16)
            sp.dma_start(condn[:, :], cond).then_inc(S["loaded_ident_cond"], 16)
            with nc.allow_non_contiguous_dma(reason="small vectors"):
                sp.dma_start(bih[:, :], b_ih.rearrange("(m p) -> p m", p=P)).then_inc(S["loaded_biases"], 16)
                sp.dma_start(bhh[:, :], b_hh.rearrange("(m p) -> p m", p=P)).then_inc(S["loaded_biases"], 16)
                sp.dma_start(att_bias[:, 0, :], b_in.rearrange("(m p) -> p m", p=P)).then_inc(S["loaded_biases"], 16)
                sp.dma_start(att_bias[:, 1, :], b_gate.rearrange("(m p) -> p m", p=P)).then_inc(S["loaded_biases"], 16)
            with nc.allow_non_contiguous_dma(reason="small vectors"):
                sp.dma_start(lambda_consts[:, 0:KT], lam_d.rearrange("(m p) -> p m", p=P)).then_inc(S["loaded_vectors"], 16)
                sp.dma_start(ln_consts[:, 0:KT], gam.rearrange("(m p) -> p m", p=P)).then_inc(S["loaded_vectors"], 16)
                sp.dma_start(ln_consts[:, KT:2 * KT], bet.rearrange("(m p) -> p m", p=P)).then_inc(S["loaded_vectors"], 16)
            sp.dma_start(rms_weight[:, :], rmsw.unsqueeze(0).broadcast_to([32, D])).then_inc(S["loaded_vectors"], 16)
            sp.dma_start(query[:, :], cond[1:2, :].broadcast_to([32, D])).then_inc(S["loaded_vectors"], 16)
            for b in range(B):
                sp.dma_start(x_rows[XT * b:XT * b + XT, :, :], x[b].rearrange("(c t) d -> t c d", t=XT)).then_inc(S["loaded_x"], 16)
            sp.dma_start(whh_f32, W_hh.rearrange("(k p) n -> p k n", p=P)).then_inc(S["loaded_whh"], 16)
            sp.dma_start(gate_w_rows[:, 0], W_in.rearrange("(m p) d -> p m d", p=P)).then_inc(S["loaded_gate_w"], 16)
            sp.dma_start(gate_w_rows[:, 1], W_gate.rearrange("(m p) d -> p m d", p=P)).then_inc(S["loaded_gate_w"], 16)
            sp.dma_start(wih_f32[:, :, :], W_ih.rearrange("(k p) n -> p k n", p=P)).then_inc(S["loaded_wih"], 16)
            sp.wait_ge(S["h0_ready"], 3)
            sp.dma_start(proj_w_rows[:, 0], Wk.rearrange("(m p) d -> p m d", p=P)).then_inc(S["loaded_proj_w"], 16)
            sp.dma_start(proj_w_rows[:, 1], Wo.rearrange("(m p) d -> p m d", p=P)).then_inc(S["loaded_proj_w"], 16)
            nfull = HID // P
            rest = HID - nfull * P
            for n, w in enumerate((w1, w3, w2)):
                sp.wait_ge(S["w_rows_cleared"], n + 1)
                done = S[("loaded_w1", "loaded_w3", "loaded_w2")[n]]
                if n < 2:
                    v = w_rows[n].rearrange("p (h d) -> p h d", d=D)
                    sp.dma_start(v[:, 0:nfull, :], w[0:nfull * P, :].rearrange("(h p) d -> p h d", p=P)).then_inc(done, 16)
                    sp.dma_start(v[0:rest, nfull, :], w[nfull * P:HID, :]).then_inc(done, 16)
                else:
                    v = w_rows[n].rearrange("p (k h) -> p k h", k=KT)
                    for k in range(2):
                        sp.dma_start(v[:, 2 * k:2 * k + 2, 0:HID], w.rearrange("(k p) h -> p k h", p=P)[:, 2 * k:2 * k + 2, :]).then_inc(done, 16)
            for b in range(B):
                for tt in range(4):
                    n = 4 * b + tt
                    sp.wait_ge(S["out_rows_ready"], n + 1)
                    sp.dma_start(out[b, tt * P:(tt + 1) * P, :], out_rows[:, n % 2, :]).then_inc(S[("stored_even", "stored_odd")[n % 2]], 16)
            sp.wait_ge(S["stored_even"], 8 * 16)
            sp.wait_ge(S["stored_odd"], 8 * 16)

        @block.gpsimd
        def _(pool):
            pool.wait_ge(S["ln_bound"], 1)
            nc.gpsimd.partition_all_reduce(ffn_consts[:, 10:12], ffn_consts[:, 8:10], P, RMAX).then_inc(S["ln_bound"], 1)
            pool.wait_ge(S["maxima_done"], 5)
            nc.gpsimd.partition_all_reduce(maxima[:, 5:10], maxima[:, 0:5], P, RMAX).then_inc(S["maxima_all"], 1)

            def zero(n, w):
                return zeros[:, 0:1].unsqueeze(2).broadcast_to([P, n, w])

            def load_xs(chunk, par, first=False):
                if not first:
                    pool.wait_ge(S["x_split"], 3 * chunk)
                nc.gpsimd.tensor_tensor(x_scaled.rearrange("p k (t b) -> p k t b", b=B), x_units[:, :, bass.ds(chunk * CH, CH), :],
                                        scl[:, 4:5].unsqueeze(2).unsqueeze(3).broadcast_to([P, KT, CH, B]), ALU.mult).then_inc(S["x_split"], 1)
                pool.wait_ge(S["x_split"], 3 * chunk + 1)
                nc.gpsimd.tensor_tensor(x_parts[:, par, :, 0, :], x_scaled, zero(KT, TOK), ALU.add).then_inc(S["x_split"], 1)
                pool.wait_ge(S["x_split"], 3 * chunk + 2)
                nc.gpsimd.tensor_tensor(x_parts[:, par, :, 1, :], x_scaled, x_parts[:, par, :, 0, :], ALU.subtract).then_inc(S["x_split"], 1)

            def split(chunk, par):
                n = CH * KT
                src = gi_next[:, par].rearrange("p s k c -> p (s k) c")
                dst = gi_parts[:, par].rearrange("p s k c -> p (s k) c")
                rz, nn = src[:, :, 0:8], src[:, :, 8:12]

                def slots(c):
                    return dst[:, :, c:32:4], dst[:, :, 36 + c:60:7]

                for e, (a, w) in enumerate(((rz, 8), (nn, 4))):
                    nc.gpsimd.tensor_tensor(slots(0)[e], a, zero(n, w), ALU.add).then_inc(S["gi_split"], 1)
                pool.wait_ge(S["gi_split"], 8 * chunk + 2)
                for e, (a, w) in enumerate(((rz, 8), (nn, 4))):
                    nc.gpsimd.tensor_tensor(a, a, slots(0)[e], ALU.subtract).then_inc(S["gi_split"], 1)
                pool.wait_ge(S["gi_split"], 8 * chunk + 4)
                for e, (a, w) in enumerate(((rz, 8), (nn, 4))):
                    nc.gpsimd.tensor_tensor(slots(1)[e], a, zero(n, w), ALU.add).then_inc(S["gi_split"], 1)
                pool.wait_ge(S["gi_split"], 8 * chunk + 6)
                for e, (a, w) in enumerate(((rz, 8), (nn, 4))):
                    nc.gpsimd.tensor_tensor(slots(2)[e], a, slots(1)[e], ALU.subtract).then_inc(S["gi_split"], 1)

            def keep_h(c, par):
                pool.wait_ge(S["h_step_done"], 2 * CH * c)
                nc.gpsimd.tensor_tensor(h_all[:, :, bass.ds((c - 1) * CH, CH), :].rearrange("p k t b -> p t k b"),
                                        h_steps[:, par].rearrange("p t (k b) -> p t k b", b=B),
                                        scl[:, 6:7].unsqueeze(2).unsqueeze(3).broadcast_to([P, CH, KT, B]), ALU.mult).then_inc(S["h_kept"], 1)

            pool.wait_ge(S["wih_split"], 2 * KT)
            pool.wait_ge(S["x_T_even_read"], 8)
            pool.wait_ge(S["x_T_odd_read"], 8)
            load_xs(0, 0, True)
            load_xs(1, 1)
            pool.wait_ge(S["gi_tile_read"], 12)
            split(0, 0)
            load_xs(2, 0)

            def add_x(blk):
                ts = slice(blk * TS, (blk + 1) * TS)
                pool.wait_ge(S["linear_scan_done"], 16 * (blk + 1))
                nc.gpsimd.tensor_tensor(x_mid[:, :, :, ts].rearrange("p k b t -> p k t b"), x_units[:, :, ts, :], h_all[:, :, ts, :], ALU.add).then_inc(S["x_mid_done"], 1)

            def chunk(c, par, first):
                if not first:
                    keep_h(c, 1 - par)
                    pool.wait_ge(S["n_products_done"], 2 * CH * c)
                pool.wait_ge(S["gi_tile_read"], 12 * (c + 2))
                split(c + 1, 1 - par)
                load_xs(c + 3, 1 - par)

            chunk(0, 0, True)
            chunk(1, 1, False)
            with pool.Fori(1, NCH // 2) as i:
                chunk(2 * i, 0, False)
                chunk(2 * i + 1, 1, False)

            keep_h(NCH, 1)
            def pad_zero(n):
                if n < 2:
                    v = w_rows[n].rearrange("p (h d) -> p h d", d=D)[:, HID // P, :]
                else:
                    v = w_rows[n].rearrange("p (k h) -> p k h", k=KT)[:, :, HID:HP]
                nc.gpsimd.memset(v, 0.0).then_inc(S["w_rows_cleared"], 1)

            for blk in range(NTB):
                ts = slice(blk * TS, (blk + 1) * TS)
                pool.wait_ge(S["gate_sigmoid_done"], 8 * blk + 4)
                pool.wait_ge(S["h_low_done"], 4 * (blk + 1))
                nc.gpsimd.tensor_tensor(h_all[:, :, ts, :], h_all[:, :, ts, :], sig_in[:, blk % 2].rearrange("p k (t b) -> p k t b", b=B),
                                        ALU.mult).then_inc(S["gated_h_done"], 1)
                if blk:
                    add_x(blk - 1)
            def sum_abs(n):
                pool.wait_ge(S["abs_sums_done"], 4 * (n + 1))
                nc.gpsimd.partition_all_reduce(abs_sums[:, 1, 4 * n:4 * n + 4], abs_sums[:, 0, 4 * n:4 * n + 4], P, RADD).then_inc(S["abs_sums_all"], 1)

            def sum_k(src, ready, n):
                pool.wait_ge(S[ready], n)
                nc.gpsimd.tensor_tensor(xsum[:, :], src[:, 0, :], src[:, 1, :], ALU.add).then_inc(S["k_tiles_added"], 1)
                for k in (2, 3):
                    sums[0] += 1
                    pool.wait_ge(S["k_tiles_added"], sums[0])
                    nc.gpsimd.tensor_tensor(xsum[:, :], xsum[:, :], src[:, k, :], ALU.add).then_inc(S["k_tiles_added"], 1)
                sums[0] += 1

            sums = [0]
            pool.wait_ge(S["unit_tile_done"], 12 * (NCH + 2) + 8 * NTB)
            pool.wait_ge(S["gated_h_done"], NTB)
            pad_zero(0)
            pool.wait_ge(S["linear_scan_done"], 16 * NTB)
            pad_zero(1)
            add_x(NTB - 1)
            sum_abs(0)
            pool.wait_ge(S["ternary_done"], 1)
            pad_zero(2)
            sum_abs(1)
            sum_k(centered, "ln_x_done", KT)
            sum_abs(2)
            pool.wait_ge(S["mean_done"], 1)
            sum_k(squared, "squares_done", 1)
            for b in range(1, B):
                pool.wait_ge(S["var_done"], b)
                sum_k(centered, "ln_x_done", KT * (b + 1))
                pool.wait_ge(S["mean_done"], b + 1)
                sum_k(squared, "squares_done", b + 1)

        @block.tensor
        def _(pe):
            pe.wait_ge(S["loaded_ident_cond"], 32)
            for k in range(KT):
                mm = pe.transpose(bank[7][:, k * B:(k + 1) * B], condn[:, k * P:(k + 1) * P], ident[0:B, 0:B])
            mm.then_inc(S["cond_transposed"], 1)
            pe.wait_ge(S["loaded_x"], 16 * B)
            for c in range(NXT):
                if c >= 4:
                    pe.wait_ge(S["x_T_even_read"] if c % 2 == 0 else S["x_T_odd_read"], (c - 4) // 2 + 1)
                for k in range(KT):
                    mm = pe.transpose(bank[c % 4][:, k * P:(k + 1) * P], x_rows[:, c, k * P:(k + 1) * P], ident[:, :])
                mm.then_inc(S["prologue_transposed"], 1)

            def transpose_w(n):
                w, k = divmod(n, KT)
                if n >= 4:
                    pe.wait_ge(S["gate_w_low_done"], n - 3)
                for m in range(KT):
                    mm = pe.transpose(bank[n % 4][:, m * P:(m + 1) * P], gate_w_rows[:, w, m, k * P:(k + 1) * P], ident[:, :])
                mm.then_inc(S["prologue_transposed"], 1)

            pe.wait_ge(S["loaded_gate_w"], 32)
            pe.wait_ge(S["x_T_even_read"], 8)
            pe.wait_ge(S["x_T_odd_read"], 8)
            for n in range(4):
                transpose_w(n)

            PRODUCTS = [(k, w, p) for k in range(KT) for w, p in ((0, 0), (0, 1), (1, 0))]

            def product(m, j, bk, par):
                k, w, p = PRODUCTS[j]
                mm = pe.matmul(bk[:, 0:TOK], wih_parts[:, w, k, m * P:(m + 1) * P], x_parts[:, par, k, p, :], start=(j == 0), stop=(j == 11))
                if j == 11:
                    mm.then_inc(S["unit_tile_done"], 1)

            pe.wait_ge(S["cond_transposed"], 2)
            pe.wait_ge(S["wih_split"], 2 * KT)
            def gi_early(chunk):
                pe.wait_ge(S["x_split"], 3 * (chunk + 1))
                for m in range(12):
                    if chunk or m >= 2:
                        pe.wait_ge(S["gi_tile_read"], 12 * chunk + m - 1)
                    for j in range(12):
                        product(m, j, gi_bank[m % 2], chunk)

            gi_early(0)
            for n in range(4, 8):
                transpose_w(n)
            gi_early(1)
            pe.wait_ge(S["h0_ready"], 3)
            pe.wait_ge(S["whh_low_done"], KT)

            def inject(g, hf, s, par):
                w = sum_cols[g]
                pe.matmul(gate_bank[g][hf][:, 0:2 * w].rearrange("p (k c) -> p k c", k=2), identS[:, :],
                          gi_parts[:, par, s, 2 * hf:2 * hf + 2, sum_at[g]:sum_at[g] + w], start=True, stop=False, skip_group_check=True)

            def products(g, hf, kh, s, tiles=(0, 1)):
                w7 = sum_cols[g] // B
                for m in tiles:
                    o = gate_bank[g][hf][:, m * sum_cols[g]:(m + 1) * sum_cols[g]].rearrange("p (b c) -> p b c", c=w7)[:, :, 0:4]
                    for w in range(2):
                        for k in (2 * kh, 2 * kh + 1):
                            mm = pe.matmul(o, whh_parts[:, w, k, g * D + (2 * hf + m) * P:g * D + (2 * hf + m + 1) * P], H_parts[:, s % 2, k, :, :],
                                           start=False, stop=(kh == 1 and w == 1 and k == KT - 1), skip_group_check=True)
                return mm

            def step(c, s, par, first):
                t = c * CH + s
                if s == 0:
                    pe.wait_ge(S["gi_split"], 8 * (c + 1))

                def start_sums(g, hf):
                    if not first:
                        pe.wait_ge(S[("r_parts_added", "z_parts_added", "n_scan_done")[g]], 2 * t - 1 + hf)
                    inject(g, hf, s, par)

                for g in range(3):
                    start_sums(g, 0)
                if not first:
                    pe.wait_ge(S["h_parts_ready"], 2 * t - 1)
                for g in range(3):
                    products(g, 0, 0, s)
                start_sums(0, 1)
                products(0, 1, 0, s, (0,))
                if not first:
                    pe.wait_ge(S["h_parts_ready"], 2 * t)
                for g, done in ((0, "r_products_done"), (1, "z_products_done"), (2, "n_products_done")):
                    products(g, 0, 1, s).then_inc(S[done], 1)
                products(0, 1, 0, s, (1,))
                products(0, 1, 1, s).then_inc(S["r_products_done"], 1)
                for g, done in ((1, "z_products_done"), (2, "n_products_done")):
                    start_sums(g, 1)
                    products(g, 1, 0, s)
                    products(g, 1, 1, s).then_inc(S[done], 1)
                for f in range(FILL_PER_STEP * s, FILL_PER_STEP * (s + 1)):
                    m, j = divmod(f, 12)
                    if j == 0:
                        if m == 0:
                            pe.wait_ge(S["x_split"], 3 * (c + 3))
                        pe.wait_ge(S["gi_tile_read"], 12 * (c + 2) + max(m - 1, 0))
                    product(m, j, gi_bank[m % 2], par)

            for s in range(2 * CH):
                step(s // CH, s % CH, s // CH, s == 0)
            with pe.Fori(1, NCH // 2) as i:
                for s in range(2 * CH):
                    step(2 * i + s // CH, s % CH, s // CH, False)

            pe.wait_ge(S["gi_tile_read"], 12 * (NCH + 2))
            pe.wait_ge(S["h_parts_ready"], 2 * T)
            for blk in range(NTB):
                pe.wait_ge(S["h_low_done"], 4 * (blk + 1))
                for m in range(8):
                    n = 8 * blk + m
                    if n >= 8:
                        pe.wait_ge(S["gate_sigmoid_done"], n - 7)
                    gate, e = divmod(m, KT)
                    for j, (k, w, p) in enumerate(PRODUCTS):
                        mm = pe.matmul(bank[m][:, :], gate_w_parts[:, gate, w, k, e * P:(e + 1) * P], h_parts[:, blk % 2, k, p, :],
                                       start=(j == 0), stop=(j == 11))
                    mm.then_inc(S["unit_tile_done"], 1)
            pe.wait_ge(S["loaded_proj_w"], 32)
            for n in range(8):
                w, k = divmod(n, KT)
                if n == 0:
                    pe.wait_ge(S["gate_sigmoid_done"], 8 * NTB)
                if n >= 4:
                    pe.wait_ge(S["proj_w_T_read"], n - 3)
                for m in range(KT):
                    mm = pe.transpose(bank[n % 4][:, m * P:(m + 1) * P], proj_w_rows[:, w, m, k * P:(k + 1) * P], ident[:, :])
                mm.then_inc(S["proj_w_transposed"], 1)
            pe.wait_ge(S["proj_w_T_read"], 8)
            pe.wait_ge(S["block_sums_done"], KT * NTB)
            for k in range(KT):
                mm = pe.matmul(bank[4][0:32, :], block_sums_T[:, k, :], proj_wT[:, 0, k, :], start=(k == 0), stop=(k == KT - 1))
            mm.then_inc(S["keys_done"], 1)
            pe.wait_ge(S["scores_done"], 1)
            pe.transpose(bank[5][0:1, 0:32], att_cols[:, 4:5], ident[0:32, 0:32]).then_inc(S["scores_row_done"], 1)
            pe.wait_ge(S["att_weights_done"], 1)
            pe.matmul(bank[6][:, 0:32], row_ones[0:1, :], att_rows[0:1, 96:128], start=True, stop=True).then_inc(S["att_broadcast"], 1)
            pe.wait_ge(S["attended_done"], 1)
            for m in range(KT):
                for k in range(KT):
                    mm = pe.matmul(bank[7][:, m * B:(m + 1) * B], proj_wT[:, 1, k, m * P:(m + 1) * P], attended[:, k * B:(k + 1) * B],
                                   start=(k == 0), stop=(k == KT - 1))
            mm.then_inc(S["proj_products_done"], 1)
            hA, hB, Ob, Lb, Tb = bank[0:2], bank[2:4], bank[4:6], bank[6], bank[7]

            def ln_mean(b):
                pe.wait_ge(S["ln_x_done"], KT * (b + 1))
                if b:
                    pe.wait_ge(S["std_done"], b)
                pe.wait_ge(S["k_tiles_added"], 6 * b + 3)
                pe.matmul(Lb[:, :], mean_ones[:, :], xsum[:, :], start=True, stop=True).then_inc(S["mean_done"], 1)

            def ln_var(b):
                pe.wait_ge(S["centered_done"], b + 1)
                pe.wait_ge(S["squares_done"], b + 1)
                pe.wait_ge(S["k_tiles_added"], 6 * b + 6)
                pe.matmul(Lb[:, :], mean_ones[:, :], xsum[:, :], start=True, stop=True).then_inc(S["var_done"], 1)

            def ternary(n):
                nb = 6 * n
                pe.wait_ge(S["ternary_done"], n + 1)
                for blk in range(HT * KT):
                    if blk % 8 == 0:
                        if nb >= 4:
                            pe.wait_ge(S["ternary_T_even_read"] if nb % 2 == 0 else S["ternary_T_odd_read"], (nb - 4) // 2 + 1)
                        bk = bank[nb % 4][:, :].bitcast(F16)
                    if n < 2:
                        k, h = divmod(blk, HT)
                        src = ternary_w[n][:, h * D + k * P:h * D + (k + 1) * P]
                    else:
                        h, k = divmod(blk, KT)
                        src = ternary_w[n][:, k * HP + h * P:k * HP + (h + 1) * P]
                    mm = pe.transpose(bk[:, (blk % 8) * P:(blk % 8 + 1) * P], src, ident16[:, :])
                    if blk % 8 == 7 or blk == HT * KT - 1:
                        mm.then_inc(S["ternary_transposed"], 1)
                        nb += 1
            pe.wait_ge(S["projected_done"], 1)
            ternary(0)
            ln_mean(0)
            ternary(1)
            ln_var(0)
            ternary(2)
            pe.wait_ge(S["ternary_T_even_read"], 9)
            pe.wait_ge(S["ternary_T_odd_read"], 9)
            for b in range(B):
                pe.wait_ge(S["y_low_done"], KT * (b + 1))
                for h in range(HT):
                    n = HT * b + h
                    if n >= 2:
                        pe.wait_ge(S["g_done"], n - 1)
                    hb = hA if n % 2 == 0 else hB
                    for qT, bk in ((q1T, hb[0]), (q3T, hb[1])):
                        for k in range(KT):
                            for part in range(2):
                                mm = pe.matmul(bk[:, :], qT[:, k, h * P:(h + 1) * P], y_parts[:, b % 2, part, k * T:(k + 1) * T],
                                               start=(k == 0 and part == 0), stop=(k == KT - 1 and part == 1))
                    mm.then_inc(S["ffn_products_done"], 1)
                    if b < B - 1 and h == 3:
                        ln_mean(b + 1)
                    if b < B - 1 and h == 7:
                        ln_var(b + 1)
                for tt in range(4):
                    n = 4 * b + tt
                    if n >= 1:
                        pe.wait_ge(S["x_out_rows_ready"], n)
                    for k in range(KT):
                        mm = pe.transpose(Tb[:, k * P:(k + 1) * P], x_mid[:, k, b, tt * P:(tt + 1) * P], ident[:, :])
                    mm.then_inc(S["x_mid_transposed"], 1)
                    if n >= 2:
                        pe.wait_ge(S["out_rows_ready"], n - 1)
                    for h in range(HT):
                        if tt == 0:
                            pe.wait_ge(S["g_low_done"], HT * b + h + 1)
                        for part in range(2):
                            mm = pe.matmul(Ob[n % 2][:, :], g_parts[:, part, h, tt * P:(tt + 1) * P], q2T[:, h, :],
                                           start=(h == 0 and part == 0), stop=(h == HT - 1 and part == 1))
                    mm.then_inc(S["out_products_done"], 1)

        @block.scalar
        def _(act):
            act.wait_ge(S["softplus_done"], 1)
            act.activation(lambda_consts[:, 8:12], lambda_consts[:, 4:8], ACT.Exp).then_inc(S["softplus_done"], 1)
            act.wait_ge(S["softplus_done"], 2)
            act.activation(lambda_consts[:, 12:16], lambda_consts[:, 8:12], ACT.Ln, bias=1.0).then_inc(S["softplus_done"], 1)

            for c in range(1, NXT, 2):
                act.wait_ge(S["prologue_transposed"], c + 1)
                act.copy(x_units[:, :, XT * c:XT * c + XT, :].rearrange("p k t b -> p k b t"),
                         bank[c % 4][:, :].rearrange("p (k b t) -> p k b t", k=KT, b=B)).then_inc(S["x_T_odd_read"], 1)
            def gi_tile(m, bk, par):
                g, k = divmod(m, KT)
                act.activation(gi_next[:, par, :, k, 4 * g:4 * g + 4], bk[:, 0:TOK].rearrange("p (t b) -> p t b", b=B),
                               ACT.Identity, scale=scl[:, 9:10], bias=bsum[:, m:m + 1]).then_inc(S["gi_tile_read"], 1)

            def gi_early(chunk):
                for m in range(12):
                    act.wait_ge(S["unit_tile_done"], 12 * chunk + m + 1)
                    gi_tile(m, gi_bank[m % 2], chunk)

            def wg_high(n):
                w, k = divmod(n, KT)
                act.wait_ge(S["prologue_transposed"], NXT + n + 1)
                act.activation(gate_w_parts[:, w, 0, k, :], bank[n % 4][:, :], ACT.Copy, scale=scl[:, 3:4]).then_inc(S["gate_w_high_done"], 1)

            act.wait_ge(S["scales_ready"], 1)
            for k in range(KT):
                act.activation(wih_parts[:, 0, k, :], wih_f32[:, k, :], ACT.Copy, scale=scl[:, 2:3]).then_inc(S["wih_split"], 1)
            for n in range(4):
                wg_high(n)
            gi_early(0)
            for n in range(4, 8):
                wg_high(n)
            for k in range(KT):
                act.activation(whh_parts[:, 0, k, :], whh_f32[:, k, :], ACT.Copy, scale=scl[:, 0:1]).then_inc(S["whh_high_done"], 1)
            gi_early(1)

            def step(c, s, par, first):
                t = c * CH + s

                def r_gate(hf):
                    act.wait_ge(S["r_parts_added"], 2 * t + hf + 1)
                    act.activation(scan_factor[:, 56 * hf + 4:56 * hf + 56:7], r_parts_sum[:, 8 * hf:8 * hf + 8], ACT.Sigmoid, scale=scl[:, 5:6]).then_inc(S["r_gate_done"], 1)

                def z_gate(hf):
                    act.wait_ge(S["z_parts_added"], 2 * t + hf + 1)
                    act.activation(z_value[:, 8 * hf:8 * hf + 8], z_parts_sum[:, 8 * hf:8 * hf + 8], ACT.Sigmoid, scale=scl[:, 5:6]).then_inc(S["z_gate_done"], 1)

                def new_state(hf):
                    act.wait_ge(S["n_scan_done"], 2 * t + hf + 1)
                    act.activation(n_value[:, 8 * hf:8 * hf + 8], scan_out[:, 56 * hf + 6:56 * hf + 56:7], ACT.Tanh, scale=scl[:, 5:6]).then_inc(S["tanh_done"], 1)

                r_gate(0)
                z_gate(0)
                new_state(0)
                r_gate(1)
                z_gate(1)
                new_state(1)
                for m in done_in(s):
                    act.wait_ge(S["unit_tile_done"], 12 * (c + 2) + m + 1)
                    if m == 0:
                        act.wait_ge(S["gi_split"], 8 * (c + 1))
                    gi_tile(m, gi_bank[m % 2], par)

            for s in range(2 * CH):
                step(s // CH, s % CH, s // CH, s == 0)
            with act.Fori(1, NCH // 2) as i:
                for s in range(2 * CH):
                    step(2 * i + s // CH, s % CH, s // CH, False)

            def high(blk):
                if blk >= 2:
                    act.wait_ge(S["unit_tile_done"], 12 * (NCH + 2) + 8 * (blk - 1))
                for k in range(KT):
                    act.activation(h_parts[:, blk % 2, k, 0, :].rearrange("p (t b) -> p t b", b=B), h_all[:, k, blk * TS:(blk + 1) * TS, :],
                                   ACT.Copy, scale=scl[:, 1:2]).then_inc(S["h_high_done"], 1)

            act.wait_ge(S["h_kept"], NCH)
            act.wait_ge(S["unit_tile_done"], 12 * (NCH + 2))
            act.wait_ge(S["n_products_done"], 2 * T)
            high(0)
            high(1)
            for blk in range(NTB):
                o = blk % 2
                for m in range(8):
                    gate, e = divmod(m, KT)
                    act.wait_ge(S["unit_tile_done"], 12 * (NCH + 2) + 8 * blk + m + 1)
                    if blk >= 2 and m == 0:
                        act.wait_ge(S["gated_h_done"], blk)
                        act.wait_ge(S["linear_scan_done"], 16 * (blk - 1))
                    dst = sig_in if gate == 0 else alpha
                    act.activation(dst[:, o, e, :], bank[m][:, :], ACT.Sigmoid, scale=scl[:, 8:9], bias=att_bias[:, gate, e:e + 1]).then_inc(S["gate_sigmoid_done"], 1)
                if blk < NTB - 2:
                    high(blk + 2)
                act.wait_ge(S["gate_sigmoid_done"], 8 * blk + 8)
                for k in range(KT):
                    act.activation(alpha[:, o, k, :], alpha[:, o, k, :], ACT.Exp, scale=lambda_consts[:, 16 + k:17 + k]).then_inc(S["alpha_done"], 1)
                act.wait_ge(S["alpha_done"], KT * (blk + 1))
                if blk >= 2:
                    act.wait_ge(S["beta_applied"], blk - 1)
                act.activation(beta[:, o], alpha[:, o], ACT.Square).then_inc(S["alpha_squared"], 1)
                act.wait_ge(S["alpha_squared"], blk + 1)
                act.activation(beta[:, o], beta[:, o], ACT.Sqrt, scale=-1.0, bias=ln_consts[:, 12:13]).then_inc(S["beta_done"], 1)
            for n in range(8):
                w, k = divmod(n, KT)
                act.wait_ge(S["proj_w_transposed"], n + 1)
                if n == 0:
                    act.wait_ge(S["unit_tile_done"], 12 * (NCH + 2) + 8 * NTB)
                act.copy(proj_wT[:, w, k, :], bank[n % 4][:, :]).then_inc(S["proj_w_T_read"], 1)
            def sum_abs(n):
                act.wait_ge(S[("loaded_w1", "loaded_w3", "loaded_w2")[n]], 32)
                for q in range(4):
                    if n or q:
                        act.wait_ge(S["abs_sums_done"], 4 * n + q)
                    act.activation(abs_w, w_rows[n][:, q * HP:(q + 1) * HP], ACT.Abs, accum_out=abs_sums[:, 0, 4 * n + q:4 * n + q + 1]).then_inc(S["abs_sums_done"], 1)

            def move_ternary(n):
                for g in range(6):
                    nb = 6 * n + g
                    if nb % 2:
                        act.wait_ge(S["ternary_transposed"], nb + 1)
                        w = 1024 if g < 5 else 512
                        dst = Q_reg[:, n * KT * HP // 2 + 512 * g:n * KT * HP // 2 + 512 * g + w // 2].bitcast(F16)
                        act.copy(dst, bank[nb % 4][:, 0:w // 2].bitcast(F16)).then_inc(S["ternary_T_odd_read"], 1)

            def ln_sq(b):
                act.wait_ge(S["centered_done"], b + 1)
                if b:
                    act.wait_ge(S["y_low_done"], KT * b)
                act.activation(squared[:, :, :], centered[:, :, :], ACT.Square).then_inc(S["squares_done"], 1)

            def ln_std(b):
                act.wait_ge(S["var_done"], b + 1)
                act.activation(std_rows[:, 0, :], Lb[:, :], ACT.Sqrt, bias=ln_consts[:, 13:14]).then_inc(S["std_done"], 1)

            def ln_y(b, tiles):
                act.wait_ge(S["normalized"], b + 1)
                if b >= 2:
                    act.wait_ge(S["ffn_products_done"], HT * (b - 1))
                for k in tiles:
                    act.activation(y_parts[:, b % 2, 0, k * T:(k + 1) * T], centered[:, k, :], ACT.Identity, scale=ln_consts[:, 8 + k:9 + k], bias=ln_beta_scaled[:, k:k + 1]).then_inc(S["y_high_done"], 1)
                    act.activation(squared[:, k, :], centered[:, k, :], ACT.Identity, scale=ln_consts[:, 8 + k:9 + k], bias=ln_beta_scaled[:, k:k + 1]).then_inc(S["y_f32_done"], 1)

            Lb = bank[6]
            sum_abs(0)
            act.wait_ge(S["keys_done"], 1)
            act.activation(keys_squared[:, :], bank[4][0:32, :], ACT.Square, accum_out=att_cols[:, 0:1]).then_inc(S["key_squares_done"], 1)
            act.wait_ge(S["key_squares_done"], 1)
            act.activation(att_cols[:, 1:2], att_cols[:, 0:1], ACT.Sqrt, scale=1.0 / D, bias=ln_consts[0:32, 13:14]).then_inc(S["rms_done"], 1)
            act.wait_ge(S["scores_shifted"], 1)
            act.activation(att_rows[0:1, 32:64], att_rows[0:1, 0:32], ACT.Exp).then_inc(S["att_exp_done"], 1)

            sum_abs(1)
            move_ternary(0)
            sum_abs(2)
            ln_sq(0)
            move_ternary(1)
            ln_std(0)
            ln_y(0, range(KT))
            move_ternary(2)
            for b in range(B):
                for h in range(HT):
                    n = HT * b + h
                    hb = bank[0:2] if n % 2 == 0 else bank[2:4]
                    act.wait_ge(S["ffn_products_done"], n + 1)
                    if n >= 2:
                        act.wait_ge(S["g_done"], n - 1)
                    act.activation(silu_h1[:, n % 2, :], hb[0][:, :], ACT.Silu, scale=ffn_consts[:, 16:17]).then_inc(S["silu_done"], 1)
                    act.wait_ge(S["g_done"], n + 1)
                    if h == 0 and b:
                        act.wait_ge(S["out_products_done"], 4 * b)
                    act.copy(g_parts[:, 0, h, :], g_f32[:, n % 2, :]).then_inc(S["g_high_done"], 1)
                    if b < B - 1 and h == 5:
                        ln_sq(b + 1)
                    if b < B - 1 and h == 8:
                        ln_std(b + 1)
                for tt in range(4):
                    n = 4 * b + tt
                    act.wait_ge(S["x_mid_transposed"], n + 1)
                    if n >= 2:
                        act.wait_ge(S["out_rows_ready"], n - 1)
                    act.copy(x_out_rows[:, n % 2, :], bank[7][:, :]).then_inc(S["x_out_rows_ready"], 1)
                    if b < B - 1 and tt < 3:
                        ln_y(b + 1, ((0,), (1,), (2, 3))[tt])

        @block.vector
        def _(v):
            ch = [0]

            def link(ins):
                ch[0] += 1
                ins.then_inc(S["dve_chain"], 1)
                v.wait_ge(S["dve_chain"], ch[0])

            v.memset(x_units[:, :, T:T + 4 * CH, :], 0.0)
            v.memset(zeros[:, :], 0.0)
            link(v.memset(scan_factor[:, :], 1.0))
            link(v.memset(scan_factor[:, 0:7 * SB:7], 0.0))
            v.wait_ge(S["loaded_biases"], 64)
            v.tensor_tensor(bsum[:, 0:8], bih[:, 0:8], bhh[:, 0:8], ALU.add)
            link(v.tensor_copy(bsum[:, 8:12], bih[:, 8:12]))
            link(v.tensor_copy(bhn_parts[:, 0, :], bhh[:, 8:12]))
            link(v.tensor_tensor(bhn_rest[:, 0, :], bhh[:, 8:12], bhn_parts[:, 0, :], ALU.subtract))
            link(v.tensor_copy(bhn_parts[:, 1, :], bhn_rest[:, 0, :]))
            link(v.tensor_tensor(bhn_parts[:, 2, :], bhn_rest[:, 0, :], bhn_parts[:, 1, :], ALU.subtract))
            v.wait_ge(S["loaded_vectors"], 80)
            link(v.tensor_scalar(lambda_consts[:, 20:24], lambda_consts[:, 0:4], -1.0, None, ALU.mult))
            v.tensor_tensor(lambda_consts[:, 4:8], lambda_consts[:, 0:4], lambda_consts[:, 20:24], ALU.min).then_inc(S["softplus_done"], 1)
            v.memset(ln_consts[:, 12:13], 1.0 + 1e-6)
            v.memset(ln_consts[:, 13:14], 1e-6)
            v.memset(ffn_consts[:, 29:30], 0.0)
            v.memset(mean_ones[:, :], 1.0 / D)
            v.memset(row_ones[:, :], 1.0)
            v.wait_ge(S["loaded_ident_cond"], 32)
            v.tensor_copy(ident16[:, :], ident[:, :])
            v.tensor_tensor(query[:, :], query[:, :], rms_weight[:, :], ALU.mult)
            v.tensor_reduce(ffn_consts[:, 8:9], ln_consts[:, 0:4], AX.X, ALU.max, apply_absolute_value=True)
            v.tensor_reduce(ffn_consts[:, 9:10], ln_consts[:, 4:8], AX.X, ALU.max, apply_absolute_value=True).then_inc(S["ln_bound"], 1)
            v.wait_ge(S["ln_bound"], 2)
            link(v.tensor_scalar(ffn_consts[:, 12:13], ffn_consts[:, 10:11], float(D) ** 0.5 * 1.01, None, ALU.mult))
            link(v.tensor_tensor(ffn_consts[:, 12:13], ffn_consts[:, 12:13], ffn_consts[:, 11:12], ALU.add))
            link(v.tensor_scalar(ffn_consts[:, 12:13], ffn_consts[:, 12:13], 1e-30, None, ALU.max))
            link(v.tensor_scalar(ffn_consts[:, 13:14].bitcast(U32), ffn_consts[:, 12:13].bitcast(U32), 0x7F800000, None, ALU.bitwise_and))
            link(v.tensor_scalar(ffn_consts[:, 13:14], ffn_consts[:, 13:14], 2.0 ** -14, None, ALU.mult))
            link(v.reciprocal(ffn_consts[:, 14:15], ffn_consts[:, 13:14]))
            v.tensor_scalar(ln_consts[:, 8:12], ln_consts[:, 0:4], ffn_consts[:, 14:15], None, ALU.mult)
            v.tensor_scalar(ln_beta_scaled[:, :], ln_consts[:, 4:8], ffn_consts[:, 14:15], None, ALU.mult)
            v.wait_ge(S["softplus_done"], 3)
            link(v.tensor_scalar(lambda_consts[:, 20:24], lambda_consts[:, 0:4], 0.0, None, ALU.max))
            link(v.tensor_tensor(lambda_consts[:, 16:20], lambda_consts[:, 20:24], lambda_consts[:, 12:16], ALU.add))
            link(v.tensor_scalar(lambda_consts[:, 16:20], lambda_consts[:, 16:20], -8.0, None, ALU.mult))

            v.wait_ge(S["cond_transposed"], 1)
            v.tensor_copy(condT[:, :], bank[7][:, 0:SB]).then_inc(S["cond_transposed"], 1)
            v.wait_ge(S["cond_transposed"], 2)
            v.tensor_reduce(maxima[:, 1:2], condT[:, :], AX.X, ALU.max, apply_absolute_value=True).then_inc(S["maxima_done"], 1)
            for c in range(0, NXT, 2):
                v.wait_ge(S["prologue_transposed"], c + 1)
                v.tensor_copy(x_units[:, :, XT * c:XT * c + XT, :].rearrange("p k t b -> p k b t"),
                              bank[c % 4][:, :].rearrange("p (k b t) -> p k b t", k=KT, b=B)).then_inc(S["x_T_even_read"], 1)
                m = v.tensor_reduce(x_maxima[:, c // 2:c // 2 + 1], x_rows[:, c:c + 2, :], AX.XY, ALU.max, apply_absolute_value=True)
            link(m)
            v.tensor_reduce(maxima[:, 4:5], x_maxima[:, :], AX.X, ALU.max).then_inc(S["maxima_done"], 1)
            v.wait_ge(S["loaded_whh"], 16)
            v.tensor_reduce(maxima[:, 0:1], whh_f32, AX.XY, ALU.max, apply_absolute_value=True).then_inc(S["maxima_done"], 1)
            v.wait_ge(S["loaded_gate_w"], 32)
            v.tensor_reduce(maxima[:, 3:4], gate_w_rows.rearrange("p w m d -> p (w m) d"), AX.XY, ALU.max, apply_absolute_value=True).then_inc(S["maxima_done"], 1)
            v.wait_ge(S["loaded_wih"], 16)
            v.tensor_reduce(maxima[:, 2:3], wih_f32, AX.XY, ALU.max, apply_absolute_value=True).then_inc(S["maxima_done"], 1)

            def scales(a, b):
                link(v.tensor_scalar(maxima[:, 5 + a:5 + b], maxima[:, 5 + a:5 + b], 1e-12, None, ALU.max))
                if a == 0:
                    link(v.tensor_scalar(maxima[:, 6:7], maxima[:, 6:7], 1.0, None, ALU.max))
                link(v.tensor_scalar(maxima[:, 11 + a:11 + b].bitcast(U32), maxima[:, 5 + a:5 + b].bitcast(U32), 0x7F800000, None, ALU.bitwise_and))
                link(v.tensor_scalar(maxima[:, 11 + a:11 + b], maxima[:, 11 + a:11 + b], 2.0 ** -13, None, ALU.mult))
                link(v.reciprocal(scl[:, a:b], maxima[:, 11 + a:11 + b]))

            v.wait_ge(S["maxima_all"], 1)
            scales(0, 5)
            v.tensor_tensor(scl[:, 9:10], maxima[:, 15:16], maxima[:, 13:14], ALU.mult)
            v.tensor_copy(scl[:, 6:7], maxima[:, 12:13])
            link(v.tensor_tensor(scl[:, 5:6], maxima[:, 11:12], maxima[:, 12:13], ALU.mult))
            v.tensor_scalar(scl[:, 11:12], scl[:, 1:2], -1.0, None, ALU.mult)
            v.tensor_tensor(scl[:, 8:9], maxima[:, 12:13], maxima[:, 14:15], ALU.mult)
            link(v.tensor_tensor(scl[:, 10:11], scl[:, 0:1], scl[:, 1:2], ALU.mult))
            v.memset(maxima[:, 10:11], 0.0).then_inc(S["scales_ready"], 1)
            v.tensor_scalar(identS[:, :], ident[:, :], scl[:, 10:11], None, ALU.mult)
            for k in range(KT):
                v.wait_ge(S["wih_split"], 2 * k + 1 if k == 0 else k + 1)
                link(v.scalar_tensor_tensor(wih_parts[:, 1, k, :], wih_f32[:, k, :], scl[:, 2:3], wih_parts[:, 0, k, :], ALU.mult, ALU.subtract))
            v.wait_ge(S["wih_split"], KT)
            link(v.memset(gi_parts, 0.0))
            for c in range(3):
                link(v.tensor_copy(gi_parts[:, :, :, :, 32 + c:60:7].rearrange("p q s k b -> p (q s) k b"), bhn_parts[:, c, :].unsqueeze(1).unsqueeze(3).broadcast_to([P, 2 * CH, KT, B])))
            v.memset(H_parts[:, 0, :, :, 2:4], 0.0).then_inc(S["wih_split"], KT)

            def wg_low(n):
                w, k = divmod(n, KT)
                v.wait_ge(S["gate_w_high_done"], n + 1)
                v.scalar_tensor_tensor(gate_w_parts[:, w, 1, k, :], bank[n % 4][:, :], scl[:, 3:4], gate_w_parts[:, w, 0, k, :], ALU.mult, ALU.subtract).then_inc(S["gate_w_low_done"], 1)

            for n in range(4):
                wg_low(n)
            v.tensor_scalar(h_steps[:, 1, CH - 1, :], condT[:, :], scl[:, 1:2], None, ALU.mult).then_inc(S["h0_ready"], 1)
            v.tensor_scalar(H_parts[:, 0, :, :, 0], condT[:, :].rearrange("p (k b) -> p k b", b=B), scl[:, 1:2], None, ALU.mult).then_inc(S["h0_ready"], 1)
            v.wait_ge(S["h0_ready"], 2)
            v.tensor_tensor(H_parts[:, 0, :, :, 1], h_steps[:, 1, CH - 1, :].rearrange("p (k b) -> p k b", b=B), H_parts[:, 0, :, :, 0], ALU.subtract).then_inc(S["h0_ready"], 1)
            for n in range(4, 8):
                wg_low(n)
            for k in range(KT):
                v.wait_ge(S["whh_high_done"], k + 1)
                v.scalar_tensor_tensor(whh_parts[:, 1, k, :], whh_f32[:, k, :], scl[:, 0:1], whh_parts[:, 0, k, :], ALU.mult, ALU.subtract).then_inc(S["whh_low_done"], 1)

            def kb(a, hf):
                return a[:, 8 * hf:8 * hf + 8].rearrange("p (k b) -> p k b", b=B)

            def step(c, s, par, first):
                t = c * CH + s
                h_before = h_steps[:, par, s - 1, :] if s else h_steps[:, 1 - par, CH - 1, :]

                def sum_parts(name, g, dst, ready, hf):
                    v.wait_ge(S[ready], 2 * t + hf + 1)
                    v.tensor_reduce(dst[:, 8 * hf:8 * hf + 8], gate_bank[g][hf][:, 0:32].rearrange("p (u c) -> p u c", c=4),
                                    AX.X, ALU.add).then_inc(S[name], 1)

                def scan_n(hf):
                    v.wait_ge(S["n_products_done"], 2 * t + hf + 1)
                    v.wait_ge(S["r_gate_done"], 2 * t + hf + 1)
                    v.tensor_tensor_scan(scan_out[:, 56 * hf:56 * hf + 56], scan_factor[:, 56 * hf:56 * hf + 56], gate_bank[2][hf][:, 0:56], 0.0,
                                         ALU.mult, ALU.add).then_inc(S["n_scan_done"], 1)

                def one_minus_z(hf):
                    v.wait_ge(S["z_gate_done"], 2 * t + hf + 1)
                    v.tensor_scalar(one_minus_z_scaled[:, 8 * hf:8 * hf + 8], z_value[:, 8 * hf:8 * hf + 8], scl[:, 11:12], scl[:, 1:2], ALU.mult, ALU.add).then_inc(S["one_minus_z_done"], 1)

                def old_part(hf):
                    v.wait_ge(S["z_gate_done"], 2 * t + hf + 1)
                    if not first:
                        v.wait_ge(S["h_step_done"], 2 * t + hf - 1)
                    v.tensor_tensor(z_part[:, 8 * hf:8 * hf + 8], z_value[:, 8 * hf:8 * hf + 8], h_before[:, 8 * hf:8 * hf + 8], ALU.mult).then_inc(S["z_part_done"], 1)
                    v.tensor_tensor(H_parts[:, (s + 1) % 2, 2 * hf:2 * hf + 2, :, 0], kb(z_value, hf), kb(h_before, hf), ALU.mult).then_inc(S["z_part_done"], 1)

                def old_part_low(hf):
                    v.wait_ge(S["z_part_done"], 2 * (2 * t + hf + 1))
                    v.tensor_tensor(H_parts[:, (s + 1) % 2, 2 * hf:2 * hf + 2, :, 1], kb(z_part, hf), H_parts[:, (s + 1) % 2, 2 * hf:2 * hf + 2, :, 0], ALU.subtract)

                def new_part(hf):
                    v.wait_ge(S["tanh_done"], 2 * t + hf + 1)
                    v.wait_ge(S["one_minus_z_done"], 2 * t + hf + 1)
                    v.tensor_tensor(n_part[:, 8 * hf:8 * hf + 8], n_value[:, 8 * hf:8 * hf + 8], one_minus_z_scaled[:, 8 * hf:8 * hf + 8], ALU.mult).then_inc(S["n_part_done"], 1)
                    v.tensor_tensor(H_parts[:, (s + 1) % 2, 2 * hf:2 * hf + 2, :, 2], kb(n_value, hf), kb(one_minus_z_scaled, hf), ALU.mult).then_inc(S["n_part_done"], 1)

                def new_part_low(hf):
                    v.wait_ge(S["n_part_done"], 2 * (2 * t + hf + 1))
                    v.tensor_tensor(H_parts[:, (s + 1) % 2, 2 * hf:2 * hf + 2, :, 3], kb(n_part, hf), H_parts[:, (s + 1) % 2, 2 * hf:2 * hf + 2, :, 2], ALU.subtract).then_inc(S["h_parts_ready"], 1)

                def state(hf):
                    if s == 0 and hf == 0 and not isinstance(c, int):
                        v.wait_ge(S["h_kept"], c - 1)
                    v.tensor_tensor(h_steps[:, par, s, 8 * hf:8 * hf + 8], z_part[:, 8 * hf:8 * hf + 8], n_part[:, 8 * hf:8 * hf + 8], ALU.add).then_inc(S["h_step_done"], 1)

                sum_parts("r_parts_added", 0, r_parts_sum, "r_products_done", 0)
                sum_parts("z_parts_added", 1, z_parts_sum, "z_products_done", 0)
                scan_n(0)
                sum_parts("r_parts_added", 0, r_parts_sum, "r_products_done", 1)
                old_part(0)
                one_minus_z(0)
                old_part_low(0)
                sum_parts("z_parts_added", 1, z_parts_sum, "z_products_done", 1)
                new_part(0)
                scan_n(1)
                new_part_low(0)
                one_minus_z(1)
                old_part(1)
                state(0)
                new_part(1)
                old_part_low(1)
                new_part_low(1)
                state(1)

            for s in range(2 * CH):
                step(s // CH, s % CH, s // CH, s == 0)
            with v.Fori(1, NCH // 2) as i:
                for s in range(2 * CH):
                    step(2 * i + s // CH, s % CH, s // CH, False)


            nb = [0]

            def evac_q():
                n, g = divmod(nb[0], 6)
                if nb[0] % 2 == 0:
                    v.wait_ge(S["ternary_transposed"], nb[0] + 1)
                    w = 1024 if g < 5 else 512
                    dst = Q_reg[:, n * KT * HP // 2 + 512 * g:n * KT * HP // 2 + 512 * g + w // 2].bitcast(F16)
                    v.tensor_copy(dst, bank[nb[0] % 4][:, 0:w // 2].bitcast(F16)).then_inc(S["ternary_T_even_read"], 1)
                nb[0] += 1

            def quant(n):
                v.wait_ge(S["abs_sums_all"], n + 1)
                link(v.tensor_reduce(ffn_consts[:, 4 + n:5 + n], abs_sums[:, 1, 4 * n:4 * n + 4], AX.X, ALU.add))
                link(v.tensor_scalar(ffn_consts[:, 20 + n:21 + n], ffn_consts[:, 4 + n:5 + n], 0.5 / (HID * D), None, ALU.mult))
                link(v.tensor_scalar(ffn_consts[:, 24 + n:25 + n], ffn_consts[:, 20 + n:21 + n], -1.0, None, ALU.mult))
                if n == 0:
                    v.wait_ge(S["x_mid_done"], NTB)
                if n == 2:
                    v.wait_ge(S["ternary_transposed"], 6)
                link(v.tensor_scalar(ternary_w[n], w_rows[n], ffn_consts[:, 20 + n:21 + n], None, ALU.is_gt))
                v.scalar_tensor_tensor(ternary_w[n], w_rows[n], ffn_consts[:, 24 + n:25 + n], ternary_w[n], ALU.is_lt, ALU.subtract).then_inc(S["ternary_done"], 1)

            def low(blk):
                for k in range(KT):
                    v.wait_ge(S["h_high_done"], KT * blk + k + 1)
                    p = h_parts[:, blk % 2, k].rearrange("p c (t b) -> p c t b", b=B)
                    v.scalar_tensor_tensor(p[:, 1], h_all[:, k, blk * TS:(blk + 1) * TS, :], scl[:, 1:2], p[:, 0], ALU.mult, ALU.subtract).then_inc(S["h_low_done"], 1)

            def block_sums(blk):
                v.wait_ge(S["x_mid_done"], blk + 1)
                for k in range(KT):
                    v.tensor_reduce(block_sums_T[:, k, :].rearrange("p (b n) -> p b n", b=B)[:, :, 2 * blk:2 * blk + 2],
                                    x_mid[:, k, :, blk * TS:(blk + 1) * TS].rearrange("p b (n t) -> p b n t", t=64), AX.X, ALU.add).then_inc(S["block_sums_done"], 1)

            v.wait_ge(S["h_kept"], NCH)
            low(0)
            low(1)
            for blk in range(NTB):
                ts = slice(blk * TS, (blk + 1) * TS)
                if blk < NTB - 2:
                    low(blk + 2)
                v.wait_ge(S["gated_h_done"], blk + 1)
                v.wait_ge(S["beta_done"], blk + 1)
                v.tensor_tensor(h_all[:, :, ts, :], beta[:, blk % 2].rearrange("p k (t b) -> p k t b", b=B), h_all[:, :, ts, :], ALU.mult).then_inc(S["beta_applied"], 1)
                v.wait_ge(S["beta_applied"], blk + 1)
                if blk:
                    v.wait_ge(S["linear_scan_done"], 16 * blk)
                for k in range(KT):
                    for b in range(B):
                        a = alpha[:, blk % 2, k, :].rearrange("p (t b) -> p t b", b=B)
                        v.tensor_tensor_scan(h_all[:, k, ts, b], a[:, :, b], h_all[:, k, ts, b],
                                             h_all[:, k, blk * TS - 1, b:b + 1] if blk else 0.0, ALU.mult, ALU.add).then_inc(S["linear_scan_done"], 1)
                if blk:
                    block_sums(blk - 1)
            block_sums(NTB - 1)
            Lb = bank[6]
            Ob = bank[4:6]

            def ln_x(b):
                if b:
                    v.wait_ge(S["y_high_done"], 4 * b)
                    v.wait_ge(S["y_f32_done"], 4 * b)
                for k in range(KT):
                    v.tensor_scalar(centered[:, k, :], x_mid[:, k, b, :], projected[:, k * B + b:k * B + b + 1], None, ALU.add).then_inc(S["ln_x_done"], 1)

            def ln_center(b):
                v.wait_ge(S["mean_done"], b + 1)
                v.tensor_tensor(centered[:, :, :], centered[:, :, :], Lb[:, :].unsqueeze(1).broadcast_to([P, KT, T]), ALU.subtract).then_inc(S["centered_done"], 1)

            def ln_recip(b, half):
                v.wait_ge(S["std_done"], b + 1)
                t2 = slice(half * T // 2, (half + 1) * T // 2)
                v.reciprocal(std_rows[:, 1, t2], std_rows[:, 0, t2]).then_inc(S["reciprocal_done"], 1)

            def ln_norm(b):
                v.wait_ge(S["reciprocal_done"], 2 * (b + 1))
                v.wait_ge(S["squares_done"], b + 1)
                v.tensor_tensor(centered[:, :, :], centered[:, :, :], std_rows[:, 1, :].unsqueeze(1).broadcast_to([P, KT, T]), ALU.mult).then_inc(S["normalized"], 1)

            def ln_low(b, tiles):
                for k in tiles:
                    v.wait_ge(S["y_f32_done"], 4 * b + k + 1)
                    v.wait_ge(S["y_high_done"], 4 * b + k + 1)
                    v.tensor_tensor(y_parts[:, b % 2, 1, k * T:(k + 1) * T], squared[:, k, :], y_parts[:, b % 2, 0, k * T:(k + 1) * T], ALU.subtract).then_inc(S["y_low_done"], 1)

            def move_ternary(n):
                for _ in range(6):
                    evac_q()

            v.wait_ge(S["proj_w_T_read"], 8)
            quant(0)
            v.wait_ge(S["keys_done"], 1)
            v.wait_ge(S["key_squares_done"], 1)
            v.tensor_tensor_reduce(out=rms_weight[:, :], in0=bank[4][0:32, :], in1=query[:, :], scale=1.0, scalar=0.0,
                                   op0=ALU.mult, op1=ALU.add, accum_out=att_cols[:, 2:3]).then_inc(S["key_dots"], 1)
            v.wait_ge(S["rms_done"], 1)
            link(v.reciprocal(att_cols[:, 3:4], att_cols[:, 1:2]))
            v.wait_ge(S["key_dots"], 1)
            v.tensor_tensor(att_cols[:, 4:5], att_cols[:, 2:3], att_cols[:, 3:4], ALU.mult).then_inc(S["scores_done"], 1)
            v.wait_ge(S["scores_row_done"], 1)
            scT = bank[5][0:1, 0:32].rearrange("p (b n) -> p b n", n=8)

            def row(o):
                return att_rows[0:1, o:o + 32].rearrange("p (b n) -> p b n", n=8)

            def per_b(o):
                return att_cols[0:1, o:o + 4].unsqueeze(2).broadcast_to([1, 4, 8])

            link(v.tensor_reduce(att_cols[0:1, 8:12], scT, AX.X, ALU.max))
            v.tensor_tensor(row(0), scT, per_b(8), ALU.subtract).then_inc(S["scores_shifted"], 1)
            v.wait_ge(S["att_exp_done"], 1)
            link(v.tensor_reduce(att_cols[0:1, 12:16], row(32), AX.X, ALU.add))
            link(v.reciprocal(att_cols[0:1, 8:12], att_cols[0:1, 12:16]))
            v.tensor_tensor(row(96), row(32), per_b(8), ALU.mult).then_inc(S["att_weights_done"], 1)
            v.wait_ge(S["att_broadcast"], 1)
            link(v.tensor_tensor(weighted_sums[:, :, :], block_sums_T[:, :, :], bank[6][:, 0:32].unsqueeze(1).broadcast_to([P, KT, 32]), ALU.mult))
            v.tensor_reduce(attended[:, :], weighted_sums[:, :, :].rearrange("p k (b n) -> p (k b) n", n=8), AX.X, ALU.add).then_inc(S["attended_done"], 1)
            v.wait_ge(S["proj_products_done"], 1)
            v.tensor_copy(projected[:, :], bank[7][:, 0:SB]).then_inc(S["projected_done"], 1)
            v.wait_ge(S["projected_done"], 1)

            ln_x(0)
            move_ternary(0)
            quant(1)
            ln_center(0)
            move_ternary(1)
            quant(2)
            ln_recip(0, 0)
            ln_recip(0, 1)
            ln_norm(0)
            link(v.tensor_tensor(ffn_consts[:, 18:19], ffn_consts[:, 10:11], ffn_consts[:, 11:12], ALU.add))
            link(v.tensor_scalar(ffn_consts[:, 18:19], ffn_consts[:, 18:19], float(D), None, ALU.mult))
            link(v.tensor_tensor(ffn_consts[:, 19:20], ffn_consts[:, 18:19], ffn_consts[:, 20:21], ALU.mult))
            link(v.tensor_tensor(ffn_consts[:, 18:19], ffn_consts[:, 18:19], ffn_consts[:, 21:22], ALU.mult))
            link(v.tensor_tensor(ffn_consts[:, 18:19], ffn_consts[:, 18:19], ffn_consts[:, 19:20], ALU.mult))
            link(v.tensor_scalar(ffn_consts[:, 18:19], ffn_consts[:, 18:19], 4.0, 1e-20, ALU.mult, ALU.max))
            link(v.tensor_scalar(ffn_consts[:, 19:20].bitcast(U32), ffn_consts[:, 18:19].bitcast(U32), 0x7F800000, None, ALU.bitwise_and))
            link(v.tensor_scalar(ffn_consts[:, 19:20], ffn_consts[:, 19:20], 2.0 ** -13, None, ALU.mult))
            link(v.reciprocal(ffn_consts[:, 18:19], ffn_consts[:, 19:20]))
            link(v.tensor_scalar(ffn_consts[:, 27:28], ffn_consts[:, 26:27], ffn_consts[:, 19:20], 2.0, ALU.mult, ALU.mult))
            link(v.reciprocal(ffn_consts[:, 28:29], ffn_consts[:, 14:15]))
            link(v.tensor_scalar(ffn_consts[:, 16:18], ffn_consts[:, 24:26], ffn_consts[:, 28:29], 2.0, ALU.mult, ALU.mult))
            link(v.tensor_scalar(ffn_consts[:, 17:18], ffn_consts[:, 17:18], ffn_consts[:, 18:19], None, ALU.mult))
            move_ternary(2)
            ln_low(0, range(KT))
            for b in range(B):
                for h in range(HT):
                    n = HT * b + h
                    hb = bank[0:2] if n % 2 == 0 else bank[2:4]
                    v.wait_ge(S["silu_done"], n + 1)
                    if n >= 2:
                        v.wait_ge(S["g_low_done"], n - 1)
                    v.scalar_tensor_tensor(g_f32[:, n % 2, :], hb[1][:, :], ffn_consts[:, 17:18], silu_h1[:, n % 2, :], ALU.mult, ALU.mult).then_inc(S["g_done"], 1)
                    v.wait_ge(S["g_high_done"], n + 1)
                    v.tensor_tensor(g_parts[:, 1, h, :], g_f32[:, n % 2, :], g_parts[:, 0, h, :], ALU.subtract).then_inc(S["g_low_done"], 1)
                    if b == B - 1:
                        continue
                    if h == 1:
                        ln_x(b + 1)
                    if h == 4:
                        ln_center(b + 1)
                    if h in (8, 9):
                        ln_recip(b + 1, h - 8)
                    if h == 10:
                        ln_norm(b + 1)
                for tt in range(4):
                    n = 4 * b + tt
                    v.wait_ge(S["out_products_done"], n + 1)
                    v.wait_ge(S["x_out_rows_ready"], n + 1)
                    if n >= 2:
                        v.wait_ge(S[("stored_even", "stored_odd")[n % 2]], 16 * (n // 2))
                    v.scalar_tensor_tensor(out_rows[:, n % 2, :], Ob[n % 2][:, :], ffn_consts[:, 27:28], x_out_rows[:, n % 2, :], ALU.mult, ALU.add).then_inc(S["out_rows_ready"], 1)
                    if b < B - 1 and tt:
                        ln_low(b + 1, ((0,), (1,), (2, 3))[tt - 1])


def kernel(**a):
    import numpy as np
    import concourse.bacc as _bacc
    from concourse.bass_utils import run_bass_kernel_spmd as _run
    nc = _bacc.Bacc("TRN2", target_bir_lowering=False, num_devices=1)
    ident = np.eye(P, dtype=np.float32)
    names = ["x", "cond_2048", "L0_cond_W_ih", "L0_cond_W_hh", "L0_cond_b_ih", "L0_cond_b_hh", "L0_attn_W_in", "L0_attn_b_in", "L0_attn_W_gate", "L0_attn_b_gate", "L0_attn_forget_lambda", "L0_cond2_rms_weight", "L0_cond2_Wk", "L0_cond2_Wo", "L0_cond2_ln_gamma", "L0_cond2_ln_beta", "L0_ffn_w1", "L0_ffn_w3", "L0_ffn_w2"]
    arrs = {n: np.ascontiguousarray(a[n]) for n in names}
    arrs["ident"] = ident
    aps = [nc.dram_tensor("in_" + n, v.shape, F32, kind="ExternalInput").ap() for n, v in arrs.items()]
    o = nc.dram_tensor("o", (B, T, D), F32, kind="ExternalOutput").ap()
    gru(nc, *aps, o)
    r = _run(nc, [{"in_" + k: v for k, v in arrs.items()}], core_ids=[0])
    return r.results[0]["o"]
```
